# Optimizing a Trainium2 kernel written in Bass

```python
import numpy as np
import jax
import jax.numpy as jnp

def _softmax(x, axis=-1):
    return jax.nn.softmax(x, axis=axis)

def _gelu(x):
    return jax.nn.gelu(x, approximate=True)

def _silu(x):
    return jax.nn.silu(x)

def _sigmoid(x):
    return jax.nn.sigmoid(x)

def _layernorm(x, axis=-1, eps=1e-05):
    m = jnp.mean(x, axis=axis, keepdims=True)
    v = jnp.var(x, axis=axis, keepdims=True)
    return (x - m) / jnp.sqrt(v + eps)

def _scatter_add(tgt, idx, src, axis=0):
    return tgt.at[idx].add(src)

def _segment_sum(src, seg, n):
    return jax.ops.segment_sum(src, seg, n)
kernel_name = 'mk_decoder_postln_d1_seqx_r4_0bc2cd'

def setup_inputs(seed: int=0):
    np.random.seed(seed)
    _w = jnp.asarray

    def _rec_inputs():
        import jax
        import jax.numpy as jnp
        _rk = jax.random.key(seed)
        x = -0.0005207 + 1.001 * jax.random.normal(jax.random.fold_in(_rk, 1), (32, 112, 256), jnp.float32)
        _lenS = 112 - jax.random.randint(jax.random.fold_in(_rk, 7), (32,), 0, max(1, 112 // 4) + 1, jnp.int32)
        _lenS2 = 375 - jax.random.randint(jax.random.fold_in(_rk, 8), (32,), 0, max(1, 375 // 4) + 1, jnp.int32)
        _ctx_1024P = jax.random.normal(jax.random.fold_in(_rk, 11), (32, 16, 256), jnp.float32)
        _ctx_1024c = jax.random.dirichlet(jax.random.fold_in(_rk, 511), 0.3 * jnp.ones((16,), jnp.float32), (32, 375))
        _ctx_1024t = jnp.einsum('bsk,bkd->bsd', _ctx_1024c, _ctx_1024P)
        _ctx_1024t = _ctx_1024t * jax.lax.rsqrt(jnp.mean(jnp.square(_ctx_1024t)) + 1e-12) * 0.953939
        ctx_1024 = 4.13588e-05 + 0.999923 * (_ctx_1024t + 0.3 * jax.random.normal(jax.random.fold_in(_rk, 611), (32, 375, 256), jnp.float32))
        _validS = jnp.arange(112)[None, :] < _lenS[:, None]
        _validS2 = jnp.arange(375)[None, :] < _lenS2[:, None]
        _causal = jnp.tril(jnp.ones((112, 112), dtype=bool))
        mask_BxS2_bf1 = jnp.ones((32, 375), dtype=bool)
        return (x, ctx_1024, mask_BxS2_bf1)
    x, ctx_1024, mask_BxS2_bf1 = _rec_inputs()

    def _L0_attn_setup():
        import jax, jax.numpy as jnp
        import numpy as np
        DIM = 256
        INNER = DIM // 2
        DSTATE = 8
        KSZ = 3
        DTRANK = max(INNER // 8, 4)
        B, L = (4, 1024)

        def _dwconv_silu(u, kern):
            c = u.shape[-1]
            v = jnp.transpose(u, (0, 2, 1))
            v = jax.lax.conv_general_dilated(v, kern, (1,), [(KSZ // 2, KSZ // 2)], dimension_numbers=('NCH', 'OIH', 'NCH'), feature_group_count=c)
            return jax.nn.silu(jnp.transpose(v, (0, 2, 1)))

        def _forward(x, W_in, Kx, Kz, W_xproj, W_dt, b_dt, A_log, D, W_out):
            h = jnp.einsum('bld,ed->ble', x, W_in)
            xb, zb = jnp.split(h, 2, axis=-1)
            xb = _dwconv_silu(xb, Kx)
            zb = _dwconv_silu(zb, Kz)
            proj = jnp.einsum('blc,oc->blo', xb, W_xproj)
            dt_raw = proj[..., :DTRANK]
            b_raw = proj[..., DTRANK:DTRANK + DSTATE]
            c_raw = proj[..., DTRANK + DSTATE:]
            delta = jnp.clip(jax.nn.softplus(jnp.einsum('blr,cr->blc', dt_raw, W_dt) + b_dt), 0.0001, 1.0)
            b_term = jnp.tanh(b_raw)
            c_term = jnp.tanh(c_raw)
            a = jax.nn.softplus(A_log) + 0.0001
            decay = jnp.clip(jnp.exp(-delta[..., None] * a), 0.0001, 1.0)
            drive = (1.0 - decay) * (b_term[:, :, None, :] * xb[..., None])

            def step(state, inp):
                dec_t, drv_t, c_t, x_t = inp
                state = dec_t * state + drv_t
                y = jnp.sum(state * c_t[:, None, :], axis=-1) + D * x_t
                return (state, y)
            tm = lambda t: jnp.moveaxis(t, 1, 0)
            state0 = jnp.zeros((x.shape[0], INNER, DSTATE), dtype=jnp.float32)
            _, ys = jax.lax.scan(step, state0, (tm(decay), tm(drive), tm(c_term), tm(xb)))
            y = jnp.moveaxis(ys, 0, 1)
            return jnp.einsum('bld,ed->ble', jnp.concatenate([y, zb], axis=-1), W_out)
        key = jax.random.key(seed)
        ks = jax.random.split(key, 8)
        s = 0.02
        x = jax.random.normal(ks[0], (B, L, DIM), dtype=jnp.float32)
        W_in = jax.random.normal(ks[1], (DIM, DIM), dtype=jnp.float32) * s
        Kx = jax.random.normal(ks[2], (INNER, 1, KSZ), dtype=jnp.float32) * 0.1
        Kz = jax.random.normal(ks[3], (INNER, 1, KSZ), dtype=jnp.float32) * 0.1
        W_xproj = jax.random.normal(ks[4], (DTRANK + 2 * DSTATE, INNER), dtype=jnp.float32) * s
        W_dt = jax.random.normal(ks[5], (INNER, DTRANK), dtype=jnp.float32) * s
        dt_init = jnp.exp(jnp.linspace(jnp.log(0.02), jnp.log(0.2), INNER))
        b_dt = jnp.log(jnp.expm1(dt_init)).astype(jnp.float32)
        A_log = jnp.log(jnp.tile(jnp.arange(1, DSTATE + 1, dtype=jnp.float32), (INNER, 1)))
        D = jnp.ones((INNER,), dtype=jnp.float32)
        W_out = jax.random.normal(ks[6], (DIM, DIM), dtype=jnp.float32) * s
        return {'x': x, 'W_in': W_in, 'Kx': Kx, 'Kz': Kz, 'W_xproj': W_xproj, 'W_dt': W_dt, 'b_dt': b_dt, 'A_log': A_log, 'D': D, 'W_out': W_out}
    _L0_attn_all = _L0_attn_setup()
    _L0_attn_in = {k: v for k, v in _L0_attn_all.items() if k in ('W_in', 'Kx', 'Kz', 'W_xproj', 'W_dt', 'b_dt', 'A_log', 'D', 'W_out')}
    del _L0_attn_all

    def _L0_xattn_setup():
        import jax, jax.numpy as jnp
        import numpy as np
        B, T, S, DM, H, D, TOPK = (4, 128, 512, 256, 16, 64, 32)
        INNER = H * D
        key = jax.random.key(seed)
        ks = jax.random.split(key, 7)
        x = jax.random.normal(ks[0], (B, T, DM), dtype=jnp.float32)
        mem_keys = jax.random.normal(ks[1], (B, S, DM), dtype=jnp.float32)
        mem_values = jax.random.normal(ks[2], (B, S, DM), dtype=jnp.float32)
        mem_mask = jnp.ones((B, S), dtype=bool)
        sc = 0.02
        Wq = sc * jax.random.normal(ks[3], (DM, INNER), dtype=jnp.float32)
        Wk = sc * jax.random.normal(ks[4], (DM, INNER), dtype=jnp.float32)
        Wv = sc * jax.random.normal(ks[5], (DM, INNER), dtype=jnp.float32)
        Wo = sc * jax.random.normal(ks[6], (INNER, DM), dtype=jnp.float32)
        inv_temp = jnp.ones((H,), dtype=jnp.float32)
        return {'x': x, 'mem_keys': mem_keys, 'mem_values': mem_values, 'mem_mask': mem_mask, 'Wq': Wq, 'Wk': Wk, 'Wv': Wv, 'Wo': Wo, 'inv_temp': inv_temp}
    _L0_xattn_all = _L0_xattn_setup()
    _L0_xattn_in = {k: v for k, v in _L0_xattn_all.items() if k in ('Wq', 'Wk', 'Wv', 'Wo', 'inv_temp')}
    del _L0_xattn_all

    def _L0_ffn_setup():
        import jax, jax.numpy as jnp
        import numpy as np
        E = 8
        K = 2
        CAP_FACTOR = 1.0
        key = jax.random.key(seed)
        ks = jax.random.split(key, 5)
        B, T, C, H = (4, 512, 256, 1024)
        x = jax.random.normal(ks[0], (B, T, C), dtype=jnp.float32)
        Wr = jax.random.normal(ks[1], (C, E), dtype=jnp.float32) * 0.02
        br = jnp.zeros((E,), jnp.float32)
        W1 = jax.random.normal(ks[2], (E, C, H), dtype=jnp.float32) * 0.02
        b1 = jnp.zeros((E, H), jnp.float32)
        W2 = jax.random.normal(ks[3], (E, H, C), dtype=jnp.float32) * 0.02
        b2 = jnp.zeros((E, C), jnp.float32)
        return {'x': x, 'Wr': Wr, 'br': br, 'W1': W1, 'b1': b1, 'W2': W2, 'b2': b2}
    _L0_ffn_all = _L0_ffn_setup()
    _L0_ffn_in = {k: v for k, v in _L0_ffn_all.items() if k in ('Wr', 'br', 'W1', 'b1', 'W2', 'b2')}
    del _L0_ffn_all
    return {'x': x, 'ctx_1024': ctx_1024, 'mask_BxS2_bf1': mask_BxS2_bf1, 'L0_attn_W_in': _L0_attn_in['W_in'], 'L0_attn_Kx': _L0_attn_in['Kx'], 'L0_attn_Kz': _L0_attn_in['Kz'], 'L0_attn_W_xproj': _L0_attn_in['W_xproj'], 'L0_attn_W_dt': _L0_attn_in['W_dt'], 'L0_attn_b_dt': _L0_attn_in['b_dt'], 'L0_attn_A_log': _L0_attn_in['A_log'], 'L0_attn_D': _L0_attn_in['D'], 'L0_attn_W_out': _L0_attn_in['W_out'], 'L0_xattn_Wq': _L0_xattn_in['Wq'], 'L0_xattn_Wk': _L0_xattn_in['Wk'], 'L0_xattn_Wv': _L0_xattn_in['Wv'], 'L0_xattn_Wo': _L0_xattn_in['Wo'], 'L0_xattn_inv_temp': _L0_xattn_in['inv_temp'], 'L0_ffn_Wr': _L0_ffn_in['Wr'], 'L0_ffn_br': _L0_ffn_in['br'], 'L0_ffn_W1': _L0_ffn_in['W1'], 'L0_ffn_b1': _L0_ffn_in['b1'], 'L0_ffn_W2': _L0_ffn_in['W2'], 'L0_ffn_b2': _L0_ffn_in['b2']}

def reference(x, ctx_1024, mask_BxS2_bf1, L0_attn_W_in, L0_attn_Kx, L0_attn_Kz, L0_attn_W_xproj, L0_attn_W_dt, L0_attn_b_dt, L0_attn_A_log, L0_attn_D, L0_attn_W_out, L0_xattn_Wq, L0_xattn_Wk, L0_xattn_Wv, L0_xattn_Wo, L0_xattn_inv_temp, L0_ffn_Wr, L0_ffn_br, L0_ffn_W1, L0_ffn_b1, L0_ffn_W2, L0_ffn_b2):
    import jax
    import jax.numpy as jnp

    def _L0_attn_ref(x, W_in, Kx, Kz, W_xproj, W_dt, b_dt, A_log, D, W_out):
        import jax, jax.numpy as jnp
        import numpy as np
        DIM = 256
        INNER = DIM // 2
        DSTATE = 8
        KSZ = 3
        DTRANK = max(INNER // 8, 4)
        B, L = (4, 1024)

        def _dwconv_silu(u, kern):
            c = u.shape[-1]
            v = jnp.transpose(u, (0, 2, 1))
            v = jax.lax.conv_general_dilated(v, kern, (1,), [(KSZ // 2, KSZ // 2)], dimension_numbers=('NCH', 'OIH', 'NCH'), feature_group_count=c)
            return jax.nn.silu(jnp.transpose(v, (0, 2, 1)))

        def _forward(x, W_in, Kx, Kz, W_xproj, W_dt, b_dt, A_log, D, W_out):
            h = jnp.einsum('bld,ed->ble', x, W_in)
            xb, zb = jnp.split(h, 2, axis=-1)
            xb = _dwconv_silu(xb, Kx)
            zb = _dwconv_silu(zb, Kz)
            proj = jnp.einsum('blc,oc->blo', xb, W_xproj)
            dt_raw = proj[..., :DTRANK]
            b_raw = proj[..., DTRANK:DTRANK + DSTATE]
            c_raw = proj[..., DTRANK + DSTATE:]
            delta = jnp.clip(jax.nn.softplus(jnp.einsum('blr,cr->blc', dt_raw, W_dt) + b_dt), 0.0001, 1.0)
            b_term = jnp.tanh(b_raw)
            c_term = jnp.tanh(c_raw)
            a = jax.nn.softplus(A_log) + 0.0001
            decay = jnp.clip(jnp.exp(-delta[..., None] * a), 0.0001, 1.0)
            drive = (1.0 - decay) * (b_term[:, :, None, :] * xb[..., None])

            def step(state, inp):
                dec_t, drv_t, c_t, x_t = inp
                state = dec_t * state + drv_t
                y = jnp.sum(state * c_t[:, None, :], axis=-1) + D * x_t
                return (state, y)
            tm = lambda t: jnp.moveaxis(t, 1, 0)
            state0 = jnp.zeros((x.shape[0], INNER, DSTATE), dtype=jnp.float32)
            _, ys = jax.lax.scan(step, state0, (tm(decay), tm(drive), tm(c_term), tm(xb)))
            y = jnp.moveaxis(ys, 0, 1)
            return jnp.einsum('bld,ed->ble', jnp.concatenate([y, zb], axis=-1), W_out)
        return _forward(x, W_in, Kx, Kz, W_xproj, W_dt, b_dt, A_log, D, W_out)

    def _L0_xattn_ref(x, mem_keys, mem_values, mem_mask, Wq, Wk, Wv, Wo, inv_temp):
        import jax, jax.numpy as jnp
        import numpy as np
        B, T, S, DM, H, D, TOPK = (4, 128, 512, 256, 16, 64, 32)
        INNER = H * D
        b, t, _ = x.shape
        s = mem_keys.shape[1]
        q = (x @ Wq).reshape(b, t, H, D).transpose(0, 2, 1, 3)
        k = (mem_keys @ Wk).reshape(b, s, H, D).transpose(0, 2, 1, 3)
        v = (mem_values @ Wv).reshape(b, s, H, D).transpose(0, 2, 1, 3)
        q = q * inv_temp.reshape(1, H, 1, 1)
        scores = jnp.einsum('bhtd,bhsd->bhts', q, k) / jnp.asarray(np.sqrt(D), x.dtype)
        scores = jnp.where(mem_mask[:, None, None, :], scores, -jnp.inf)
        full_attn = jax.nn.softmax(scores, axis=-1)
        topk_vals = jax.lax.top_k(scores, TOPK)[0]
        threshold = topk_vals[..., -1:]
        topk_mask = (scores >= threshold).astype(scores.dtype)
        sparse_attn = full_attn * topk_mask
        sparse_attn = sparse_attn / (jnp.sum(sparse_attn, axis=-1, keepdims=True) + 1e-08)
        attn = full_attn + jax.lax.stop_gradient(sparse_attn - full_attn)
        out = jnp.einsum('bhts,bhsd->bhtd', attn, v)
        out = out.transpose(0, 2, 1, 3).reshape(b, t, INNER)
        return out @ Wo

    def _L0_ffn_ref(x, Wr, br, W1, b1, W2, b2):
        import jax, jax.numpy as jnp
        import numpy as np
        E = 8
        K = 2
        CAP_FACTOR = 1.0
        B, T, C = x.shape
        N = B * T
        xf = x.reshape(N, C)
        logits = xf @ Wr + br
        topv, topi = jax.lax.top_k(logits, K)
        gates = jax.nn.softmax(topv, axis=-1)
        rw = jnp.zeros((N, E), xf.dtype).at[jnp.arange(N)[:, None], topi].set(gates)
        cap = int(N * K / E * CAP_FACTOR)
        sel = jax.nn.one_hot(topi, E, dtype=jnp.int32).sum(1)
        rank = jnp.cumsum(sel, axis=0) - sel
        keep = (sel > 0) & (rank < cap)
        tok = jnp.broadcast_to(jnp.arange(N, dtype=jnp.int32)[:, None], (N, E))
        eid = jnp.broadcast_to(jnp.arange(E, dtype=jnp.int32)[None, :], (N, E))
        rank_c = jnp.where(keep, rank, cap)
        buf = jnp.full((E, cap), N, dtype=jnp.int32)
        buf = buf.at[eid, rank_c].set(tok, mode='drop')
        xpad = jnp.concatenate([xf, jnp.zeros((1, C), xf.dtype)], axis=0)
        xg = xpad[buf]
        h = jax.nn.gelu(jnp.einsum('ecd,edh->ech', xg, W1) + b1[:, None, :], approximate=False)
        out = jnp.einsum('ech,ehd->ecd', h, W2) + b2[:, None, :]
        rw_pad = jnp.concatenate([rw, jnp.zeros((1, E), rw.dtype)], axis=0)
        w = rw_pad[buf, jnp.arange(E, dtype=jnp.int32)[:, None]]
        weighted = out * w[..., None]
        final = jnp.zeros((N + 1, C), xf.dtype).at[buf.reshape(-1)].add(weighted.reshape(-1, C))
        return final[:N].reshape(B, T, C)
    x = _layernorm(x + _L0_attn_ref(x, L0_attn_W_in, L0_attn_Kx, L0_attn_Kz, L0_attn_W_xproj, L0_attn_W_dt, L0_attn_b_dt, L0_attn_A_log, L0_attn_D, L0_attn_W_out), axis=-1)
    x = _layernorm(x + _L0_xattn_ref(x, ctx_1024, ctx_1024, mask_BxS2_bf1, L0_xattn_Wq, L0_xattn_Wk, L0_xattn_Wv, L0_xattn_Wo, L0_xattn_inv_temp), axis=-1)
    x = _layernorm(x + _L0_ffn_ref(x, L0_ffn_Wr, L0_ffn_br, L0_ffn_W1, L0_ffn_b1, L0_ffn_W2, L0_ffn_b2), axis=-1)
    return x

_drawn_inputs = setup_inputs


def setup_inputs(seed=0):
    import zlib

    import numpy as np

    out = dict(_drawn_inputs(seed))
    spreads = {'L0_attn_D': (1.0, 0.6),
     'L0_xattn_inv_temp': (1.0, 0.6),
     'L0_ffn_br': (0.0, 0.1),
     'L0_ffn_b1': (0.0, 0.354),
     'L0_ffn_b2': (0.0, 0.1)}
    factors = {'L0_attn_W_in': 4.324,
     'L0_attn_Kx': 5.472,
     'L0_attn_Kz': 6.396,
     'L0_attn_W_xproj': 25.286,
     'L0_attn_W_dt': 64.0,
     'L0_attn_b_dt': 8.0,
     'L0_attn_A_log': 46.843,
     'L0_attn_W_out': 4.615}
    for name, (base, spread) in spreads.items():
        noise = np.random.default_rng([zlib.crc32(name.encode()), seed]).standard_normal(out[name].shape)
        drawn = base * np.exp(spread * noise) if base else spread * noise
        out[name] = jnp.asarray(drawn.astype(out[name].dtype))
    for name, factor in factors.items():
        out[name] = (out[name] * factor).astype(out[name].dtype)
    return out
```

```python
from contextlib import ExitStack

import concourse.bass as bass
from concourse import mybir

F32 = mybir.dt.float32
BF16 = mybir.dt.bfloat16
I32 = mybir.dt.int32
U8 = mybir.dt.uint8
ALU = mybir.AluOpType
ACT = mybir.ActivationFunctionType
AX_X = mybir.AxisListType.X

B, T, C = 32, 112, 256
S2 = 375
KC = C // 128
INNER, NSTATE, RANK, TAPS = 128, 8, 16, 3
GB = 4
GROUPS = B // GB
GT = GB * T
H, DH = 16, 64
INNERX = H * DH
PAIRS = H // 2
SC, NSC = 125, 3
TOPK = 32
E = 8
N = B * T
HID = 1024
HM = HID // 128
CAP = N * 2 // E
NT = CAP // 128
HALF = CAP // 2
CX = C + 2
TB = -(-KC * NT // 4)
NOWHERE = 1 << 20
SEL_STEP, VAL_STEP, COUNT_STEP = 14, 15, 19
GONE = -3e38
LN_EPS = 1e-5
CLIP_LO, CLIP_HI = 1e-4, 1.0
SOFTPLUS_CAP = 10.0



def wait_apart(eng, met, *waits):
    waits = [(sem, value if isinstance(value, int) else eng.to_reg(value)) for sem, value in waits]
    eng.wait_ge(met, 1)
    for sem, value in waits:
        eng.wait_ge(sem, value)


def decoder_kernel(nc, out, ins):
    ctx = ExitStack()
    with ctx:
        def sb(name, shape, dt=F32):
            return ctx.enter_context(nc.sbuf_tensor(name, shape, dt))

        xres = sb("xres", [T, B + 1, CX])
        ident_sb = sb("ident_sb", [128, 128])
        logits = sb("logits", [T, B, E])
        fin = nc.dram_tensor("fin", [2 * N, C], F32).ap()
        xg = nc.dram_tensor("xg", [E * CAP, CX], F32).ap()
        state_space_phase(nc, xres, ident_sb, ins["xT"], ins["x"], ins["W_inT"], ins["Kx"], ins["Kz"], ins["W_xprojT"],
                          ins["W_dtT"], ins["b_dt"], ins["A_log"], ins["D"], ins["W_outT"], ins["rows_sel"], ins["ident"])
        clear_phase(nc, fin, xg)
        attention_phase(nc, xres, logits, ident_sb, ins["ctxT"], ins["mask"], ins["mask_pick"], ins["Wq"], ins["Wk"], ins["Wv"],
                        ins["Wo"], ins["inv_temp"], ins["Wr"], ins["br"])
        expert_phase(nc, xres, logits, ident_sb, ins["lower"], ins["W1"], ins["b1T"], ins["W2"], ins["b2"], fin, xg, out)


def state_space_phase(nc, xres, ident_sb, xT, x, W_inT, Kx, Kz, W_xprojT, W_dtT, b_dt, A_log, D, W_outT, rows_sel, ident):
    ctx = ExitStack()
    with ctx:
        def sb(name, shape, dt=F32):
            return ctx.enter_context(nc.sbuf_tensor("m_" + name, shape, dt))

        def ps(name, shape, dt=F32):
            return ctx.enter_context(nc.psum_tensor("m_" + name, shape, dt))

        def sem(name):
            return ctx.enter_context(nc.semaphore("m_" + name))

        w_in = sb("w_in", [128, KC, 2 * INNER])
        w_xp = sb("w_xp", [INNER, RANK + 2 * NSTATE])
        w_dt = sb("w_dt", [RANK, INNER])
        w_out = sb("w_out", [INNER, 2, C])
        taps = sb("taps", [INNER, 2, TAPS])
        bdt = sb("bdt", [INNER, 1])
        skip = sb("skip", [INNER, 1])
        alog = sb("alog", [INNER, NSTATE])
        aneg = sb("aneg", [INNER, NSTATE])
        atmp = sb("atmp", [INNER, 3, NSTATE])
        sel = sb("sel", [2 * NSTATE, 2 * NSTATE, 128])
        bc_sign = sb("bc_sign", [2 * NSTATE, 1])
        xt = sb("xt", [128, KC, GT])
        pad = sb("pad", [INNER, 2, GB, T + 2])
        conv = sb("conv", [INNER, 2, GT])
        xz = sb("xz", [INNER, 2, GT])
        dt_sb = sb("dt_sb", [RANK, GT])
        bc_sb = sb("bc_sb", [2 * NSTATE, GT])
        dl = sb("dl", [INNER, 4, GT])
        decay = sb("decay", [INNER, NSTATE, GT])
        drive = sb("drive", [INNER, NSTATE, GT])
        ysum = sb("ysum", [INNER, GT])
        y = sb("y", [INNER, GT])
        stats = sb("stats", [T, GB, 6])
        summed = sb("summed", [T, GB, C])
        mv = sb("mv", [T, GB, 2])
        veps = sb("veps", [T, GB])
        rstd = sb("rstd", [T, GB])
        neghalf = sb("neghalf", [T, GB])

        h_ps = ps("h_ps", [128, 2, 512])
        p_ps = ps("p_ps", [128, 2, 512])
        row_ps = ps("row_ps", [128, 4, 512])

        loaded = sem("weights_loaded")
        x_loaded = sem("x_loaded")
        ready = sem("setup_ready")
        a_step = sem("a_step")
        half_done = sem("half_done")
        h_done = sem("h_done")
        pad_done = sem("pad_done")
        taps_done = sem("taps_done")
        conv_done = sem("conv_done")
        xz_done = sem("xz_done")
        proj_done = sem("proj_done")
        dtbc_done = sem("dtbc_done")
        draw_done = sem("draw_done")
        dcap_done = sem("dcap_done")
        exp_done = sem("exp_done")
        log_done = sem("log_done")
        um_done = sem("um_done")
        dfix_done = sem("dfix_done")
        dsum_done = sem("dsum_done")
        delta_done = sem("delta_done")
        decay_done = sem("decay_done")
        row_done = sem("row_done")
        row_used = sem("row_used")
        clip_done = sem("clip_done")
        drive_done = sem("drive_done")
        starts_done = sem("starts_done")
        scan_done = sem("scan_done")
        reduce_done = sem("reduce_done")
        y_done = sem("y_done")
        out_done = sem("out_done")
        res_done = sem("res_done")
        stats_done = sem("stats_done")
        mv_done = sem("mv_done")
        veps_done = sem("veps_done")
        rstd_done = sem("rstd_done")
        norm_done = sem("norm_done")

        LOADS = 14

        block = ctx.enter_context(nc.Block())

        @block.sync
        def _(sp):
            sp.dma_start(w_in[:], W_inT.rearrange("(k p) e -> p k e", p=128)).then_inc(loaded, 16)
            sp.dma_start(w_xp[:], W_xprojT).then_inc(loaded, 16)
            sp.dma_start(w_dt[:], W_dtT).then_inc(loaded, 16)
            sp.dma_start(w_out[:], W_outT.rearrange("(k p) e -> p k e", p=128)).then_inc(loaded, 16)
            sp.dma_start(taps[:, 0, :], Kx.rearrange("c a k -> c (a k)")).then_inc(loaded, 16)
            sp.dma_start(taps[:, 1, :], Kz.rearrange("c a k -> c (a k)")).then_inc(loaded, 16)
            sp.dma_start(bdt[:], b_dt.rearrange("(c a) -> c a", a=1)).then_inc(loaded, 16)
            sp.dma_start(skip[:], D.rearrange("(c a) -> c a", a=1)).then_inc(loaded, 16)
            sp.dma_start(alog[:], A_log).then_inc(loaded, 16)
            sp.dma_start(sel[:], rows_sel).then_inc(loaded, 16)
            sp.dma_start(ident_sb[:], ident).then_inc(loaded, 16)
            with sp.Fori(0, GROUPS) as g:
                sp.wait_ge(loaded, 16 * 11)
                sp.wait_ge(h_done, g)
                sp.wait_ge(x_loaded, 32 * g)
                sp.dma_start(xt[:], xT.rearrange("(k p) n -> p k n", p=128)[:, :, bass.ds(g * GT, GT)]).then_inc(x_loaded, 16)
                sp.dma_start(xres[:, bass.ds(g * GB, GB), 0:C], x.rearrange("b t c -> t b c")[:, bass.ds(g * GB, GB), :]).then_inc(x_loaded, 16)

        @block.tensor
        def _(pe):
            pe.wait_ge(loaded, 16 * 11)
            with pe.Fori(0, GROUPS) as g:
                pe.wait_ge(x_loaded, 32 * (g + 1))
                pe.wait_ge(dcap_done, g)
                for half in range(2):
                    for k in range(KC):
                        mm = pe.matmul(h_ps[:, half, 0:GT], w_in[:, k, half * INNER:(half + 1) * INNER], xt[:, k, :],
                                       start=(k == 0), stop=(k == KC - 1))
                mm.then_inc(h_done, 1)
                pe.wait_ge(xz_done, g + 1)
                pe.wait_ge(res_done, g)
                pe.matmul(p_ps[0:RANK, 0, 0:GT], w_xp[:, 0:RANK], xz[:, 0, :], start=True, stop=True)
                pe.matmul(p_ps[0:2 * NSTATE, 1, 0:GT], w_xp[:, RANK:], xz[:, 0, :], start=True, stop=True).then_inc(proj_done, 1)
                pe.wait_ge(dtbc_done, g + 1)
                pe.matmul(h_ps[:, 0, 0:GT], w_dt[:], dt_sb[:], start=True, stop=True).then_inc(draw_done, 1)
                for r in range(2 * NSTATE):
                    n = g * (2 * NSTATE) + (r - 4)
                    if r >= 4:
                        pe.wait_ge(row_used, n + 1)
                    else:
                        pe.wait_ge(row_used, g * (2 * NSTATE))
                    pe.matmul(row_ps[:, r % 4, 0:GT], sel[:, r, :], bc_sb[:], start=True, stop=True).then_inc(row_done, 1)
                pe.wait_ge(y_done, g + 1)
                for b in range(GB):
                    at = slice((b % 2) * C, (b % 2 + 1) * C)
                    pe.matmul(p_ps[0:T, b // 2, at], y[:, b * T:(b + 1) * T], w_out[:, 0, :], start=True, stop=False)
                    mm = pe.matmul(p_ps[0:T, b // 2, at], xz[:, 1, b * T:(b + 1) * T], w_out[:, 1, :], start=False, stop=True)
                mm.then_inc(out_done, 1)

        @block.scalar
        def _(act):
            act.wait_ge(loaded, 16 * 11)
            act.activation(atmp[:, 0, :], alog[:], ACT.Abs).then_inc(a_step, 1)
            act.wait_ge(a_step, 1)
            act.activation(atmp[:, 0, :], atmp[:, 0, :], ACT.Exp, scale=-1.0).then_inc(a_step, 1)
            act.wait_ge(a_step, 2)
            act.activation(atmp[:, 0, :], atmp[:, 0, :], ACT.Ln, bias=1.0).then_inc(a_step, 1)
            act.wait_ge(ready, 1)
            with act.Fori(0, GROUPS) as g:
                act.wait_ge(h_done, g + 1)
                act.wait_ge(conv_done, 2 * g)
                for half in range(2):
                    act.activation(pad[:, half, :, 1:T + 1], h_ps[:, half, 0:GT].rearrange("p (b t) -> p b t", b=GB),
                                   ACT.Copy).then_inc(pad_done, 1)
                act.wait_ge(out_done, g)
                for half in range(2):
                    act.wait_ge(conv_done, 2 * g + half + 1)
                    act.activation(xz[:, half, :], conv[:, half, :], ACT.Silu).then_inc(xz_done, 1) if half else \
                        act.activation(xz[:, half, :], conv[:, half, :], ACT.Silu)
                act.wait_ge(proj_done, g + 1)
                act.activation(bc_sb[:], p_ps[0:2 * NSTATE, 1, 0:GT], ACT.Tanh, scale=bc_sign[:, 0:1])
                act.activation(dt_sb[:], p_ps[0:RANK, 0, 0:GT], ACT.Copy).then_inc(dtbc_done, 1)
                act.wait_ge(dcap_done, g + 1)
                act.activation(dl[:, 1, :], dl[:, 0, :], ACT.Exp).then_inc(exp_done, 1)
                act.wait_ge(exp_done, g + 1)
                act.activation(dl[:, 2, :], dl[:, 1, :], ACT.Ln, bias=1.0).then_inc(log_done, 1)
                act.wait_ge(delta_done, g + 1)
                for s in range(NSTATE):
                    last = act.activation(decay[:, s, :], dl[:, 0, :], ACT.Exp, scale=aneg[:, s:s + 1])
                last.then_inc(decay_done, 1)

        @block.gpsimd
        def _(pool):
            pool.memset(neghalf[:], -0.5).then_inc(half_done, 1)
            pool.wait_ge(half_done, 1)
            with pool.Fori(0, GROUPS) as g:
                pool.wait_ge(veps_done, g + 1)
                pool.tensor_tensor(rstd[:], veps[:], neghalf[:], ALU.pow).then_inc(rstd_done, 1)

        @block.vector
        def _(dve):
            dve.memset(pad[:], 0.0)
            dve.memset(xres[:, B, :], 0.0)
            dve.memset(bc_sign[:], 1.0).then_inc(starts_done, 1)
            dve.wait_ge(starts_done, 1)
            dve.memset(bc_sign[0:NSTATE, :], -1.0)
            dve.wait_ge(a_step, 3)
            dve.wait_ge(loaded, 16 * 11)
            dve.scalar_tensor_tensor(atmp[:, 1, :], alog[:], 0.0, atmp[:, 0, :], ALU.max, ALU.add).then_inc(starts_done, 1)
            dve.wait_ge(starts_done, 2)
            dve.tensor_scalar(aneg[:], atmp[:, 1, :], 1e-4, -1.0, ALU.add, ALU.mult).then_inc(ready, 1)
            with dve.Fori(0, GROUPS) as g:
                for tap in range(TAPS):
                    for half in range(2):
                        src = pad[:, half, :, tap:tap + T]
                        dst = conv[:, half, :].rearrange("p (b t) -> p b t", b=GB)
                        k = taps[:, half, tap:tap + 1]
                        if tap == 0:
                            dve.wait_ge(pad_done, 2 * g + half + 1)
                            dve.tensor_scalar(dst, src, k, None, ALU.mult).then_inc(taps_done, 1)
                        else:
                            dve.wait_ge(taps_done, g * 4 + (tap - 1) * 2 + half + 1)
                            dve.scalar_tensor_tensor(dst, src, k, dst, ALU.mult, ALU.add).then_inc(
                                taps_done if tap == 1 else conv_done, 1)
                dve.wait_ge(draw_done, g + 1)
                dve.wait_ge(decay_done, g)
                dve.tensor_scalar(dl[:, 0, :], h_ps[:, 0, 0:GT], bdt[:, 0:1], SOFTPLUS_CAP, ALU.add, ALU.min).then_inc(dcap_done, 1)
                dve.wait_ge(exp_done, g + 1)
                dve.tensor_scalar(dl[:, 3, :], dl[:, 1, :], 1.0, -1.0, ALU.add, ALU.add).then_inc(um_done, 1)
                dve.wait_ge(um_done, g + 1)
                dve.tensor_tensor(dl[:, 3, :], dl[:, 1, :], dl[:, 3, :], ALU.subtract).then_inc(dfix_done, 1)
                dve.wait_ge(dfix_done, g + 1)
                dve.wait_ge(log_done, g + 1)
                dve.tensor_tensor(dl[:, 3, :], dl[:, 2, :], dl[:, 3, :], ALU.add).then_inc(dsum_done, 1)
                dve.wait_ge(dsum_done, g + 1)
                dve.tensor_scalar(dl[:, 0, :], dl[:, 3, :], CLIP_LO, CLIP_HI, ALU.max, ALU.min).then_inc(delta_done, 1)
                for s in range(NSTATE):
                    dve.wait_ge(row_done, g * (2 * NSTATE) + s + 1)
                    dve.tensor_tensor(drive[:, s, :], row_ps[:, s % 4, 0:GT], xz[:, 0, :], ALU.mult).then_inc(row_used, 1)
                dve.wait_ge(decay_done, g + 1)
                dve.tensor_scalar(decay[:], decay[:], CLIP_LO, CLIP_HI, ALU.max, ALU.min).then_inc(clip_done, 1)
                dve.wait_ge(clip_done, g + 1)
                dve.wait_ge(row_used, g * (2 * NSTATE) + NSTATE)
                dve.scalar_tensor_tensor(drive[:], decay[:], 1.0, drive[:], ALU.subtract, ALU.mult).then_inc(drive_done, 1)
                dve.wait_ge(drive_done, g + 1)
                dve.memset(decay[:].rearrange("p s (b t) -> p s b t", b=GB)[:, :, :, 0:1], 0.0).then_inc(starts_done, 1)
                dve.wait_ge(starts_done, g + 3)
                dve.tensor_tensor_scan(drive[:].rearrange("p s t -> p (s t)"), decay[:].rearrange("p s t -> p (s t)"),
                                       drive[:].rearrange("p s t -> p (s t)"), 0.0, ALU.mult, ALU.add).then_inc(scan_done, 1)
                dve.wait_ge(scan_done, g + 1)
                for s in range(NSTATE):
                    dve.wait_ge(row_done, g * (2 * NSTATE) + NSTATE + s + 1)
                    dve.tensor_tensor(drive[:, s, :], row_ps[:, s % 4, 0:GT], drive[:, s, :], ALU.mult).then_inc(row_used, 1)
                dve.wait_ge(row_used, (g + 1) * (2 * NSTATE))
                dve.tensor_reduce(ysum[:], drive[:].rearrange("p s t -> p t s"), AX_X, ALU.add).then_inc(reduce_done, 1)
                dve.wait_ge(reduce_done, g + 1)
                dve.scalar_tensor_tensor(y[:], xz[:, 0, :], skip[:, 0:1], ysum[:], ALU.mult, ALU.add).then_inc(y_done, 1)
                dve.wait_ge(out_done, g + 1)
                dve.wait_ge(x_loaded, 32 * (g + 1))
                for h in range(2):
                    xr = xres[:, bass.ds(g * GB + 2 * h, 2), 0:C]
                    last = dve.tensor_tensor(summed[:, 2 * h:2 * h + 2, :], p_ps[0:T, h, :].rearrange("p (b c) -> p b c", b=2),
                                             xr, ALU.add)
                last.then_inc(res_done, 1)
                dve.wait_ge(res_done, g + 1)
                for b in range(GB):
                    last = dve.bn_stats(stats[:, b, :], summed[:, b, :])
                last.then_inc(stats_done, 1)
                dve.wait_ge(ready, 1)
                dve.wait_ge(stats_done, g + 1)
                for b in range(GB):
                    last = dve.bn_aggr(mv[:, b, :], stats[:, b, :])
                last.then_inc(mv_done, 1)
                dve.wait_ge(mv_done, g + 1)
                dve.tensor_scalar(veps[:], mv[:, :, 1], LN_EPS, None, ALU.add).then_inc(veps_done, 1)
                dve.wait_ge(rstd_done, g + 1)
                for b in range(GB):
                    xr = xres[:, bass.ds(g * GB + b, 1), 0:C].rearrange("p b c -> p (b c)")
                    last = dve.tensor_scalar(xr, summed[:, b, :], mv[:, b, 0:1], rstd[:, b:b + 1], ALU.subtract, ALU.mult)
                last.then_inc(norm_done, 1)
            dve.wait_ge(norm_done, GROUPS)


def attention_phase(nc, xres, logits, ident_sb, ctxT, mask, mask_pick, Wq, Wk, Wv, Wo, inv_temp, Wr, br):
    ctx = ExitStack()
    with ctx:
        def sb(name, shape, dt=F32):
            return ctx.enter_context(nc.sbuf_tensor("x_" + name, shape, dt))

        def ps(name, shape, dt=F32):
            return ctx.enter_context(nc.psum_tensor("x_" + name, shape, dt))

        def sem(name):
            return ctx.enter_context(nc.semaphore("x_" + name))

        wq = sb("wq", [128, KC, INNERX])
        wk = sb("wk", [128, KC, INNERX])
        wv = sb("wv", [128, KC, INNERX])
        wo = sb("wo", [128, PAIRS, C])
        wr = sb("wr", [128, KC, E])
        br_sb = sb("br_sb", [T, E])
        temp = sb("temp", [128, H])
        mask_u8 = sb("mask_u8", [B, S2], U8)
        mask_bias = sb("mask_bias", [128, S2], BF16)
        pick = sb("pick", [128, B, T], BF16)
        ctx_sb = [sb(f"ctx_sb{i}", [128, KC, S2]) for i in range(2)]
        xT = sb("xT_att", [128, KC, T])
        qT = sb("qT", [128, PAIRS, T])
        kT = sb("kT", [128, PAIRS, S2])
        v = sb("v", [SC, NSC, H, DH + 1])
        work = sb("work", [T, 2, S2])
        top = sb("top", [T, 2, 2, TOPK])
        s_sb = sb("s_sb", [T, 4, S2])
        prob = sb("prob", [T, 4, S2])
        nmax = sb("nmax", [T, 4])
        full_sum = sb("full_sum", [T, H])
        kept = sb("kept", [T, 2, S2])
        total = sb("total", [T, H])
        rtotal = sb("rtotal", [T, H])
        pT = sb("pT", [SC, 2, NSC, T])
        o = sb("o", [T, 8, DH])
        oT = sb("oT", [128, PAIRS, T])
        summed = sb("summed_att", [T, C])
        stats = sb("stats_att", [T, 6])
        mv = sb("mv_att", [T, 2])
        veps = sb("veps_att", [T, 1])
        rstd = sb("rstd_att", [T, 1])
        neghalf = sb("neghalf_att", [T, 1])
        x_stage = sb("x_stage", [T, C])
        x2 = sb("x2", [T, C])
        x2T = sb("x2T", [128, KC, T])

        s_ps = ps("s_ps", [T, 2, 512])
        pT_ps = ps("pT_ps", [SC, 2, 512])
        o_ps = ps("o_ps", [T, 2, 512])
        w_ps = ps("w_ps", [128, 2, 512])

        loaded = sem("att_loaded")
        ctx_loaded = [sem(f"ctx_loaded{i}") for i in range(2)]
        masked = sem("masked")
        wq_done = sem("wq_done")
        half_done = sem("att_half_done")
        xT_done, xT_copied = sem("xT_done"), sem("xT_copied")
        kq_done, kq_copied = sem("kq_done"), sem("kq_copied")
        v_done, v_copied = sem("v_done"), sem("v_copied")
        s_done, s_copied, max_done, rep_done = sem("s_done"), sem("s_copied"), sem("max_done"), sem("rep_done")
        nmax_done, exp_done, kept_done, p_done = sem("nmax_done"), sem("exp_done"), sem("kept_done"), sem("p_done")
        pT_done, pT_copied, pv_done = sem("pT_done"), sem("pT_copied"), sem("pv_done")
        total_done, rtotal_done, o_done = sem("total_done"), sem("rtotal_done"), sem("o_done")
        oT_done, oT_copied, wo_done = sem("oT_done"), sem("oT_copied"), sem("wo_done")
        sum_done, stats_done, mv_done = sem("sum_done"), sem("stats_done_att"), sem("mv_done_att")
        veps_done, rstd_done, x2_done = sem("veps_done_att"), sem("rstd_done_att"), sem("x2_done")
        x2T_done, x2T_copied = sem("x2T_done"), sem("x2T_copied")
        stage_done, x2_kept = sem("stage_done"), sem("x2_kept")
        lg_done, lg_copied = sem("lg_done"), sem("lg_copied")

        LOADS = 16 * 9
        scale = float(DH) ** -0.5

        def run(eng, batch, lead_in, lead_out):
            lead_in((0, 0, 0))
            batch((0, 0, 0), (1, 0, 1), False, True)
            with eng.Fori(0, B // 2 - 1) as i:
                batch((2 * i + 1, i, 1), (2 * i + 2, i + 1, 0), True, True)
                batch((2 * i + 2, i + 1, 0), (2 * i + 3, i + 1, 1), True, True)
            batch((B - 1, B // 2 - 1, 1), (B, B // 2, 0), True, False)
            lead_out((B - 1, B // 2 - 1, 1))

        block = ctx.enter_context(nc.Block())

        @block.sync
        def _(sp):
            sp.dma_start(mask_u8[:], mask).then_inc(loaded, 16)
            sp.dma_start(wq[:], Wq.rearrange("(k p) e -> p k e", p=128)).then_inc(loaded, 16)
            sp.dma_start(temp[:], inv_temp.rearrange("(a h) -> a h", a=1).to_broadcast([128, H])).then_inc(loaded, 16)
            sp.dma_start(wk[:], Wk.rearrange("(k p) e -> p k e", p=128)).then_inc(loaded, 16)
            sp.dma_start(pick[:], mask_pick).then_inc(loaded, 16)
            sp.dma_start(wv[:], Wv.rearrange("(k p) e -> p k e", p=128)).then_inc(loaded, 16)
            sp.dma_start(wo[:], Wo.rearrange("(k p) e -> p k e", p=128)).then_inc(loaded, 16)
            sp.dma_start(wr[:], Wr.rearrange("(k p) e -> p k e", p=128)).then_inc(loaded, 16)
            sp.dma_start(br_sb[:], br.rearrange("(a h) -> a h", a=1).to_broadcast([T, E])).then_inc(loaded, 16)
            src = ctxT.rearrange("b (k p) s -> b p k s", p=128)
            for b in range(2):
                sp.dma_start(ctx_sb[b][:], src[b]).then_inc(ctx_loaded[b], 16)
            with sp.Fori(0, B // 2 - 1) as i:
                for p in range(2):
                    sp.wait_ge(loaded, LOADS)
                    sp.wait_ge(v_done, (2 * i + p) * PAIRS + PAIRS)
                    sp.dma_start(ctx_sb[p][:], src[bass.ds(2 * i + p + 2, 1)].rearrange("b p k s -> p (b k) s")).then_inc(
                        ctx_loaded[p], 16)

        @block.tensor
        def _(pe):
            def x_transpose(b):
                n, _, _ = b
                pe.wait_ge(stage_done, n + 1)
                for k in range(KC):
                    mm = pe.transpose(w_ps[:, 1, k * T:(k + 1) * T], x_stage[:, k * 128:(k + 1) * 128], ident_sb[0:T, 0:T])
                mm.then_inc(xT_done, 1)

            def keys_queries(b, p):
                n, half, par = b
                if p == 0:
                    pe.wait_ge(ctx_loaded[par], 16 * (half + 1))
                    pe.wait_ge(xT_copied, n + 1)
                pe.wait_ge(kq_copied, n * PAIRS + p)
                for k in range(KC):
                    pe.matmul(w_ps[:, 0, 0:S2], wk[:, k, p * 128:(p + 1) * 128], ctx_sb[par][:, k, :],
                              start=(k == 0), stop=(k == KC - 1))
                for k in range(KC):
                    mm = pe.matmul(w_ps[:, 0, 384:384 + T], wq[:, k, p * 128:(p + 1) * 128], xT[:, k, :],
                                   start=(k == 0), stop=(k == KC - 1))
                mm.then_inc(kq_done, 1)

            def values(b, p):
                n, half, par = b
                pe.wait_ge(v_copied, n * PAIRS + p)
                for c in range(NSC):
                    for k in range(KC):
                        mm = pe.matmul(w_ps[0:SC, 1, c * 128:(c + 1) * 128], ctx_sb[par][:, k, c * SC:(c + 1) * SC],
                                       wv[:, k, p * 128:(p + 1) * 128], start=(k == 0), stop=(k == KC - 1))
                mm.then_inc(v_done, 1)

            def scores(b, p):
                n, _, _ = b
                for hh in range(2):
                    h = 2 * p + hh
                    at = slice(64 * hh, 64 * hh + 64)
                    pe.wait_ge(loaded, LOADS)
                    if not (isinstance(n, int) and n == 0 and h < 2):
                        pe.wait_ge(s_copied, n * H + (h - 1))
                    pe.matmul(s_ps[:, hh, 0:S2], pick[:, bass.ds(n, 1), :].rearrange("p b t -> p (b t)"), mask_bias[:],
                              start=True, stop=False)
                    if hh == 0:
                        pe.wait_ge(kq_copied, n * PAIRS + p + 1)
                    pe.matmul(s_ps[:, hh, 0:S2], qT[at, p, :], kT[at, p, :], start=False, stop=True).then_inc(s_done, 1)

            def prob_transpose(b, p, hh):
                n, _, _ = b
                h = 2 * p + hh
                pe.wait_ge(p_done, n * H + h + 1)
                if not (isinstance(n, int) and n == 0 and h < 2):
                    pe.wait_ge(pT_copied, n * H + (h - 1))
                for c in range(NSC):
                    mm = pe.transpose(pT_ps[:, hh, c * T:(c + 1) * T], prob[:, h % 4, c * SC:(c + 1) * SC], ident_sb[0:T, 0:T])
                mm.then_inc(pT_done, 1)

            def prob_values(b, p, hh):
                n, _, _ = b
                h = 2 * p + hh
                pe.wait_ge(pT_copied, n * H + h + 1)
                if hh == 0:
                    pe.wait_ge(v_copied, n * PAIRS + p + 1)
                if h % 8 == 0:
                    pe.wait_ge(o_done, n * 2 + h // 8)
                for c in range(NSC):
                    at = slice(h % 4 * (DH + 1), (h % 4 + 1) * (DH + 1))
                    mm = pe.matmul(o_ps[:, h % 8 // 4, at], pT[:, hh, c, :], v[:, c, h, :],
                                   start=(c == 0), stop=(c == NSC - 1))
                if hh == 1:
                    mm.then_inc(pv_done, 1)

            def out_transpose(b, half):
                n, _, _ = b
                pe.wait_ge(o_done, n * 2 + half + 1)
                for q in range(4):
                    mm = pe.transpose(w_ps[:, 1, q * T:(q + 1) * T], o[:, 2 * q:2 * q + 2, :].rearrange("p h d -> p (h d)"),
                                      ident_sb[0:T, 0:T])
                mm.then_inc(oT_done, 1)

            def out_project(b):
                n, _, _ = b
                pe.wait_ge(oT_copied, n * 2 + 2)
                for p in range(PAIRS):
                    mm = pe.matmul(w_ps[0:T, 1, 0:C], oT[:, p, :], wo[:, p, :], start=(p == 0), stop=(p == PAIRS - 1))
                mm.then_inc(wo_done, 1)

            def x2_transpose(b):
                n, _, _ = b
                pe.wait_ge(x2_done, n + 1)
                for k in range(KC):
                    mm = pe.transpose(w_ps[:, 1, k * T:(k + 1) * T], x2[:, k * 128:(k + 1) * 128], ident_sb[0:T, 0:T])
                mm.then_inc(x2T_done, 1)

            def router(b):
                n, _, _ = b
                pe.wait_ge(x2T_copied, n + 1)
                for k in range(KC):
                    mm = pe.matmul(w_ps[0:T, 1, 0:E], x2T[:, k, :], wr[:, k, :], start=(k == 0), stop=(k == KC - 1))
                mm.then_inc(lg_done, 1)

            def before(b):
                return (b[0] - 1, None, None)

            def lead_in(b):
                pe.wait_ge(loaded, LOADS)
                pe.wait_ge(wq_done, 1)
                pe.wait_ge(masked, 2)
                x_transpose(b)
                for p in range(PAIRS):
                    keys_queries(b, p)
                    if p > 1:
                        values(b, p - 2)
                pe.wait_ge(v_copied, PAIRS - 2)
                x_transpose((1, 0, 1))
                scores(b, 0)

            def batch(b, nb, has_prev, has_next):
                for j in range(PAIRS):
                    prev, p = (b, j - 1) if j else (before(b), PAIRS - 1)
                    prev2, p2 = (b, j - 2) if j > 1 else (before(b), PAIRS - 2 + j)
                    if j > 1 or has_prev:
                        prob_values(prev2, p2, 1)
                    if j < PAIRS - 1:
                        scores(b, j + 1)
                    elif has_next:
                        scores(nb, 0)
                    if has_next:
                        keys_queries(nb, j)
                    if j or has_prev:
                        prob_transpose(prev, p, 0)
                    if j < 2:
                        if j == 0:
                            pe.wait_ge(xT_copied, b[0] + 2)
                        values(b, PAIRS - 2 + j)
                    elif has_next:
                        if j == 2 and has_prev:
                            pe.wait_ge(sum_done, b[0])
                        if j == 5 and has_prev:
                            pe.wait_ge(x2T_copied, b[0])
                        if j == 6 and has_prev:
                            pe.wait_ge(lg_copied, b[0])
                        if j == 7:
                            pe.wait_ge(oT_copied, b[0] * 2 + 1)
                        values(nb, j - 2)
                    if j or has_prev:
                        prob_transpose(prev, p, 1)
                        prob_values(prev, p, 0)
                    copied = b[0] * PAIRS + PAIRS - 1 + j
                    if j == 1 and has_prev:
                        pe.wait_ge(v_copied, copied)
                        out_transpose(before(b), 1)
                        out_project(before(b))
                    if j == 4 and has_prev:
                        if has_next:
                            pe.wait_ge(v_copied, copied)
                        x2_transpose(before(b))
                    if j == 5 and has_prev:
                        if has_next:
                            pe.wait_ge(v_copied, copied)
                        router(before(b))
                    if j == 6:
                        if has_next:
                            pe.wait_ge(v_copied, copied)
                        else:
                            pe.wait_ge(lg_copied, b[0])
                        out_transpose(b, 0)
                    if j == PAIRS - 1 and has_next:
                        pe.wait_ge(v_copied, copied)
                        x_transpose((nb[0] + 1, None, None))

            def lead_out(b):
                prob_values(b, PAIRS - 2, 1)
                prob_transpose(b, PAIRS - 1, 0)
                prob_transpose(b, PAIRS - 1, 1)
                prob_values(b, PAIRS - 1, 0)
                prob_values(b, PAIRS - 1, 1)
                pe.wait_ge(oT_copied, 2 * b[0] + 1)
                out_transpose(b, 1)
                out_project(b)
                x2_transpose(b)
                router(b)

            run(pe, batch, lead_in, lead_out)

        @block.scalar
        def _(act):
            def x_copy(n):
                act.wait_ge(xT_done, n + 1)
                act.wait_ge(kq_done, n * PAIRS)
                act.activation(xT[:].rearrange("p k t -> p (k t)"), w_ps[:, 1, 0:KC * T], ACT.Copy).then_inc(xT_copied, 1)

            def keys_queries(b, p):
                n, _, _ = b
                act.wait_ge(kq_done, n * PAIRS + p + 1)
                if not (isinstance(n, int) and n == 0):
                    act.wait_ge(s_done, (n - 1) * H + 2 * p + 2)
                act.activation(kT[:, p, :], w_ps[:, 0, 0:S2], ACT.Copy)
                act.activation(qT[:, p, :], w_ps[:, 0, 384:384 + T], ACT.Copy).then_inc(kq_copied, 1)

            def values(b, p):
                n, _, _ = b
                act.wait_ge(v_done, n * PAIRS + p + 1)
                if not (isinstance(n, int) and n == 0):
                    act.wait_ge(pv_done, (n - 1) * PAIRS + p + 1)
                act.activation(v[:, :, 2 * p:2 * p + 2, 0:DH],
                               w_ps[0:SC, 1, 0:NSC * 128].rearrange("p (c h d) -> p c h d", c=NSC, h=2),
                               ACT.Copy).then_inc(v_copied, 1)

            def prob_copy(b, p, hh):
                n, _, _ = b
                h = 2 * p + hh
                act.wait_ge(pT_done, n * H + h + 1)
                if not (isinstance(n, int) and n == 0 and p == 0):
                    act.wait_ge(pv_done, n * PAIRS + p)
                act.activation(pT[:, hh, :, :].rearrange("p c t -> p (c t)"), pT_ps[:, hh, 0:NSC * T], ACT.Copy).then_inc(pT_copied, 1)

            def score_copy(b, p, hh):
                n, _, _ = b
                h = 2 * p + hh
                act.wait_ge(s_done, n * H + h + 1)
                if not (isinstance(n, int) and n == 0 and h < 4):
                    act.wait_ge(kept_done, n * H + (h - 3))
                act.activation(s_sb[:, h % 4, :], s_ps[:, hh, 0:S2], ACT.Copy).then_inc(s_copied, 1)

            def exps(b, p, hh):
                n, _, _ = b
                h = 2 * p + hh
                act.wait_ge(nmax_done, n * H + h + 1)
                if not (isinstance(n, int) and n == 0 and h < 4):
                    act.wait_ge(pT_done, n * H + (h - 3))
                act.activation(prob[:, h % 4, :], s_sb[:, h % 4, :], ACT.Exp, bias=nmax[:, h % 4:h % 4 + 1], scale=scale,
                               accum_out=full_sum[:, h:h + 1]).then_inc(exp_done, 1)

            def out_copy(b, half):
                n, _, _ = b
                act.wait_ge(oT_done, n * 2 + half + 1)
                if not (isinstance(n, int) and n == 0):
                    act.wait_ge(wo_done, n)
                act.activation(oT[:, 4 * half:4 * half + 4, :].rearrange("p q t -> p (q t)"), w_ps[:, 1, 0:4 * T],
                               ACT.Copy).then_inc(oT_copied, 1)

            def x2_copy(b):
                n, _, _ = b
                act.wait_ge(x2T_done, n + 1)
                act.wait_ge(lg_done, n)
                act.activation(x2T[:].rearrange("p k t -> p (k t)"), w_ps[:, 1, 0:KC * T], ACT.Copy).then_inc(x2T_copied, 1)

            def before(b):
                return (b[0] - 1, None, None)

            def lead_in(b):
                x_copy(0)
                for p in range(PAIRS):
                    keys_queries(b, p)
                    if p > 1:
                        values(b, p - 2)
                x_copy(1)
                score_copy(b, 0, 0)
                score_copy(b, 0, 1)

            def batch(b, nb, has_prev, has_next):
                for j in range(PAIRS):
                    prev, p = (b, j - 1) if j else (before(b), PAIRS - 1)
                    exps(b, j, 0)
                    exps(b, j, 1)
                    if j < PAIRS - 1:
                        score_copy(b, j + 1, 0)
                    elif has_next:
                        score_copy(nb, 0, 0)
                    if has_next:
                        keys_queries(nb, j)
                    if j or has_prev:
                        prob_copy(prev, p, 0)
                    if j < PAIRS - 1:
                        score_copy(b, j + 1, 1)
                    elif has_next:
                        score_copy(nb, 0, 1)
                    if j < 2:
                        values(b, PAIRS - 2 + j)
                    elif has_next:
                        values(nb, j - 2)
                    if j or has_prev:
                        prob_copy(prev, p, 1)
                    if j == 1 and has_prev:
                        out_copy(before(b), 1)
                    if j == 4 and has_prev:
                        x2_copy(before(b))
                    if j == 6:
                        out_copy(b, 0)
                    if j == PAIRS - 1 and has_next:
                        x_copy(nb[0] + 1)

            def lead_out(b):
                prob_copy(b, PAIRS - 1, 0)
                prob_copy(b, PAIRS - 1, 1)
                out_copy(b, 1)
                x2_copy(b)

            run(act, batch, lead_in, lead_out)

        @block.gpsimd
        def _(pool):
            pool.memset(neghalf[:], -0.5).then_inc(half_done, 1)
            pool.wait_ge(half_done, 1)

            def stage(n):
                pool.wait_ge(half_done, 1)
                pool.wait_ge(xT_done, n)
                pool.tensor_copy(x_stage[:], xres[:, bass.ds(n, 1), 0:C].rearrange("p b c -> p (b c)")).then_inc(stage_done, 1)

            def lead_in(b):
                stage(0)
                stage(1)

            def keep(n):
                pool.wait_ge(half_done, 1)
                pool.wait_ge(x2_done, n + 1)
                pool.tensor_copy(xres[:, bass.ds(n, 1), 0:C].rearrange("p b c -> p (b c)"), x2[:]).then_inc(x2_kept, 1)

            def norm(n):
                pool.wait_ge(veps_done, n + 1)
                pool.tensor_tensor(rstd[:], veps[:], neghalf[:], ALU.pow).then_inc(rstd_done, 1)

            def keep_mask(b, p, hh):
                n, _, _ = b
                waits = [(max_done, n * 64 + p * 8 + 6 + hh + 1)]
                if not (isinstance(n, int) and n == 0 and p == 0):
                    waits.append((p_done, n * H + (2 * p + hh - 1)))
                wait_apart(pool, half_done, *waits)
                pool.tensor_scalar(kept[:, hh, :], s_sb[:, (2 * p + hh) % 4, :], top[:, p % 2, hh, TOPK - 1:TOPK], None,
                                   ALU.is_ge).then_inc(kept_done, 1)

            def keep_probs(b, p, hh):
                n, _, _ = b
                h = 2 * p + hh
                pool.wait_ge(kept_done, n * H + h + 1)
                pool.wait_ge(exp_done, n * H + h + 1)
                pool.tensor_tensor(prob[:, h % 4, :], prob[:, h % 4, :], kept[:, hh, :], ALU.mult).then_inc(p_done, 1)

            def max_negate(b, j, hh):
                n, _, _ = b
                h = 2 * j + hh
                if not (isinstance(n, int) and n == 0 and h < 4):
                    pool.wait_ge(exp_done, n * H + (h - 3))
                wait_apart(pool, half_done, (max_done, n * 64 + j * 8 + hh + 1))
                pool.tensor_scalar(nmax[:, h % 4:h % 4 + 1], top[:, j % 2, hh, 0:1], -scale, 0.0, ALU.mult, ALU.add).then_inc(
                    nmax_done, 1)

            def before(b):
                return (b[0] - 1, None, None)

            def batch(b, nb, has_prev, has_next):
                n = b[0]
                for j in range(PAIRS):
                    prev, p = (b, j - 1) if j else (before(b), PAIRS - 1)
                    if j or has_prev:
                        keep_mask(prev, p, 0)
                    max_negate(b, j, 0)
                    max_negate(b, j, 1)
                    if j or has_prev:
                        keep_probs(prev, p, 0)
                        keep_mask(prev, p, 1)
                        keep_probs(prev, p, 1)
                    if j == 3 and has_prev:
                        norm(n - 1)
                    if j == 5 and has_prev:
                        keep(n - 1)
                    if j == 5 and has_next:
                        stage(n + 2)

            def lead_out(b):
                for hh in range(2):
                    keep_mask(b, PAIRS - 1, hh)
                    keep_probs(b, PAIRS - 1, hh)
                norm(b[0])
                keep(b[0])

            run(pool, batch, lead_in, lead_out)

        @block.vector
        def _(dve):
            def half_out(b, half, part):
                n, _, _ = b
                hs = slice(8 * half, 8 * half + 8)
                m = n * 2 + half + 1
                o_half = o_ps[:, :, 0:4 * (DH + 1)].rearrange("p k (h d) -> p k h d", d=DH + 1)
                if part == 0:
                    dve.wait_ge(pv_done, n * PAIRS + 4 * half + 4)
                    dve.scalar_tensor_tensor(total[:, hs].rearrange("p (k h) -> p k h", k=2),
                                             full_sum[:, hs].rearrange("p (k h) -> p k h", k=2), 1e-8, o_half[:, :, :, DH],
                                             ALU.mult, ALU.add).then_inc(total_done, 1)
                if part == 1:
                    dve.wait_ge(total_done, m)
                    dve.reciprocal(rtotal[:, hs], total[:, hs]).then_inc(rtotal_done, 1)
                if part == 2:
                    dve.wait_ge(rtotal_done, m)
                    dve.wait_ge(oT_done, m - 1)
                    dve.tensor_tensor(o[:].rearrange("p (k h) d -> p k h d", k=2), o_half[:, :, :, 0:DH],
                                      rtotal[:, hs].rearrange("p (k h) -> p k h", k=2).unsqueeze(3).to_broadcast([T, 2, 4, DH]),
                                      ALU.mult).then_inc(o_done, 1)

            def residual(b, part):
                n, _, _ = b
                xr = xres[:, bass.ds(n, 1), 0:C].rearrange("p b c -> p (b c)")
                if part == 0:
                    dve.wait_ge(wo_done, n + 1)
                    dve.tensor_tensor(summed[:], w_ps[0:T, 1, 0:C], xr, ALU.add).then_inc(sum_done, 1)
                if part == 1:
                    dve.wait_ge(sum_done, n + 1)
                    dve.bn_stats(stats[:], summed[:]).then_inc(stats_done, 1)
                if part == 2:
                    dve.wait_ge(wq_done, 1)
                    dve.wait_ge(stats_done, n + 1)
                    dve.bn_aggr(mv[:], stats[:]).then_inc(mv_done, 1)
                if part == 3:
                    dve.wait_ge(mv_done, n + 1)
                    dve.tensor_scalar(veps[:], mv[:, 1:2], LN_EPS, None, ALU.add).then_inc(veps_done, 1)
                if part == 4:
                    dve.wait_ge(rstd_done, n + 1)
                    dve.wait_ge(x2T_done, n)
                    dve.wait_ge(x2_kept, n)
                    dve.tensor_scalar(x2[:], summed[:], mv[:, 0:1], rstd[:, 0:1], ALU.subtract, ALU.mult).then_inc(x2_done, 1)

            def logit_copy(b):
                n, _, _ = b
                dve.wait_ge(lg_done, n + 1)
                dve.tensor_tensor(logits[:, bass.ds(n, 1), :].rearrange("p b e -> p (b e)"), w_ps[0:T, 1, 0:E], br_sb[:],
                                  ALU.add).then_inc(lg_copied, 1)

            def before(b):
                return (b[0] - 1, None, None)

            def lead_in(b):
                dve.memset(v[:, :, :, DH:DH + 1], 1.0)
                dve.memset(mask_bias[:], 0.0).then_inc(masked, 1)
                dve.wait_ge(masked, 1)
                dve.wait_ge(loaded, LOADS)
                dve.tensor_scalar(mask_bias[0:B, :], mask_u8[:], 1.0, 1e30, ALU.subtract, ALU.mult).then_inc(masked, 1)
                for k in range(KC):
                    w = wq[:, k, :].rearrange("p (h d) -> p h d", h=H)
                    last = dve.tensor_tensor(w, w, temp[:].unsqueeze(2).to_broadcast([128, H, DH]), ALU.mult)
                last.then_inc(wq_done, 1)

            def batch(b, nb, has_prev, has_next):
                n = b[0]
                for j in range(PAIRS):
                    for r in range(TOPK // 8):
                        for hh in range(2):
                            h = 2 * j + hh
                            src = s_sb[:, h % 4, :] if r == 0 else work[:, hh, :]
                            if r == 0:
                                wait_apart(dve, wq_done, (s_copied, n * H + h + 1))
                            else:
                                wait_apart(dve, wq_done, (rep_done, n * 48 + j * 6 + 2 * (r - 1) + hh + 1))
                            dve.max(top[:, j % 2, hh, 8 * r:8 * r + 8], src).then_inc(max_done, 1)
                        if j == 1 and has_prev and r < 3:
                            half_out(before(b), 1, r)
                        if j == 5 and r < 3:
                            half_out(b, 0, r)
                        if r == TOPK // 8 - 1:
                            break
                        for hh in range(2):
                            h = 2 * j + hh
                            src = s_sb[:, h % 4, :] if r == 0 else work[:, hh, :]
                            wait_apart(dve, wq_done, (max_done, n * 64 + j * 8 + 2 * r + hh + 1))
                            dve.match_replace(work[:, hh, :], top[:, j % 2, hh, 8 * r:8 * r + 8], src, GONE).then_inc(rep_done, 1)
                        if j == 2 and has_prev and r < 2:
                            residual(before(b), r)
                        if j == 3 and has_prev and r < 2:
                            residual(before(b), 2 + r)
                        if j == 4 and has_prev and r == 0:
                            residual(before(b), 4)
                        if j == 6 and has_prev and r == 0:
                            logit_copy(before(b))

            def lead_out(b):
                for part in range(3):
                    half_out(b, 1, part)
                for part in range(5):
                    residual(b, part)
                logit_copy(b)

            run(dve, batch, lead_in, lead_out)
            dve.wait_ge(x2_kept, B)
            dve.wait_ge(lg_copied, B)


def expert_phase(nc, xres, logits, ident_sb, lower, W1, b1T, W2, b2, fin, xg, out):
    ctx = ExitStack()
    with ctx:
        def sb(name, shape, dt=F32):
            return ctx.enter_context(nc.sbuf_tensor("e_" + name, shape, dt))

        def ps(name, shape, dt=F32):
            return ctx.enter_context(nc.psum_tensor("e_" + name, shape, dt))

        def sem(name):
            return ctx.enter_context(nc.semaphore("e_" + name))

        BE = B * E
        lower_sb = sb("lower_sb", [T, 2, T], BF16)
        first = sb("first", [T, E])
        token = sb("token", [T, B])
        reset = sb("reset", [T, E, B])
        pick1, pick2 = sb("pick1", [T, B, E]), sb("pick2", [T, B, E])
        rest, tmp = sb("rest", [T, B, E]), sb("tmp", [T, B, E])
        sel = sb("sel", [T, B, E], BF16)
        val = sb("val", [T, 2, B])
        where = sb("where", [T, 2, B])
        gate = sb("gate", [T, 2, B])
        den = sb("den", [T, B])
        count = sb("count", [T, E, B])
        upto = sb("upto", [T, E, B])
        rank = sb("rank", [T, B, E])
        rankc = sb("rankc", [T, 2, B])
        over = sb("over", [T, 2, B])
        slot_f = sb("slot_f", [T, 2, B])
        slot = sb("slot", [T, 2, B], I32)
        target = sb("target", [T, 2, B], I32)
        w1 = [sb(f"w1_{i}", [128, KC, HID]) for i in range(2)]
        w2 = [sb(f"w2_{i}", [128, HM, C]) for i in range(2)]
        b1_sb = [sb(f"b1_{i}", [128, HM]) for i in range(2)]
        b2_sb = sb("b2_sb", [128, E, C])
        rows = [sb(f"rows{i}", [128, NT, CX]) for i in range(2)]
        rowsT = [sb(f"rowsT{i}", [128, KC, CAP]) for i in range(2)]
        hT = sb("hT", [128, HM, CAP])
        ysum = sb("ysum_e", [128, 2, C])
        yrow = [sb(f"yrow{i}", [128, NT, C]) for i in range(2)]
        part = [sb(f"part{i}", [T, 2, GB, C]) for i in range(2)]
        stats = sb("stats_e", [T, GB, 6])
        mv = sb("mv_e", [T, GB, 2])
        veps = sb("veps_e", [T, GB])
        rstd = sb("rstd_e", [T, GB])
        neghalf = sb("neghalf_e", [T, GB])

        t_ps = ps("t_ps", [128, 2, 512])
        h_ps = ps("h_ps_e", [128, 4, 512])
        y_ps = ps("y_ps", [128, 2, 512])

        consts = sem("consts")
        pool_done = sem("pool_done")
        d = sem("route_step")
        exp_done = sem("gate_exp_done")
        counted = sem("counted")
        x_sent = [sem(f"x_sent{i}") for i in range(2)]
        aux_done = sem("aux_done")
        e_loaded = [sem(f"e_loaded{i}") for i in range(2)]
        rows_loaded = [sem(f"rows_loaded{i}") for i in range(2)]
        rt_done, rt_copied = sem("rt_done"), sem("rt_copied")
        h_done, h_copied = sem("h_done_e"), sem("h_copied")
        y_done, y_added, y_scaled = sem("y_done_e"), sem("y_added"), sem("y_scaled")
        y_sent = [sem(f"y_sent{i}") for i in range(2)]
        part_loaded = [sem(f"part_loaded{i}") for i in range(2)]
        add1_done, add2_done = sem("add1_done"), sem("add2_done")
        stats_done, mv_done, veps_done, rstd_done = sem("stats_done_e"), sem("mv_done_e"), sem("veps_done_e"), sem("rstd_done_e")
        norm_done = sem("norm_done_e")
        o_sent = [sem(f"o_sent{i}") for i in range(2)]

        block = ctx.enter_context(nc.Block())
        w1_v = W1.rearrange("e (k p) h -> e p k h", p=128)
        w2_v = W2.rearrange("e (m p) c -> e p m c", p=128)
        xg_v = xg.rearrange("(e i p) c -> e p i c", e=E, p=128)
        fin_v = fin.rearrange("(c b t) d -> b t c d", c=2, t=T)
        out_v = out.rearrange("b t c -> t b c")

        @block.sync
        def _(sp):
            sp.dma_start(lower_sb[:], lower).then_inc(consts, 16)
            sp.dma_start(b2_sb[:], b2.rearrange("(a e) c -> a e c", a=1).to_broadcast([128, E, C])).then_inc(consts, 16)
            for p in range(2):
                sp.dma_start(w1[p][:], w1_v[p]).then_inc(e_loaded[p], 16)
                sp.dma_start(w2[p][:], w2_v[p]).then_inc(e_loaded[p], 16)
                sp.dma_start(b1_sb[p][:], b1T[p]).then_inc(e_loaded[p], 16)
            sp.wait_ge(x_sent[0], 16 * B)
            sp.wait_ge(x_sent[1], 16 * B)
            for p in range(2):
                sp.dma_start(rows[p][:], xg_v[p]).then_inc(rows_loaded[p], 16)
            with sp.Fori(0, E // 2 - 1) as i:
                for p in range(2):
                    e = 2 * i + p
                    sp.wait_ge(consts, 32)
                    sp.wait_ge(h_copied, 16 * e + 16)
                    sp.dma_start(w1[p][:], w1_v[bass.ds(e + 2, 1)].rearrange("e p k h -> p (e k) h")).then_inc(e_loaded[p], 16)
                    sp.dma_start(b1_sb[p][:], b1T[bass.ds(e + 2, 1)].rearrange("e p m -> p (e m)")).then_inc(e_loaded[p], 16)
                    sp.wait_ge(y_done, NT * e + NT)
                    sp.dma_start(w2[p][:], w2_v[bass.ds(e + 2, 1)].rearrange("e p k h -> p (e k) h")).then_inc(e_loaded[p], 16)
                    sp.wait_ge(y_sent[p], 16 * NT * (i + 1))
                    sp.dma_start(rows[p][:], xg_v[bass.ds(e + 2, 1)].rearrange("e p i c -> p (e i) c")).then_inc(rows_loaded[p], 16)
            for p in range(2):
                sp.wait_ge(y_sent[p], 16 * NT * (E // 2))
            for g in range(2):
                for c in range(2):
                    sp.dma_start(part[g][:, c], fin_v[g * GB:(g + 1) * GB, :, c, :].rearrange("b t d -> t b d")).then_inc(part_loaded[g], 16)
            for g in range(GROUPS):
                p = g % 2
                sp.wait_ge(norm_done, g + 1)
                sp.dma_start(out_v[:, g * GB:(g + 1) * GB, :], part[p][:, 0]).then_inc(o_sent[p], 16)
                if g + 2 < GROUPS:
                    sp.wait_ge(o_sent[p], 16 * (g // 2 + 1))
                    for c in range(2):
                        sp.dma_start(part[p][:, c], fin_v[(g + 2) * GB:(g + 3) * GB, :, c, :].rearrange("b t d -> t b d")).then_inc(
                            part_loaded[p], 16)
            for p in range(2):
                sp.wait_ge(o_sent[p], 16 * (GROUPS // 2))

        @block.gpsimd
        def _(pool):
            pool.memset(neghalf[:], -0.5).then_inc(pool_done, 1)
            pool.iota(first[:], [[-1, E]], base=E, channel_multiplier=0, allow_small_or_imprecise_dtypes=True).then_inc(pool_done, 1)
            pool.iota(token[:], [[T, B]], base=0, channel_multiplier=1, allow_small_or_imprecise_dtypes=True).then_inc(pool_done, 1)
            for c in range(2):
                pool.wait_ge(aux_done, c + 1)
                for b in range(B):
                    pool.indirect_dma_start(xg, bass.IndirectOffsetOnAxis(ap=slot[:, c, b:b + 1], axis=0), xres[:, b, :], None,
                                            bounds_check=E * CAP - 1, oob_is_err=False).then_inc(x_sent[c], 16)
            bound = pool.to_reg(2 * N - 1)
            with pool.Fori(0, E // 2) as i:
                for p in range(2):
                    for t in range(NT):
                        wait_apart(pool, pool_done, (y_scaled, (2 * i + p) * NT + t + 1))
                        pool.indirect_dma_start(fin, bass.IndirectOffsetOnAxis(ap=rows[p][:, t, C + 1:C + 2].bitcast(I32), axis=0),
                                                yrow[p][:, t, :], None, bounds_check=bound, oob_is_err=False).then_inc(y_sent[p], 16)
            for g in range(GROUPS):
                pool.wait_ge(veps_done, g + 1)
                pool.tensor_tensor(rstd[:], veps[:], neghalf[:], ALU.pow).then_inc(rstd_done, 1)

        @block.tensor
        def _(pe):
            pe.wait_ge(consts, 32)
            pe.wait_ge(d, SEL_STEP)
            s = sel[:].rearrange("p b e -> p (b e)")
            pe.matmul(t_ps[0:T, 0, 0:BE], lower_sb[:, 0, :], s, start=True, stop=True)
            pe.matmul(t_ps[0:T, 1, 0:BE], lower_sb[:, 1, :], s, start=True, stop=True).then_inc(counted, 1)

            def turn(p, e, i):
                pe.wait_ge(rows_loaded[p], 16 * (i + 1))
                q = 0
                for k in range(KC):
                    for t in range(NT):
                        if q % 4 == 0:
                            n = e * TB + q // 4
                            if isinstance(n, int) and n < 2:
                                pass
                            else:
                                pe.wait_ge(rt_copied, n - 1)
                        mm = pe.transpose(t_ps[:, (q // 4) % 2, (q % 4) * 128:(q % 4 + 1) * 128], rows[p][:, t, k * 128:(k + 1) * 128], ident_sb[:])
                        q += 1
                        if q % 4 == 0 or q == KC * NT:
                            mm.then_inc(rt_done, 1)

            def expert(p, e, i, last):
                pe.wait_ge(e_loaded[p], 48 * (i + 1))
                pe.wait_ge(rt_copied, (e + 1) * TB)
                for m in range(HM):
                    for half in range(2):
                        n = e * 16 + 2 * m + half
                        if not (isinstance(n, int) and n < 4):
                            pe.wait_ge(h_copied, n - 3)
                        for k in range(KC):
                            mm = pe.matmul(h_ps[:, (2 * m + half) % 4, 0:HALF], w1[p][:, k, m * 128:(m + 1) * 128],
                                           rowsT[p][:, k, half * HALF:(half + 1) * HALF], start=(k == 0), stop=(k == KC - 1))
                        mm.then_inc(h_done, 1)
                if not last:
                    turn(1 - p, e + 1, i + p)
                for t in range(NT):
                    n = e * NT + t
                    if not (isinstance(n, int) and n < 2):
                        pe.wait_ge(y_added, n - 1)
                    if t == 0:
                        pe.wait_ge(h_copied, (e + 1) * 16)
                    for m in range(HM):
                        mm = pe.matmul(y_ps[:, (p * NT + t) % 2, 0:C], hT[:, m, t * 128:(t + 1) * 128], w2[p][:, m, :],
                                       start=(m == 0), stop=(m == HM - 1))
                    mm.then_inc(y_done, 1)

            pe.wait_ge(d, COUNT_STEP)
            turn(0, 0, 0)
            expert(0, 0, 0, False)
            with pe.Fori(0, E // 2 - 1) as i:
                expert(1, 2 * i + 1, i, False)
                expert(0, 2 * i + 2, i + 1, False)
            expert(1, E - 1, E // 2 - 1, True)

        @block.scalar
        def _(act):
            act.wait_ge(d, VAL_STEP)
            act.activation(gate[:, 1, :], gate[:, 1, :], ACT.Exp).then_inc(exp_done, 1)

            def turn(p, e):
                q = 0
                done = 0
                while q < KC * NT:
                    k = min(4, KC * NT - q)
                    act.wait_ge(rt_done, e * TB + done + 1)
                    if done == 0 and not (isinstance(e, int) and e < 2):
                        act.wait_ge(h_done, (e - 1) * 16)
                    flat = rowsT[p][:].rearrange("p k n -> p (k n)")
                    act.activation(flat[:, q * 128:(q + k) * 128], t_ps[:, done % 2, 0:k * 128], ACT.Copy).then_inc(rt_copied, 1)
                    q += k
                    done += 1

            def expert(p, e, last):
                for m in range(HM):
                    for half in range(2):
                        act.wait_ge(h_done, e * 16 + 2 * m + half + 1)
                        if m == 0 and half == 0:
                            act.wait_ge(y_done, e * NT)
                        act.activation(hT[:, m, half * HALF:(half + 1) * HALF], h_ps[:, (2 * m + half) % 4, 0:HALF], ACT.Gelu,
                                       bias=b1_sb[p][:, m:m + 1]).then_inc(h_copied, 1)
                if not last:
                    turn(1 - p, e + 1)

            turn(0, 0)
            expert(0, 0, False)
            with act.Fori(0, E // 2 - 1) as i:
                expert(1, 2 * i + 1, False)
                expert(0, 2 * i + 2, False)
            expert(1, E - 1, True)

        @block.vector
        def _(dve):
            def over_e(a):
                return a.unsqueeze(2).to_broadcast([T, B, E])

            first_b = first[:].unsqueeze(1).to_broadcast([T, B, E])
            n = [0]

            def step(ins):
                ins.then_inc(d, 1)
                n[0] += 1
                dve.wait_ge(d, n[0])

            dve.wait_ge(pool_done, 3)
            step(dve.memset(reset[:], 1.0))
            step(dve.memset(reset[:, :, 0:1], 0.0))
            step(dve.tensor_reduce(val[:, 0, :], logits[:], AX_X, ALU.max))
            step(dve.tensor_tensor(tmp[:], logits[:], over_e(val[:, 0, :]), ALU.is_equal))
            step(dve.tensor_tensor(tmp[:], tmp[:], first_b, ALU.mult))
            step(dve.tensor_reduce(where[:, 0, :], tmp[:], AX_X, ALU.max))
            step(dve.tensor_tensor(pick1[:], over_e(where[:, 0, :]), first_b, ALU.is_equal))
            step(dve.scalar_tensor_tensor(rest[:], pick1[:], GONE, logits[:], ALU.mult, ALU.add))
            step(dve.tensor_reduce(val[:, 1, :], rest[:], AX_X, ALU.max))
            step(dve.tensor_tensor(tmp[:], rest[:], over_e(val[:, 1, :]), ALU.is_equal))
            step(dve.tensor_tensor(tmp[:], tmp[:], first_b, ALU.mult))
            step(dve.tensor_reduce(where[:, 1, :], tmp[:], AX_X, ALU.max))
            step(dve.tensor_tensor(pick2[:], over_e(where[:, 1, :]), first_b, ALU.is_equal))
            step(dve.tensor_tensor(sel[:], pick1[:], pick2[:], ALU.add))
            assert n[0] == SEL_STEP
            step(dve.tensor_tensor(gate[:, 1, :], val[:, 1, :], val[:, 0, :], ALU.subtract))
            assert n[0] == VAL_STEP
            dve.wait_ge(counted, 1)
            step(dve.tensor_copy(count[:], t_ps[0:T, 1, 0:BE].rearrange("p (b e) -> p e b", e=E)))
            step(dve.tensor_tensor_scan(upto[:].rearrange("p e b -> p (e b)"), reset[:].rearrange("p e b -> p (e b)"),
                                        count[:].rearrange("p e b -> p (e b)"), 0.0, ALU.mult, ALU.add))
            step(dve.tensor_tensor(upto[:], upto[:], count[:], ALU.subtract))
            step(dve.tensor_tensor(rank[:], t_ps[0:T, 0, 0:BE].rearrange("p (b e) -> p b e", e=E),
                                   upto[:].rearrange("p e b -> p b e"), ALU.add))
            assert n[0] == COUNT_STEP
            for c, pick in enumerate((pick1, pick2)):
                step(dve.tensor_tensor(tmp[:], rank[:], pick[:], ALU.mult))
                step(dve.tensor_reduce(rankc[:, c, :], tmp[:], AX_X, ALU.add))
            step(dve.tensor_scalar(over[:], rankc[:], float(CAP), float(E * CAP), ALU.is_ge, ALU.mult))
            step(dve.tensor_scalar(slot_f[:], where[:], -float(CAP), float(E * CAP), ALU.mult, ALU.add))
            step(dve.tensor_tensor(slot_f[:], slot_f[:], rankc[:], ALU.add))
            step(dve.tensor_tensor(slot_f[:], slot_f[:], over[:], ALU.add))
            step(dve.tensor_copy(slot[:], slot_f[:]))
            step(dve.tensor_copy(target[:, 0, :], token[:]))
            step(dve.tensor_scalar(target[:, 1, :], token[:], float(N), None, ALU.add))
            dve.wait_ge(exp_done, 1)
            step(dve.tensor_scalar(den[:], gate[:, 1, :], 1.0, None, ALU.add))
            step(dve.reciprocal(gate[:, 0, :], den[:]))
            step(dve.tensor_tensor(gate[:, 1, :], gate[:, 1, :], gate[:, 0, :], ALU.mult))
            for c in range(2):
                if c:
                    dve.wait_ge(x_sent[0], 16 * B)
                step(dve.tensor_copy(xres[:, 0:B, C], gate[:, c, :]))
                dve.tensor_copy(xres[:, 0:B, C + 1].bitcast(I32), target[:, c, :]).then_inc(aux_done, 1)

            def expert(p, e, i):
                for t in range(NT):
                    dve.wait_ge(y_done, e * NT + t + 1)
                    if not (isinstance(e, int) and e == 0 and t < 2):
                        dve.wait_ge(y_scaled, e * NT + (t - 1))
                    dve.tensor_tensor(ysum[:, (p * NT + t) % 2, :], y_ps[:, (p * NT + t) % 2, 0:C], b2_of(e), ALU.add).then_inc(y_added, 1)
                    if t == 0:
                        dve.wait_ge(y_sent[p], 16 * NT * i)
                    dve.wait_ge(y_added, e * NT + t + 1)
                    dve.tensor_scalar(yrow[p][:, t, :], ysum[:, (p * NT + t) % 2, :], rows[p][:, t, C:C + 1], None, ALU.mult).then_inc(y_scaled, 1)

            def b2_of(e):
                if isinstance(e, int):
                    return b2_sb[:, e, :]
                return b2_sb[:, bass.ds(e, 1), :].rearrange("p e c -> p (e c)")

            expert(0, 0, 0)
            expert(1, 1, 0)
            with dve.Fori(1, E // 2) as i:
                expert(0, 2 * i, i)
                expert(1, 2 * i + 1, i)
            for g in range(GROUPS):
                pt = part[g % 2]
                xr = xres[:, g * GB:(g + 1) * GB, 0:C]
                dve.wait_ge(part_loaded[g % 2], 32 * (g // 2 + 1))
                dve.tensor_tensor(pt[:, 0], pt[:, 0], pt[:, 1], ALU.add).then_inc(add1_done, 1)
                dve.wait_ge(add1_done, g + 1)
                dve.tensor_tensor(pt[:, 0], pt[:, 0], xr, ALU.add).then_inc(add2_done, 1)
                dve.wait_ge(add2_done, g + 1)
                for b in range(GB):
                    last = dve.bn_stats(stats[:, b, :], pt[:, 0, b, :])
                last.then_inc(stats_done, 1)
                dve.wait_ge(stats_done, g + 1)
                for b in range(GB):
                    last = dve.bn_aggr(mv[:, b, :], stats[:, b, :])
                last.then_inc(mv_done, 1)
                dve.wait_ge(mv_done, g + 1)
                dve.tensor_scalar(veps[:], mv[:, :, 1], LN_EPS, None, ALU.add).then_inc(veps_done, 1)
                dve.wait_ge(rstd_done, g + 1)
                for b in range(GB):
                    last = dve.tensor_scalar(pt[:, 0, b, :], pt[:, 0, b, :], mv[:, b, 0:1], rstd[:, b:b + 1], ALU.subtract, ALU.mult)
                last.then_inc(norm_done, 1)


def clear_phase(nc, fin, xg):
    R = 8
    with nc.sbuf_tensor("blank", [128, R, CX], F32) as blank, nc.semaphore("blank_done") as blank_done, \
            nc.semaphore("cleared") as cleared, nc.Block() as block:
        @block.vector
        def _(dve):
            dve.memset(blank[:], 0.0).then_inc(blank_done, 1)
            dve.wait_ge(blank_done, 1)
            dve.memset(blank[:, :, C + 1:CX].bitcast(I32), NOWHERE).then_inc(blank_done, 1)

        @block.sync
        def _(sp):
            sp.wait_ge(blank_done, 2)
            n = 0
            for i in range(E * CAP // (128 * R)):
                sp.dma_start(xg.rearrange("(i p r) c -> i p r c", p=128, r=R)[i], blank[:]).then_inc(cleared, 16)
                n += 1
            for i in range(2 * N // (128 * R)):
                sp.dma_start(fin.rearrange("(i p r) c -> i p r c", p=128, r=R)[i], blank[:, :, 0:C]).then_inc(cleared, 16)
                n += 1
            sp.wait_ge(cleared, 16 * n)


def kernel(**inputs):
    import ml_dtypes
    import numpy as np
    from concourse import bacc
    from concourse.bass_utils import run_bass_kernel_spmd

    a = {k: np.asarray(v) for k, v in inputs.items()}
    tri = np.triu(np.ones((T, T)), 1)
    pick_rows = np.zeros((128, B, T), ml_dtypes.bfloat16)
    for b in range(B):
        pick_rows[b, b] = 1
    spread = np.zeros((2 * NSTATE, 2 * NSTATE, 128), np.float32)
    for r in range(2 * NSTATE):
        spread[r, r] = 1
    arrays = {
        "x": a["x"],
        "xT": a["x"].reshape(N, C).T,
        "W_inT": a["L0_attn_W_in"].T,
        "Kx": a["L0_attn_Kx"],
        "Kz": a["L0_attn_Kz"],
        "W_xprojT": a["L0_attn_W_xproj"].T,
        "W_dtT": a["L0_attn_W_dt"].T,
        "b_dt": a["L0_attn_b_dt"],
        "A_log": a["L0_attn_A_log"],
        "D": a["L0_attn_D"],
        "W_outT": a["L0_attn_W_out"].T,
        "ctxT": a["ctx_1024"].transpose(0, 2, 1),
        "mask": a["mask_BxS2_bf1"].view(np.uint8),
        "Wq": a["L0_xattn_Wq"],
        "Wk": a["L0_xattn_Wk"],
        "Wv": a["L0_xattn_Wv"],
        "Wo": a["L0_xattn_Wo"],
        "inv_temp": a["L0_xattn_inv_temp"],
        "Wr": a["L0_ffn_Wr"],
        "br": a["L0_ffn_br"],
        "W1": a["L0_ffn_W1"],
        "b1T": a["L0_ffn_b1"].reshape(E, HM, 128).transpose(0, 2, 1),
        "W2": a["L0_ffn_W2"],
        "b2": a["L0_ffn_b2"],
        "ident": np.eye(128, dtype=np.float32),
        "rows_sel": spread,
        "mask_pick": pick_rows,
        "lower": np.stack([tri, np.ones((T, T))], 1).astype(ml_dtypes.bfloat16),
    }
    nc = bacc.Bacc("TRN2", target_bir_lowering=False, num_devices=1)
    feeds, ins = {}, {}
    for name, value in arrays.items():
        value = np.ascontiguousarray(value)
        feeds[f"in_{name}"] = value
        ins[name] = nc.dram_tensor(f"in_{name}", value.shape, mybir.dt.from_np(value.dtype), kind="ExternalInput").ap()
    out = nc.dram_tensor("out_0", (B, T, C), F32, kind="ExternalOutput").ap()
    decoder_kernel(nc, out, ins)
    result = run_bass_kernel_spmd(nc, [feeds], core_ids=[0])
    return result.results[0]["out_0"]
```

```python
from contextlib import ExitStack

import concourse.bass as bass
from concourse import mybir

F32 = mybir.dt.float32
BF16 = mybir.dt.bfloat16
I32 = mybir.dt.int32
U8 = mybir.dt.uint8
ALU = mybir.AluOpType
ACT = mybir.ActivationFunctionType
AX_X = mybir.AxisListType.X

B, T, C = 32, 112, 256
S2 = 375
KC = C // 128
INNER, NSTATE, RANK, TAPS = 128, 8, 16, 3
GB = 4
GROUPS = B // GB
GT = GB * T
DT_AT, BC_AT, BC_ROWS = 32, (0, 64, 96), 112
BLANK_ROWS = 8
H, DH = 16, 64
INNERX = H * DH
PAIRS = H // 2
SC, NSC = 125, 3
TOPK = 32
E = 8
N = B * T
HID = 1024
HM = HID // 128
CAP = N * 2 // E
NT = CAP // 128
HALF = CAP // 2
CX = C + 2
TB = -(-KC * NT // 4)
NOWHERE = 1 << 20
SEL_STEP, VAL_STEP, COUNT_STEP = 14, 15, 19
GONE = -3e38
LN_EPS = 1e-5
CLIP_LO, CLIP_HI = 1e-4, 1.0
SOFTPLUS_CAP = 10.0



def wait_apart(eng, met, *waits):
    waits = [(sem, value if isinstance(value, int) else eng.to_reg(value)) for sem, value in waits]
    eng.wait_ge(met, 1)
    for sem, value in waits:
        eng.wait_ge(sem, value)


def decoder_kernel(nc, out, ins):
    ctx = ExitStack()
    with ctx:
        def sb(name, shape, dt=F32):
            return ctx.enter_context(nc.sbuf_tensor(name, shape, dt))

        xres = sb("xres", [T, B + 1, CX])
        ident_sb = sb("ident_sb", [128, 128])
        logits = sb("logits", [T, B, E])
        fin = nc.dram_tensor("fin", [2 * N, C], F32).ap()
        xg = nc.dram_tensor("xg", [E * CAP, CX], F32).ap()
        state_space_phase(nc, xres, ident_sb, ins["xT"], ins["x"], ins["W_inT"], ins["Kx"], ins["Kz"], ins["W_xprojT"],
                          ins["W_dtT"], ins["b_dt"], ins["A_log"], ins["D"], ins["W_outT"], ins["rows_sel"], ins["ident"], fin, xg)
        attention_phase(nc, xres, logits, ident_sb, ins["ctxT"], ins["mask"], ins["mask_pick"], ins["Wq"], ins["Wk"], ins["Wv"],
                        ins["Wo"], ins["inv_temp"], ins["Wr"], ins["br"])
        expert_phase(nc, xres, logits, ident_sb, ins["lower"], ins["W1"], ins["b1T"], ins["W2"], ins["b2"], fin, xg, out)


def state_space_phase(nc, xres, ident_sb, xT, x, W_inT, Kx, Kz, W_xprojT, W_dtT, b_dt, A_log, D, W_outT, rows_sel, ident, fin, xg):
    ctx = ExitStack()
    with ctx:
        def sb(name, shape, dt=F32):
            return ctx.enter_context(nc.sbuf_tensor("m_" + name, shape, dt))

        def ps(name, shape, dt=F32):
            return ctx.enter_context(nc.psum_tensor("m_" + name, shape, dt))

        def sem(name):
            return ctx.enter_context(nc.semaphore("m_" + name))

        w_in = sb("w_in", [128, KC, 2 * INNER])
        w_xp = sb("w_xp", [INNER, RANK + 2 * NSTATE])
        w_rep = sb("w_rep", [INNER, BC_ROWS])
        w_dt = sb("w_dt", [DT_AT + RANK, INNER])
        w_out = sb("w_out", [INNER, 2, C])
        taps = sb("taps", [INNER, 2, TAPS])
        bdt = sb("bdt", [INNER, 1])
        skip = sb("skip", [INNER, 1])
        dskip = sb("dskip", [INNER, INNER])
        alog = sb("alog", [INNER, NSTATE])
        aneg = sb("aneg", [INNER, NSTATE])
        atmp = sb("atmp", [INNER, 2, NSTATE])
        sel = sb("sel", [BC_ROWS, 2 * NSTATE, 128], BF16)
        bc_sign = sb("bc_sign", [BC_ROWS, 1])
        blank = sb("blank", [128, BLANK_ROWS, CX])
        xt = [sb(f"xt{i}", [128, KC, GT]) for i in range(2)]
        pad = sb("pad", [INNER, 2, GB, T + 2])
        conv = sb("conv", [INNER, 2, GT])
        xz = [sb(f"xz{i}", [INNER, 2, GT]) for i in range(2)]
        dt_sb = sb("dt_sb", [DT_AT + RANK, GT])
        bc = sb("bc", [BC_ROWS, GT])
        bc_rest = sb("bc_rest", [BC_ROWS, GT])
        bc_parts = [sb(f"bc_parts{i}", [BC_ROWS, GT], BF16) for i in range(2)]
        dl = sb("dl", [INNER, 4, GT])
        decay = [sb(f"decay{i}", [INNER, NSTATE, GT]) for i in range(2)]
        drive = sb("drive", [INNER, NSTATE, GT])
        y = sb("y", [INNER, GT])
        stats = sb("stats", [T, GB, 6])
        summed = sb("summed", [T, GB, C])
        mv = sb("mv", [T, GB, 2])
        veps = sb("veps", [T, GB])
        rstd = sb("rstd", [T, GB])
        neghalf = sb("neghalf", [T, GB])

        h_ps = ps("h_ps", [128, 2, 512])
        p_ps = ps("p_ps", [128, 512])
        row_ps = ps("row_ps", [128, 2, 512])
        y_ps = ps("y_ps", [128, 512])
        o_ps = ps("o_ps", [T, 2, 512])

        loaded = sem("weights_loaded")
        x_loaded = [sem(f"x_loaded{i}") for i in range(2)]
        ready, a_step, half_done, set_done = sem("setup_ready"), sem("a_step"), sem("half_done"), sem("set_done")
        blank_done, cleared = sem("blank_done"), sem("cleared")
        h_done, pad_done, taps_done, conv_done = sem("h_done"), sem("pad_done"), sem("taps_done"), sem("conv_done")
        xz_done, proj_done, bc_done, dt_done = sem("xz_done"), sem("proj_done"), sem("bc_done"), sem("dt_done")
        part_done, rest_done, split_done = sem("part_done"), sem("rest_done"), sem("split_done")
        draw_done, dcap_done, exp_done, log_done = sem("draw_done"), sem("dcap_done"), sem("exp_done"), sem("log_done")
        um_done, dfix_done, dsum_done, delta_done = sem("um_done"), sem("dfix_done"), sem("dsum_done"), sem("delta_done")
        decay_done, row_done, row_used = sem("decay_done"), sem("row_done"), sem("row_used")
        clip_done, drive_done, starts_done, scan_done = sem("clip_done"), sem("drive_done"), sem("starts_done"), sem("scan_done")
        ysum_done, y_done, out_done, res_done = sem("ysum_done"), sem("y_done"), sem("out_done"), sem("res_done")
        stats_done, mv_done, veps_done = sem("stats_done"), sem("mv_done"), sem("veps_done")
        rstd_done, norm_done = sem("rstd_done"), sem("norm_done")

        LOADS = 16 * 11
        NR = 2 * NSTATE

        def run(eng, project, step, finish):
            project((0, 0, 0))
            step((0, 0, 0), (1, 0, 1))
            with eng.Fori(0, GROUPS // 2 - 1) as i:
                step((2 * i + 1, i, 1), (2 * i + 2, i + 1, 0))
                step((2 * i + 2, i + 1, 0), (2 * i + 3, i + 1, 1))
            step((GROUPS - 1, GROUPS // 2 - 1, 1), None)
            finish((GROUPS - 1, GROUPS // 2 - 1, 1))

        def is_first(k, below=1):
            return isinstance(k, int) and k < below

        block = ctx.enter_context(nc.Block())

        @block.sync
        def _(sp):
            def load(k, q):
                xt_src = xT.rearrange("(k p) n -> p k n", p=128)
                x_src = x.rearrange("b t c -> t b c")
                if isinstance(k, int):
                    sp.dma_start(xt[q][:], xt_src[:, :, k * GT:(k + 1) * GT]).then_inc(x_loaded[q], 16)
                    sp.dma_start(xres[:, k * GB:(k + 1) * GB, 0:C], x_src[:, k * GB:(k + 1) * GB, :]).then_inc(x_loaded[q], 16)
                else:
                    sp.dma_start(xt[q][:], xt_src[:, :, bass.ds(k * GT, GT)]).then_inc(x_loaded[q], 16)
                    sp.dma_start(xres[:, bass.ds(k * GB, GB), 0:C], x_src[:, bass.ds(k * GB, GB), :]).then_inc(x_loaded[q], 16)

            sp.dma_start(w_in[:], W_inT.rearrange("(k p) e -> p k e", p=128)).then_inc(loaded, 16)
            load(0, 0)
            sp.dma_start(taps[:, 0, :], Kx.rearrange("c a k -> c (a k)")).then_inc(loaded, 16)
            sp.dma_start(taps[:, 1, :], Kz.rearrange("c a k -> c (a k)")).then_inc(loaded, 16)
            sp.dma_start(w_xp[:], W_xprojT).then_inc(loaded, 16)
            sp.dma_start(w_dt[DT_AT:DT_AT + RANK, :], W_dtT).then_inc(loaded, 16)
            sp.dma_start(bdt[:], b_dt.rearrange("(c a) -> c a", a=1)).then_inc(loaded, 16)
            sp.dma_start(skip[:], D.rearrange("(c a) -> c a", a=1)).then_inc(loaded, 16)
            sp.dma_start(alog[:], A_log).then_inc(loaded, 16)
            sp.dma_start(ident_sb[:], ident).then_inc(loaded, 16)
            sp.dma_start(sel[:], rows_sel).then_inc(loaded, 16)
            sp.dma_start(w_out[:], W_outT.rearrange("(k p) e -> p k e", p=128)).then_inc(loaded, 16)
            load(1, 1)
            sp.wait_ge(blank_done, 2)
            n = 0
            for i in range(E * CAP // (128 * BLANK_ROWS)):
                sp.dma_start(xg.rearrange("(i p r) c -> i p r c", p=128, r=BLANK_ROWS)[i], blank[:]).then_inc(cleared, 16)
                n += 1
            for i in range(2 * N // (128 * BLANK_ROWS)):
                sp.dma_start(fin.rearrange("(i p r) c -> i p r c", p=128, r=BLANK_ROWS)[i], blank[:, :, 0:C]).then_inc(cleared, 16)
                n += 1
            with sp.Fori(0, GROUPS // 2 - 1) as i:
                for q in range(2):
                    sp.wait_ge(loaded, LOADS)
                    sp.wait_ge(h_done, 2 * i + q + 1)
                    load(2 * i + q + 2, q)
            sp.wait_ge(cleared, 16 * n)

        @block.tensor
        def _(pe):
            def h_product(k, half_k, q):
                pe.wait_ge(x_loaded[q], 32 * (half_k + 1))
                if not is_first(k):
                    pe.wait_ge(pad_done, 2 * k)
                    pe.wait_ge(dcap_done, k)
                for half in range(2):
                    for c in range(KC):
                        mm = pe.matmul(h_ps[:, half, 0:GT], w_in[:, c, half * INNER:(half + 1) * INNER], xt[q][:, c, :],
                                       start=(c == 0), stop=(c == KC - 1))
                mm.then_inc(h_done, 1)

            def low_rank(k, q):
                pe.wait_ge(xz_done, 2 * k + 1)
                if not is_first(k):
                    pe.wait_ge(dt_done, k)
                pe.matmul(p_ps[0:BC_ROWS, 0:GT], w_rep[:], xz[q][:, 0, :], start=True, stop=True).then_inc(proj_done, 1)

            def raw_delta(k):
                pe.wait_ge(dt_done, k + 1)
                pe.matmul(h_ps[:, 0, 0:GT], w_dt[DT_AT:DT_AT + RANK, :], dt_sb[DT_AT:DT_AT + RANK, :],
                          start=True, stop=True).then_inc(draw_done, 1)

            def row(k, q, r):
                if not (is_first(k) and r < 2):
                    pe.wait_ge(row_used, k * NR + (r - 1))
                pe.matmul(row_ps[:, r % 2, 0:GT], sel[:, r, :], bc_parts[q][:], start=True, stop=True).then_inc(row_done, 1)

            def out_product(k, q):
                pe.wait_ge(y_done, k + 1)
                if not is_first(k):
                    pe.wait_ge(res_done, k)
                for b in range(GB):
                    at = slice((b % 2) * C, (b % 2 + 1) * C)
                    pe.matmul(o_ps[:, b // 2, at], y[:, b * T:(b + 1) * T], w_out[:, 0, :], start=True, stop=False)
                    mm = pe.matmul(o_ps[:, b // 2, at], xz[q][:, 1, b * T:(b + 1) * T], w_out[:, 1, :], start=False, stop=True)
                mm.then_inc(out_done, 1)

            def project(a):
                k, half_k, q = a
                pe.wait_ge(loaded, LOADS)
                h_product(k, half_k, q)
                pe.wait_ge(ready, 1)
                low_rank(k, q)
                raw_delta(k)

            def step(a, nx):
                k, _, q = a
                pe.wait_ge(split_done, k + 1)
                row(k, q, 0)
                row(k, q, 1)
                if nx:
                    h_product(*nx)
                for r in range(2, NSTATE):
                    row(k, q, r)
                if not is_first(k):
                    out_product(k - 1, 1 - q)
                row(k, q, NSTATE)
                row(k, q, NSTATE + 1)
                if nx:
                    low_rank(nx[0], nx[2])
                    raw_delta(nx[0])
                if not is_first(k):
                    pe.wait_ge(y_done, k)
                pe.matmul(y_ps[:, 0:GT], dskip[:], xz[q][:, 0, :], start=True, stop=False)
                for s in range(NSTATE):
                    pe.wait_ge(row_used, k * NR + NSTATE + s + 1)
                    mm = pe.matmul(y_ps[:, 0:GT], ident_sb[:], drive[:, s, :], start=False, stop=(s == NSTATE - 1))
                    if s + 2 < NSTATE:
                        row(k, q, NSTATE + s + 2)
                mm.then_inc(ysum_done, 1)

            def finish(a):
                out_product(a[0], a[2])

            run(pe, project, step, finish)

        @block.scalar
        def _(act):
            def pad_copy(k):
                act.wait_ge(h_done, k + 1)
                if not is_first(k):
                    act.wait_ge(conv_done, 2 * k)
                for half in range(2):
                    act.activation(pad[:, half, :, 1:T + 1], h_ps[:, half, 0:GT].rearrange("p (b t) -> p b t", b=GB),
                                   ACT.Copy).then_inc(pad_done, 1)

            def silu(k, q):
                if not is_first(k, 2):
                    act.wait_ge(out_done, k - 1)
                for half in range(2):
                    act.wait_ge(conv_done, 2 * k + half + 1)
                    act.activation(xz[q][:, half, :], conv[:, half, :], ACT.Silu).then_inc(xz_done, 1)

            def low_rank(k):
                act.wait_ge(proj_done, k + 1)
                if not is_first(k):
                    act.wait_ge(split_done, k)
                act.activation(bc[:], p_ps[0:BC_ROWS, 0:GT], ACT.Tanh, scale=bc_sign[:, 0:1]).then_inc(bc_done, 1)
                act.activation(dt_sb[DT_AT:DT_AT + RANK, :], p_ps[DT_AT:DT_AT + RANK, 0:GT], ACT.Copy).then_inc(dt_done, 1)

            def soft(k):
                act.wait_ge(dcap_done, k + 1)
                act.activation(dl[:, 1, :], dl[:, 0, :], ACT.Exp).then_inc(exp_done, 1)
                act.wait_ge(exp_done, k + 1)
                act.activation(dl[:, 2, :], dl[:, 1, :], ACT.Ln, bias=1.0).then_inc(log_done, 1)

            def decays(k, q):
                act.wait_ge(delta_done, k + 1)
                if not is_first(k, 2):
                    act.wait_ge(scan_done, k - 1)
                for s in range(NSTATE):
                    last = act.activation(decay[q][:, s, :], dl[:, 0, :], ACT.Exp, scale=aneg[:, s:s + 1])
                last.then_inc(decay_done, 1)

            def y_copy(k):
                act.wait_ge(ysum_done, k + 1)
                if not is_first(k):
                    act.wait_ge(out_done, k)
                act.activation(y[:], y_ps[:, 0:GT], ACT.Copy).then_inc(y_done, 1)

            def project(a):
                k, _, q = a
                act.wait_ge(loaded, LOADS)
                act.activation(atmp[:, 0, :], alog[:], ACT.Abs).then_inc(a_step, 1)
                act.wait_ge(a_step, 1)
                act.activation(atmp[:, 0, :], atmp[:, 0, :], ACT.Exp, scale=-1.0).then_inc(a_step, 1)
                act.wait_ge(a_step, 2)
                act.activation(atmp[:, 0, :], atmp[:, 0, :], ACT.Ln, bias=1.0).then_inc(a_step, 1)
                act.wait_ge(set_done, 1)
                pad_copy(k)
                silu(k, q)
                act.wait_ge(ready, 1)
                low_rank(k)
                soft(k)
                decays(k, q)

            def step(a, nx):
                k, _, q = a
                if not is_first(k):
                    y_copy(k - 1)
                if nx:
                    pad_copy(nx[0])
                    silu(nx[0], nx[2])
                    low_rank(nx[0])
                    soft(nx[0])
                    decays(nx[0], nx[2])

            def finish(a):
                y_copy(a[0])

            run(act, project, step, finish)

        @block.gpsimd
        def _(pool):
            pool.memset(neghalf[:], -0.5).then_inc(half_done, 1)
            pool.wait_ge(half_done, 1)

            def split(k, q):
                mid, low = BC_AT[1], BC_AT[2]
                waits = [(bc_done, k + 1)]
                if not is_first(k, 2):
                    waits.append((row_done, (k - 1) * NR))
                wait_apart(pool, half_done, *waits)
                pool.tensor_copy(bc_parts[q][:], bc[:]).then_inc(part_done, 1)
                pool.wait_ge(part_done, 2 * k + 1)
                pool.tensor_tensor(bc_rest[mid:, :], bc[mid:, :], bc_parts[q][mid:, :], ALU.subtract).then_inc(rest_done, 1)
                wait_apart(pool, half_done, (rest_done, 2 * k + 1))
                pool.tensor_copy(bc_parts[q][mid:, :], bc_rest[mid:, :]).then_inc(part_done, 1)
                pool.wait_ge(part_done, 2 * k + 2)
                pool.tensor_tensor(bc_rest[low:, :], bc_rest[low:, :], bc_parts[q][low:, :], ALU.subtract).then_inc(rest_done, 1)
                wait_apart(pool, half_done, (rest_done, 2 * k + 2))
                pool.tensor_copy(bc_parts[q][low:, :], bc_rest[low:, :]).then_inc(split_done, 1)

            def power(k):
                pool.wait_ge(veps_done, k + 1)
                pool.tensor_tensor(rstd[:], veps[:], neghalf[:], ALU.pow).then_inc(rstd_done, 1)

            def project(a):
                split(a[0], a[2])

            def step(a, nx):
                if not is_first(a[0]):
                    power(a[0] - 1)
                if nx:
                    split(nx[0], nx[2])

            def finish(a):
                power(a[0])

            run(pool, project, step, finish)

        @block.vector
        def _(dve):
            def convolve(k):
                for tap in range(TAPS):
                    for half in range(2):
                        src = pad[:, half, :, tap:tap + T]
                        dst = conv[:, half, :].rearrange("p (b t) -> p b t", b=GB)
                        w = taps[:, half, tap:tap + 1]
                        if tap == 0:
                            dve.wait_ge(pad_done, 2 * k + half + 1)
                            if not is_first(k):
                                dve.wait_ge(xz_done, 2 * k + (half - 1))
                            dve.tensor_scalar(dst, src, w, None, ALU.mult).then_inc(taps_done, 1)
                        else:
                            dve.wait_ge(taps_done, k * 4 + (tap - 1) * 2 + half + 1)
                            dve.scalar_tensor_tensor(dst, src, w, dst, ALU.mult, ALU.add).then_inc(
                                taps_done if tap == 1 else conv_done, 1)

            def delta(k, part):
                if part == 0:
                    dve.wait_ge(draw_done, k + 1)
                    if not is_first(k):
                        dve.wait_ge(decay_done, k)
                    dve.tensor_scalar(dl[:, 0, :], h_ps[:, 0, 0:GT], bdt[:, 0:1], SOFTPLUS_CAP, ALU.add, ALU.min).then_inc(dcap_done, 1)
                if part == 1:
                    dve.wait_ge(exp_done, k + 1)
                    dve.tensor_scalar(dl[:, 3, :], dl[:, 1, :], 1.0, -1.0, ALU.add, ALU.add).then_inc(um_done, 1)
                if part == 2:
                    dve.wait_ge(um_done, k + 1)
                    dve.tensor_tensor(dl[:, 3, :], dl[:, 1, :], dl[:, 3, :], ALU.subtract).then_inc(dfix_done, 1)
                if part == 3:
                    dve.wait_ge(dfix_done, k + 1)
                    dve.wait_ge(log_done, k + 1)
                    dve.tensor_tensor(dl[:, 3, :], dl[:, 2, :], dl[:, 3, :], ALU.add).then_inc(dsum_done, 1)
                if part == 4:
                    dve.wait_ge(dsum_done, k + 1)
                    dve.tensor_scalar(dl[:, 0, :], dl[:, 3, :], CLIP_LO, CLIP_HI, ALU.max, ALU.min).then_inc(delta_done, 1)

            def norm(k, part):
                if part == 0:
                    dve.wait_ge(out_done, k + 1)
                    if not is_first(k):
                        dve.wait_ge(norm_done, k)
                    for h in range(2):
                        if isinstance(k, int):
                            xr = xres[:, k * GB + 2 * h:k * GB + 2 * h + 2, 0:C]
                        else:
                            xr = xres[:, bass.ds(k * GB + 2 * h, 2), 0:C]
                        last = dve.tensor_tensor(summed[:, 2 * h:2 * h + 2, :], o_ps[:, h, :].rearrange("p (b c) -> p b c", b=2),
                                                 xr, ALU.add)
                    last.then_inc(res_done, 1)
                if part == 1:
                    dve.wait_ge(res_done, k + 1)
                    for b in range(GB):
                        last = dve.bn_stats(stats[:, b, :], summed[:, b, :])
                    last.then_inc(stats_done, 1)
                if part == 2:
                    wait_apart(dve, ready, (stats_done, k + 1))
                    for b in range(GB):
                        last = dve.bn_aggr(mv[:, b, :], stats[:, b, :])
                    last.then_inc(mv_done, 1)
                if part == 3:
                    dve.wait_ge(mv_done, k + 1)
                    dve.tensor_scalar(veps[:], mv[:, :, 1], LN_EPS, None, ALU.add).then_inc(veps_done, 1)
                if part == 4:
                    dve.wait_ge(rstd_done, k + 1)
                    for b in range(GB):
                        if isinstance(k, int):
                            xr = xres[:, k * GB + b, 0:C]
                        else:
                            xr = xres[:, bass.ds(k * GB + b, 1), 0:C].rearrange("p b c -> p (b c)")
                        last = dve.tensor_scalar(xr, summed[:, b, :], mv[:, b, 0:1], rstd[:, b:b + 1], ALU.subtract, ALU.mult)
                    last.then_inc(norm_done, 1)

            def project(a):
                k, _, q = a
                dve.memset(pad[:], 0.0).then_inc(set_done, 1)
                dve.memset(blank[:], 0.0).then_inc(blank_done, 1)
                dve.memset(xres[:, B, :], 0.0)
                dve.memset(w_rep[:], 0.0)
                dve.memset(bc_sign[:], 1.0).then_inc(set_done, 1)
                dve.wait_ge(blank_done, 1)
                dve.memset(blank[:, :, C + 1:CX].bitcast(I32), NOWHERE).then_inc(blank_done, 1)
                dve.wait_ge(set_done, 2)
                dve.wait_ge(loaded, LOADS)
                for at in BC_AT:
                    dve.memset(bc_sign[at:at + NSTATE, :], -1.0)
                    dve.tensor_copy(w_rep[:, at:at + NR], w_xp[:, RANK:])
                dve.tensor_copy(w_rep[:, DT_AT:DT_AT + RANK], w_xp[:, 0:RANK])
                dve.tensor_scalar(dskip[:], ident_sb[:], skip[:, 0:1], None, ALU.mult)
                dve.wait_ge(a_step, 3)
                dve.scalar_tensor_tensor(atmp[:, 1, :], alog[:], 0.0, atmp[:, 0, :], ALU.max, ALU.add).then_inc(set_done, 1)
                dve.wait_ge(set_done, 3)
                dve.tensor_scalar(aneg[:], atmp[:, 1, :], 1e-4, -1.0, ALU.add, ALU.mult).then_inc(ready, 1)
                convolve(k)
                for part in range(5):
                    delta(k, part)

            def step(a, nx):
                k, _, q = a
                dve.wait_ge(decay_done, k + 1)
                dve.tensor_scalar(decay[q][:], decay[q][:], CLIP_LO, CLIP_HI, ALU.max, ALU.min).then_inc(clip_done, 1)
                for s in range(NSTATE):
                    dve.wait_ge(row_done, k * NR + s + 1)
                    if s == 0 and not is_first(k):
                        dve.wait_ge(ysum_done, k)
                    dve.tensor_tensor(drive[:, s, :], row_ps[:, s % 2, 0:GT], xz[q][:, 0, :], ALU.mult).then_inc(row_used, 1)
                if nx:
                    convolve(nx[0])
                if not is_first(k):
                    norm(k - 1, 0)
                dve.wait_ge(clip_done, k + 1)
                dve.wait_ge(row_used, k * NR + NSTATE)
                dve.scalar_tensor_tensor(drive[:], decay[q][:], 1.0, drive[:], ALU.subtract, ALU.mult).then_inc(drive_done, 1)
                if not is_first(k):
                    norm(k - 1, 1)
                dve.wait_ge(drive_done, k + 1)
                dve.memset(decay[q][:].rearrange("p s (b t) -> p s b t", b=GB)[:, :, :, 0:1], 0.0).then_inc(starts_done, 1)
                if not is_first(k):
                    norm(k - 1, 2)
                if nx:
                    delta(nx[0], 0)
                dve.wait_ge(starts_done, k + 1)
                dve.tensor_tensor_scan(drive[:].rearrange("p s t -> p (s t)"), decay[q][:].rearrange("p s t -> p (s t)"),
                                       drive[:].rearrange("p s t -> p (s t)"), 0.0, ALU.mult, ALU.add).then_inc(scan_done, 1)
                if not is_first(k):
                    norm(k - 1, 3)
                if nx:
                    delta(nx[0], 1)
                    delta(nx[0], 2)
                for s in range(NSTATE):
                    dve.wait_ge(row_done, k * NR + NSTATE + s + 1)
                    if s == 0:
                        dve.wait_ge(scan_done, k + 1)
                    dve.tensor_tensor(drive[:, s, :], row_ps[:, s % 2, 0:GT], drive[:, s, :], ALU.mult).then_inc(row_used, 1)
                    if s == 2 and nx:
                        delta(nx[0], 3)
                    if s == 3 and nx:
                        delta(nx[0], 4)
                if not is_first(k):
                    norm(k - 1, 4)

            def finish(a):
                for part in range(5):
                    norm(a[0], part)
                dve.wait_ge(norm_done, GROUPS)

            run(dve, project, step, finish)


def attention_phase(nc, xres, logits, ident_sb, ctxT, mask, mask_pick, Wq, Wk, Wv, Wo, inv_temp, Wr, br):
    ctx = ExitStack()
    with ctx:
        def sb(name, shape, dt=F32):
            return ctx.enter_context(nc.sbuf_tensor("x_" + name, shape, dt))

        def ps(name, shape, dt=F32):
            return ctx.enter_context(nc.psum_tensor("x_" + name, shape, dt))

        def sem(name):
            return ctx.enter_context(nc.semaphore("x_" + name))

        wq = sb("wq", [128, KC, INNERX])
        wk = sb("wk", [128, KC, INNERX])
        wv = sb("wv", [128, KC, INNERX])
        wo = sb("wo", [128, PAIRS, C])
        wr = sb("wr", [128, KC, E])
        br_sb = sb("br_sb", [T, E])
        temp = sb("temp", [128, H])
        mask_u8 = sb("mask_u8", [B, S2], U8)
        mask_bias = sb("mask_bias", [128, S2], BF16)
        pick = sb("pick", [128, B, T], BF16)
        ctx_sb = [sb(f"ctx_sb{i}", [128, KC, S2]) for i in range(2)]
        xT = sb("xT_att", [128, KC, T])
        qT = sb("qT", [128, PAIRS, T])
        kT = sb("kT", [128, PAIRS, S2])
        v = sb("v", [SC, NSC, H, DH + 1])
        work = sb("work", [T, 2, S2])
        top = sb("top", [T, 2, 2, TOPK])
        s_sb = sb("s_sb", [T, 4, S2])
        prob = sb("prob", [T, 4, S2])
        nmax = sb("nmax", [T, 4])
        full_sum = sb("full_sum", [T, H])
        kept = sb("kept", [T, 2, S2])
        total = sb("total", [T, H])
        rtotal = sb("rtotal", [T, H])
        pT = sb("pT", [SC, 2, NSC, T])
        o = sb("o", [T, 8, DH])
        oT = sb("oT", [128, PAIRS, T])
        summed = sb("summed_att", [T, C])
        stats = sb("stats_att", [T, 6])
        mv = sb("mv_att", [T, 2])
        veps = sb("veps_att", [T, 1])
        rstd = sb("rstd_att", [T, 1])
        neghalf = sb("neghalf_att", [T, 1])
        x_stage = sb("x_stage", [T, C])
        x2 = sb("x2", [T, C])
        x2T = sb("x2T", [128, KC, T])

        s_ps = ps("s_ps", [T, 2, 512])
        pT_ps = ps("pT_ps", [SC, 2, 512])
        o_ps = ps("o_ps", [T, 2, 512])
        w_ps = ps("w_ps", [128, 2, 512])

        loaded = sem("att_loaded")
        ctx_loaded = [sem(f"ctx_loaded{i}") for i in range(2)]
        masked = sem("masked")
        wq_done = sem("wq_done")
        half_done = sem("att_half_done")
        xT_done, xT_copied = sem("xT_done"), sem("xT_copied")
        kq_done, kq_copied = sem("kq_done"), sem("kq_copied")
        v_done, v_copied = sem("v_done"), sem("v_copied")
        s_done, s_copied, max_done, rep_done = sem("s_done"), sem("s_copied"), sem("max_done"), sem("rep_done")
        nmax_done, exp_done, kept_done, p_done = sem("nmax_done"), sem("exp_done"), sem("kept_done"), sem("p_done")
        pT_done, pT_copied, pv_done = sem("pT_done"), sem("pT_copied"), sem("pv_done")
        total_done, rtotal_done, o_done = sem("total_done"), sem("rtotal_done"), sem("o_done")
        oT_done, oT_copied, wo_done = sem("oT_done"), sem("oT_copied"), sem("wo_done")
        sum_done, stats_done, mv_done = sem("sum_done"), sem("stats_done_att"), sem("mv_done_att")
        veps_done, rstd_done, x2_done = sem("veps_done_att"), sem("rstd_done_att"), sem("x2_done")
        x2T_done, x2T_copied = sem("x2T_done"), sem("x2T_copied")
        stage_done, x2_kept = sem("stage_done"), sem("x2_kept")
        lg_done, lg_copied = sem("lg_done"), sem("lg_copied")

        LOADS = 16 * 9
        scale = float(DH) ** -0.5

        def run(eng, batch, lead_in, lead_out):
            lead_in((0, 0, 0))
            batch((0, 0, 0), (1, 0, 1), False, True)
            with eng.Fori(0, B // 2 - 1) as i:
                batch((2 * i + 1, i, 1), (2 * i + 2, i + 1, 0), True, True)
                batch((2 * i + 2, i + 1, 0), (2 * i + 3, i + 1, 1), True, True)
            batch((B - 1, B // 2 - 1, 1), (B, B // 2, 0), True, False)
            lead_out((B - 1, B // 2 - 1, 1))

        block = ctx.enter_context(nc.Block())

        @block.sync
        def _(sp):
            sp.dma_start(mask_u8[:], mask).then_inc(loaded, 16)
            sp.dma_start(wq[:], Wq.rearrange("(k p) e -> p k e", p=128)).then_inc(loaded, 16)
            sp.dma_start(temp[:], inv_temp.rearrange("(a h) -> a h", a=1).to_broadcast([128, H])).then_inc(loaded, 16)
            sp.dma_start(wk[:], Wk.rearrange("(k p) e -> p k e", p=128)).then_inc(loaded, 16)
            sp.dma_start(pick[:], mask_pick).then_inc(loaded, 16)
            sp.dma_start(wv[:], Wv.rearrange("(k p) e -> p k e", p=128)).then_inc(loaded, 16)
            sp.dma_start(wo[:], Wo.rearrange("(k p) e -> p k e", p=128)).then_inc(loaded, 16)
            sp.dma_start(wr[:], Wr.rearrange("(k p) e -> p k e", p=128)).then_inc(loaded, 16)
            sp.dma_start(br_sb[:], br.rearrange("(a h) -> a h", a=1).to_broadcast([T, E])).then_inc(loaded, 16)
            src = ctxT.rearrange("b (k p) s -> b p k s", p=128)
            for b in range(2):
                sp.dma_start(ctx_sb[b][:], src[b]).then_inc(ctx_loaded[b], 16)
            with sp.Fori(0, B // 2 - 1) as i:
                for p in range(2):
                    sp.wait_ge(loaded, LOADS)
                    sp.wait_ge(v_done, (2 * i + p) * PAIRS + PAIRS)
                    sp.dma_start(ctx_sb[p][:], src[bass.ds(2 * i + p + 2, 1)].rearrange("b p k s -> p (b k) s")).then_inc(
                        ctx_loaded[p], 16)

        @block.tensor
        def _(pe):
            def x_transpose(b):
                n, _, _ = b
                pe.wait_ge(stage_done, n + 1)
                for k in range(KC):
                    mm = pe.transpose(w_ps[:, 1, k * T:(k + 1) * T], x_stage[:, k * 128:(k + 1) * 128], ident_sb[0:T, 0:T])
                mm.then_inc(xT_done, 1)

            def keys_queries(b, p):
                n, half, par = b
                if p == 0:
                    pe.wait_ge(ctx_loaded[par], 16 * (half + 1))
                    pe.wait_ge(xT_copied, n + 1)
                pe.wait_ge(kq_copied, n * PAIRS + p)
                for k in range(KC):
                    pe.matmul(w_ps[:, 0, 0:S2], wk[:, k, p * 128:(p + 1) * 128], ctx_sb[par][:, k, :],
                              start=(k == 0), stop=(k == KC - 1))
                for k in range(KC):
                    mm = pe.matmul(w_ps[:, 0, 384:384 + T], wq[:, k, p * 128:(p + 1) * 128], xT[:, k, :],
                                   start=(k == 0), stop=(k == KC - 1))
                mm.then_inc(kq_done, 1)

            def values(b, p):
                n, half, par = b
                pe.wait_ge(v_copied, n * PAIRS + p)
                for c in range(NSC):
                    for k in range(KC):
                        mm = pe.matmul(w_ps[0:SC, 1, c * 128:(c + 1) * 128], ctx_sb[par][:, k, c * SC:(c + 1) * SC],
                                       wv[:, k, p * 128:(p + 1) * 128], start=(k == 0), stop=(k == KC - 1))
                mm.then_inc(v_done, 1)

            def scores(b, p):
                n, _, _ = b
                for hh in range(2):
                    h = 2 * p + hh
                    at = slice(64 * hh, 64 * hh + 64)
                    pe.wait_ge(loaded, LOADS)
                    if not (isinstance(n, int) and n == 0 and h < 2):
                        pe.wait_ge(s_copied, n * H + (h - 1))
                    pe.matmul(s_ps[:, hh, 0:S2], pick[:, bass.ds(n, 1), :].rearrange("p b t -> p (b t)"), mask_bias[:],
                              start=True, stop=False)
                    if hh == 0:
                        pe.wait_ge(kq_copied, n * PAIRS + p + 1)
                    pe.matmul(s_ps[:, hh, 0:S2], qT[at, p, :], kT[at, p, :], start=False, stop=True).then_inc(s_done, 1)

            def prob_transpose(b, p, hh):
                n, _, _ = b
                h = 2 * p + hh
                pe.wait_ge(p_done, n * H + h + 1)
                if not (isinstance(n, int) and n == 0 and h < 2):
                    pe.wait_ge(pT_copied, n * H + (h - 1))
                for c in range(NSC):
                    mm = pe.transpose(pT_ps[:, hh, c * T:(c + 1) * T], prob[:, h % 4, c * SC:(c + 1) * SC], ident_sb[0:T, 0:T])
                mm.then_inc(pT_done, 1)

            def prob_values(b, p, hh):
                n, _, _ = b
                h = 2 * p + hh
                pe.wait_ge(pT_copied, n * H + h + 1)
                if hh == 0:
                    pe.wait_ge(v_copied, n * PAIRS + p + 1)
                if h % 8 == 0:
                    pe.wait_ge(o_done, n * 2 + h // 8)
                for c in range(NSC):
                    at = slice(h % 4 * (DH + 1), (h % 4 + 1) * (DH + 1))
                    mm = pe.matmul(o_ps[:, h % 8 // 4, at], pT[:, hh, c, :], v[:, c, h, :],
                                   start=(c == 0), stop=(c == NSC - 1))
                if hh == 1:
                    mm.then_inc(pv_done, 1)

            def out_transpose(b, half):
                n, _, _ = b
                pe.wait_ge(o_done, n * 2 + half + 1)
                for q in range(4):
                    mm = pe.transpose(w_ps[:, 1, q * T:(q + 1) * T], o[:, 2 * q:2 * q + 2, :].rearrange("p h d -> p (h d)"),
                                      ident_sb[0:T, 0:T])
                mm.then_inc(oT_done, 1)

            def out_project(b):
                n, _, _ = b
                pe.wait_ge(oT_copied, n * 2 + 2)
                for p in range(PAIRS):
                    mm = pe.matmul(w_ps[0:T, 1, 0:C], oT[:, p, :], wo[:, p, :], start=(p == 0), stop=(p == PAIRS - 1))
                mm.then_inc(wo_done, 1)

            def x2_transpose(b):
                n, _, _ = b
                pe.wait_ge(x2_done, n + 1)
                for k in range(KC):
                    mm = pe.transpose(w_ps[:, 1, k * T:(k + 1) * T], x2[:, k * 128:(k + 1) * 128], ident_sb[0:T, 0:T])
                mm.then_inc(x2T_done, 1)

            def router(b):
                n, _, _ = b
                pe.wait_ge(x2T_copied, n + 1)
                for k in range(KC):
                    mm = pe.matmul(w_ps[0:T, 1, 0:E], x2T[:, k, :], wr[:, k, :], start=(k == 0), stop=(k == KC - 1))
                mm.then_inc(lg_done, 1)

            def before(b):
                return (b[0] - 1, None, None)

            def lead_in(b):
                pe.wait_ge(loaded, LOADS)
                pe.wait_ge(wq_done, 1)
                pe.wait_ge(masked, 2)
                x_transpose(b)
                for p in range(PAIRS):
                    keys_queries(b, p)
                    if p > 1:
                        values(b, p - 2)
                pe.wait_ge(v_copied, PAIRS - 2)
                x_transpose((1, 0, 1))
                scores(b, 0)

            def batch(b, nb, has_prev, has_next):
                for j in range(PAIRS):
                    prev, p = (b, j - 1) if j else (before(b), PAIRS - 1)
                    prev2, p2 = (b, j - 2) if j > 1 else (before(b), PAIRS - 2 + j)
                    if j > 1 or has_prev:
                        prob_values(prev2, p2, 1)
                    if j < PAIRS - 1:
                        scores(b, j + 1)
                    elif has_next:
                        scores(nb, 0)
                    if has_next:
                        keys_queries(nb, j)
                    if j or has_prev:
                        prob_transpose(prev, p, 0)
                    if j < 2:
                        if j == 0:
                            pe.wait_ge(xT_copied, b[0] + 2)
                        values(b, PAIRS - 2 + j)
                    elif has_next:
                        if j == 2 and has_prev:
                            pe.wait_ge(sum_done, b[0])
                        if j == 5 and has_prev:
                            pe.wait_ge(x2T_copied, b[0])
                        if j == 6 and has_prev:
                            pe.wait_ge(lg_copied, b[0])
                        if j == 7:
                            pe.wait_ge(oT_copied, b[0] * 2 + 1)
                        values(nb, j - 2)
                    if j or has_prev:
                        prob_transpose(prev, p, 1)
                        prob_values(prev, p, 0)
                    copied = b[0] * PAIRS + PAIRS - 1 + j
                    if j == 1 and has_prev:
                        pe.wait_ge(v_copied, copied)
                        out_transpose(before(b), 1)
                        out_project(before(b))
                    if j == 4 and has_prev:
                        if has_next:
                            pe.wait_ge(v_copied, copied)
                        x2_transpose(before(b))
                    if j == 5 and has_prev:
                        if has_next:
                            pe.wait_ge(v_copied, copied)
                        router(before(b))
                    if j == 6:
                        if has_next:
                            pe.wait_ge(v_copied, copied)
                        else:
                            pe.wait_ge(lg_copied, b[0])
                        out_transpose(b, 0)
                    if j == PAIRS - 1 and has_next:
                        pe.wait_ge(v_copied, copied)
                        x_transpose((nb[0] + 1, None, None))

            def lead_out(b):
                prob_values(b, PAIRS - 2, 1)
                prob_transpose(b, PAIRS - 1, 0)
                prob_transpose(b, PAIRS - 1, 1)
                prob_values(b, PAIRS - 1, 0)
                prob_values(b, PAIRS - 1, 1)
                pe.wait_ge(oT_copied, 2 * b[0] + 1)
                out_transpose(b, 1)
                out_project(b)
                x2_transpose(b)
                router(b)

            run(pe, batch, lead_in, lead_out)

        @block.scalar
        def _(act):
            def x_copy(n):
                act.wait_ge(xT_done, n + 1)
                act.wait_ge(kq_done, n * PAIRS)
                act.activation(xT[:].rearrange("p k t -> p (k t)"), w_ps[:, 1, 0:KC * T], ACT.Copy).then_inc(xT_copied, 1)

            def keys_queries(b, p):
                n, _, _ = b
                act.wait_ge(kq_done, n * PAIRS + p + 1)
                if not (isinstance(n, int) and n == 0):
                    act.wait_ge(s_done, (n - 1) * H + 2 * p + 2)
                act.activation(kT[:, p, :], w_ps[:, 0, 0:S2], ACT.Copy)
                act.activation(qT[:, p, :], w_ps[:, 0, 384:384 + T], ACT.Copy).then_inc(kq_copied, 1)

            def values(b, p):
                n, _, _ = b
                act.wait_ge(v_done, n * PAIRS + p + 1)
                if not (isinstance(n, int) and n == 0):
                    act.wait_ge(pv_done, (n - 1) * PAIRS + p + 1)
                act.activation(v[:, :, 2 * p:2 * p + 2, 0:DH],
                               w_ps[0:SC, 1, 0:NSC * 128].rearrange("p (c h d) -> p c h d", c=NSC, h=2),
                               ACT.Copy).then_inc(v_copied, 1)

            def prob_copy(b, p, hh):
                n, _, _ = b
                h = 2 * p + hh
                act.wait_ge(pT_done, n * H + h + 1)
                if not (isinstance(n, int) and n == 0 and p == 0):
                    act.wait_ge(pv_done, n * PAIRS + p)
                act.activation(pT[:, hh, :, :].rearrange("p c t -> p (c t)"), pT_ps[:, hh, 0:NSC * T], ACT.Copy).then_inc(pT_copied, 1)

            def score_copy(b, p, hh):
                n, _, _ = b
                h = 2 * p + hh
                act.wait_ge(s_done, n * H + h + 1)
                if not (isinstance(n, int) and n == 0 and h < 4):
                    act.wait_ge(kept_done, n * H + (h - 3))
                act.activation(s_sb[:, h % 4, :], s_ps[:, hh, 0:S2], ACT.Copy).then_inc(s_copied, 1)

            def exps(b, p, hh):
                n, _, _ = b
                h = 2 * p + hh
                act.wait_ge(nmax_done, n * H + h + 1)
                if not (isinstance(n, int) and n == 0 and h < 4):
                    act.wait_ge(pT_done, n * H + (h - 3))
                act.activation(prob[:, h % 4, :], s_sb[:, h % 4, :], ACT.Exp, bias=nmax[:, h % 4:h % 4 + 1], scale=scale,
                               accum_out=full_sum[:, h:h + 1]).then_inc(exp_done, 1)

            def out_copy(b, half):
                n, _, _ = b
                act.wait_ge(oT_done, n * 2 + half + 1)
                if not (isinstance(n, int) and n == 0):
                    act.wait_ge(wo_done, n)
                act.activation(oT[:, 4 * half:4 * half + 4, :].rearrange("p q t -> p (q t)"), w_ps[:, 1, 0:4 * T],
                               ACT.Copy).then_inc(oT_copied, 1)

            def x2_copy(b):
                n, _, _ = b
                act.wait_ge(x2T_done, n + 1)
                act.activation(x2T[:].rearrange("p k t -> p (k t)"), w_ps[:, 1, 0:KC * T], ACT.Copy).then_inc(x2T_copied, 1)

            def before(b):
                return (b[0] - 1, None, None)

            def lead_in(b):
                x_copy(0)
                for p in range(PAIRS):
                    keys_queries(b, p)
                    if p > 1:
                        values(b, p - 2)
                x_copy(1)
                score_copy(b, 0, 0)
                score_copy(b, 0, 1)

            def batch(b, nb, has_prev, has_next):
                for j in range(PAIRS):
                    prev, p = (b, j - 1) if j else (before(b), PAIRS - 1)
                    exps(b, j, 0)
                    exps(b, j, 1)
                    if j < PAIRS - 1:
                        score_copy(b, j + 1, 0)
                    elif has_next:
                        score_copy(nb, 0, 0)
                    if has_next:
                        keys_queries(nb, j)
                    if j or has_prev:
                        prob_copy(prev, p, 0)
                    if j < PAIRS - 1:
                        score_copy(b, j + 1, 1)
                    elif has_next:
                        score_copy(nb, 0, 1)
                    if j < 2:
                        values(b, PAIRS - 2 + j)
                    elif has_next:
                        values(nb, j - 2)
                    if j or has_prev:
                        prob_copy(prev, p, 1)
                    if j == 1 and has_prev:
                        out_copy(before(b), 1)
                    if j == 4 and has_prev:
                        x2_copy(before(b))
                    if j == 6:
                        out_copy(b, 0)
                    if j == PAIRS - 1 and has_next:
                        x_copy(nb[0] + 1)

            def lead_out(b):
                prob_copy(b, PAIRS - 1, 0)
                prob_copy(b, PAIRS - 1, 1)
                out_copy(b, 1)
                x2_copy(b)

            run(act, batch, lead_in, lead_out)

        @block.gpsimd
        def _(pool):
            pool.memset(neghalf[:], -0.5).then_inc(half_done, 1)
            pool.wait_ge(half_done, 1)

            def stage(n):
                pool.wait_ge(half_done, 1)
                pool.wait_ge(xT_done, n)
                pool.tensor_copy(x_stage[:], xres[:, bass.ds(n, 1), 0:C].rearrange("p b c -> p (b c)")).then_inc(stage_done, 1)

            def lead_in(b):
                stage(0)
                stage(1)

            def keep(n):
                pool.wait_ge(half_done, 1)
                pool.wait_ge(x2_done, n + 1)
                pool.tensor_copy(xres[:, bass.ds(n, 1), 0:C].rearrange("p b c -> p (b c)"), x2[:]).then_inc(x2_kept, 1)

            def norm(n):
                pool.wait_ge(veps_done, n + 1)
                pool.tensor_tensor(rstd[:], veps[:], neghalf[:], ALU.pow).then_inc(rstd_done, 1)

            def keep_mask(b, p, hh):
                n, _, _ = b
                waits = [(max_done, n * 64 + p * 8 + 6 + hh + 1)]
                if not (isinstance(n, int) and n == 0 and p == 0):
                    waits.append((p_done, n * H + (2 * p + hh - 1)))
                wait_apart(pool, half_done, *waits)
                pool.tensor_scalar(kept[:, hh, :], s_sb[:, (2 * p + hh) % 4, :], top[:, p % 2, hh, TOPK - 1:TOPK], None,
                                   ALU.is_ge).then_inc(kept_done, 1)

            def keep_probs(b, p, hh):
                n, _, _ = b
                h = 2 * p + hh
                pool.wait_ge(kept_done, n * H + h + 1)
                pool.wait_ge(exp_done, n * H + h + 1)
                pool.tensor_tensor(prob[:, h % 4, :], prob[:, h % 4, :], kept[:, hh, :], ALU.mult).then_inc(p_done, 1)

            def max_negate(b, j, hh):
                n, _, _ = b
                h = 2 * j + hh
                if not (isinstance(n, int) and n == 0 and h < 4):
                    pool.wait_ge(exp_done, n * H + (h - 3))
                wait_apart(pool, half_done, (max_done, n * 64 + j * 8 + hh + 1))
                pool.tensor_scalar(nmax[:, h % 4:h % 4 + 1], top[:, j % 2, hh, 0:1], -scale, 0.0, ALU.mult, ALU.add).then_inc(
                    nmax_done, 1)

            def before(b):
                return (b[0] - 1, None, None)

            def batch(b, nb, has_prev, has_next):
                n = b[0]
                for j in range(PAIRS):
                    prev, p = (b, j - 1) if j else (before(b), PAIRS - 1)
                    if j or has_prev:
                        keep_mask(prev, p, 0)
                    max_negate(b, j, 0)
                    max_negate(b, j, 1)
                    if j or has_prev:
                        keep_probs(prev, p, 0)
                        keep_mask(prev, p, 1)
                        keep_probs(prev, p, 1)
                    if j == 3 and has_prev:
                        norm(n - 1)
                    if j == 5 and has_prev:
                        keep(n - 1)
                    if j == 5 and has_next:
                        stage(n + 2)

            def lead_out(b):
                for hh in range(2):
                    keep_mask(b, PAIRS - 1, hh)
                    keep_probs(b, PAIRS - 1, hh)
                norm(b[0])
                keep(b[0])

            run(pool, batch, lead_in, lead_out)

        @block.vector
        def _(dve):
            def half_out(b, half, part):
                n, _, _ = b
                hs = slice(8 * half, 8 * half + 8)
                m = n * 2 + half + 1
                o_half = o_ps[:, :, 0:4 * (DH + 1)].rearrange("p k (h d) -> p k h d", d=DH + 1)
                if part == 0:
                    dve.wait_ge(pv_done, n * PAIRS + 4 * half + 4)
                    dve.scalar_tensor_tensor(total[:, hs].rearrange("p (k h) -> p k h", k=2),
                                             full_sum[:, hs].rearrange("p (k h) -> p k h", k=2), 1e-8, o_half[:, :, :, DH],
                                             ALU.mult, ALU.add).then_inc(total_done, 1)
                if part == 1:
                    dve.wait_ge(total_done, m)
                    dve.reciprocal(rtotal[:, hs], total[:, hs]).then_inc(rtotal_done, 1)
                if part == 2:
                    dve.wait_ge(rtotal_done, m)
                    dve.wait_ge(oT_done, m - 1)
                    dve.tensor_tensor(o[:].rearrange("p (k h) d -> p k h d", k=2), o_half[:, :, :, 0:DH],
                                      rtotal[:, hs].rearrange("p (k h) -> p k h", k=2).unsqueeze(3).to_broadcast([T, 2, 4, DH]),
                                      ALU.mult).then_inc(o_done, 1)

            def residual(b, part):
                n, _, _ = b
                xr = xres[:, bass.ds(n, 1), 0:C].rearrange("p b c -> p (b c)")
                if part == 0:
                    dve.wait_ge(wo_done, n + 1)
                    dve.tensor_tensor(summed[:], w_ps[0:T, 1, 0:C], xr, ALU.add).then_inc(sum_done, 1)
                if part == 1:
                    dve.wait_ge(sum_done, n + 1)
                    dve.bn_stats(stats[:], summed[:]).then_inc(stats_done, 1)
                if part == 2:
                    dve.wait_ge(wq_done, 1)
                    dve.wait_ge(stats_done, n + 1)
                    dve.bn_aggr(mv[:], stats[:]).then_inc(mv_done, 1)
                if part == 3:
                    dve.wait_ge(mv_done, n + 1)
                    dve.tensor_scalar(veps[:], mv[:, 1:2], LN_EPS, None, ALU.add).then_inc(veps_done, 1)
                if part == 4:
                    dve.wait_ge(rstd_done, n + 1)
                    dve.tensor_scalar(x2[:], summed[:], mv[:, 0:1], rstd[:, 0:1], ALU.subtract, ALU.mult).then_inc(x2_done, 1)

            def logit_copy(b):
                n, _, _ = b
                dve.wait_ge(lg_done, n + 1)
                dve.tensor_tensor(logits[:, bass.ds(n, 1), :].rearrange("p b e -> p (b e)"), w_ps[0:T, 1, 0:E], br_sb[:],
                                  ALU.add).then_inc(lg_copied, 1)

            def before(b):
                return (b[0] - 1, None, None)

            def lead_in(b):
                dve.memset(v[:, :, :, DH:DH + 1], 1.0)
                dve.memset(mask_bias[:], 0.0).then_inc(masked, 1)
                dve.wait_ge(masked, 1)
                dve.wait_ge(loaded, LOADS)
                dve.tensor_scalar(mask_bias[0:B, :], mask_u8[:], 1.0, 1e30, ALU.subtract, ALU.mult).then_inc(masked, 1)
                for k in range(KC):
                    w = wq[:, k, :].rearrange("p (h d) -> p h d", h=H)
                    last = dve.tensor_tensor(w, w, temp[:].unsqueeze(2).to_broadcast([128, H, DH]), ALU.mult)
                last.then_inc(wq_done, 1)

            def batch(b, nb, has_prev, has_next):
                n = b[0]
                for j in range(PAIRS):
                    for r in range(TOPK // 8):
                        for hh in range(2):
                            h = 2 * j + hh
                            src = s_sb[:, h % 4, :] if r == 0 else work[:, hh, :]
                            if r == 0:
                                wait_apart(dve, wq_done, (s_copied, n * H + h + 1))
                            else:
                                wait_apart(dve, wq_done, (rep_done, n * 48 + j * 6 + 2 * (r - 1) + hh + 1))
                            dve.max(top[:, j % 2, hh, 8 * r:8 * r + 8], src).then_inc(max_done, 1)
                        if j == 1 and has_prev and r < 3:
                            half_out(before(b), 1, r)
                        if j == 5 and r < 3:
                            half_out(b, 0, r)
                        if r == TOPK // 8 - 1:
                            break
                        for hh in range(2):
                            h = 2 * j + hh
                            src = s_sb[:, h % 4, :] if r == 0 else work[:, hh, :]
                            wait_apart(dve, wq_done, (max_done, n * 64 + j * 8 + 2 * r + hh + 1))
                            dve.match_replace(work[:, hh, :], top[:, j % 2, hh, 8 * r:8 * r + 8], src, GONE).then_inc(rep_done, 1)
                        if j == 2 and has_prev and r < 2:
                            residual(before(b), r)
                        if j == 3 and has_prev and r < 2:
                            residual(before(b), 2 + r)
                        if j == 4 and has_prev and r == 0:
                            residual(before(b), 4)
                        if j == 6 and has_prev and r == 0:
                            logit_copy(before(b))

            def lead_out(b):
                for part in range(3):
                    half_out(b, 1, part)
                for part in range(5):
                    residual(b, part)
                logit_copy(b)

            run(dve, batch, lead_in, lead_out)
            dve.wait_ge(x2_kept, B)
            dve.wait_ge(lg_copied, B)


def expert_phase(nc, xres, logits, ident_sb, lower, W1, b1T, W2, b2, fin, xg, out):
    ctx = ExitStack()
    with ctx:
        def sb(name, shape, dt=F32):
            return ctx.enter_context(nc.sbuf_tensor("e_" + name, shape, dt))

        def ps(name, shape, dt=F32):
            return ctx.enter_context(nc.psum_tensor("e_" + name, shape, dt))

        def sem(name):
            return ctx.enter_context(nc.semaphore("e_" + name))

        BE = B * E
        lower_sb = sb("lower_sb", [T, 2, T], BF16)
        first = sb("first", [T, E])
        token = sb("token", [T, B])
        reset = sb("reset", [T, E, B])
        pick1, pick2 = sb("pick1", [T, B, E]), sb("pick2", [T, B, E])
        rest, tmp = sb("rest", [T, B, E]), sb("tmp", [T, B, E])
        sel = sb("sel", [T, B, E], BF16)
        val = sb("val", [T, 2, B])
        where = sb("where", [T, 2, B])
        gate = sb("gate", [T, 2, B])
        den = sb("den", [T, B])
        count = sb("count", [T, E, B])
        upto = sb("upto", [T, E, B])
        rank = sb("rank", [T, B, E])
        rankc = sb("rankc", [T, 2, B])
        over = sb("over", [T, 2, B])
        slot_f = sb("slot_f", [T, 2, B])
        slot = sb("slot", [T, 2, B], I32)
        target = sb("target", [T, 2, B], I32)
        w1 = [sb(f"w1_{i}", [128, KC, HID]) for i in range(2)]
        w2 = [sb(f"w2_{i}", [128, HM, C]) for i in range(2)]
        b1_sb = [sb(f"b1_{i}", [128, HM]) for i in range(2)]
        b2_sb = sb("b2_sb", [128, E, C])
        rows = [sb(f"rows{i}", [128, NT, CX]) for i in range(2)]
        rowsT = [sb(f"rowsT{i}", [128, KC, CAP]) for i in range(2)]
        hT = sb("hT", [128, HM, CAP])
        ysum = sb("ysum_e", [128, 2, C])
        yrow = [sb(f"yrow{i}", [128, NT, C]) for i in range(2)]
        part = [sb(f"part{i}", [T, 2, GB, C]) for i in range(2)]
        stats = sb("stats_e", [T, GB, 6])
        mv = sb("mv_e", [T, GB, 2])
        veps = sb("veps_e", [T, GB])
        rstd = sb("rstd_e", [T, GB])
        neghalf = sb("neghalf_e", [T, GB])

        t_ps = ps("t_ps", [128, 2, 512])
        h_ps = ps("h_ps_e", [128, 4, 512])
        y_ps = ps("y_ps", [128, 2, 512])

        consts = sem("consts")
        pool_done = sem("pool_done")
        d = sem("route_step")
        exp_done = sem("gate_exp_done")
        counted = sem("counted")
        x_sent = [sem(f"x_sent{i}") for i in range(2)]
        aux_done = sem("aux_done")
        e_loaded = [sem(f"e_loaded{i}") for i in range(2)]
        rows_loaded = [sem(f"rows_loaded{i}") for i in range(2)]
        rt_done, rt_copied = sem("rt_done"), sem("rt_copied")
        h_done, h_copied = sem("h_done_e"), sem("h_copied")
        y_done, y_added, y_scaled = sem("y_done_e"), sem("y_added"), sem("y_scaled")
        y_sent = [sem(f"y_sent{i}") for i in range(2)]
        part_loaded = [sem(f"part_loaded{i}") for i in range(2)]
        add1_done, add2_done = sem("add1_done"), sem("add2_done")
        stats_done, mv_done, veps_done, rstd_done = sem("stats_done_e"), sem("mv_done_e"), sem("veps_done_e"), sem("rstd_done_e")
        norm_done = sem("norm_done_e")
        o_sent = [sem(f"o_sent{i}") for i in range(2)]

        block = ctx.enter_context(nc.Block())
        w1_v = W1.rearrange("e (k p) h -> e p k h", p=128)
        w2_v = W2.rearrange("e (m p) c -> e p m c", p=128)
        xg_v = xg.rearrange("(e i p) c -> e p i c", e=E, p=128)
        fin_v = fin.rearrange("(c b t) d -> b t c d", c=2, t=T)
        out_v = out.rearrange("b t c -> t b c")

        @block.sync
        def _(sp):
            sp.dma_start(lower_sb[:], lower).then_inc(consts, 16)
            sp.dma_start(b2_sb[:], b2.rearrange("(a e) c -> a e c", a=1).to_broadcast([128, E, C])).then_inc(consts, 16)
            for p in range(2):
                sp.dma_start(w1[p][:], w1_v[p]).then_inc(e_loaded[p], 16)
                sp.dma_start(w2[p][:], w2_v[p]).then_inc(e_loaded[p], 16)
                sp.dma_start(b1_sb[p][:], b1T[p]).then_inc(e_loaded[p], 16)
            sp.wait_ge(x_sent[0], 16 * B)
            sp.wait_ge(x_sent[1], 16 * B)
            for p in range(2):
                sp.dma_start(rows[p][:], xg_v[p]).then_inc(rows_loaded[p], 16)
            with sp.Fori(0, E // 2 - 1) as i:
                for p in range(2):
                    e = 2 * i + p
                    sp.wait_ge(consts, 32)
                    sp.wait_ge(h_copied, 16 * e + 16)
                    sp.dma_start(w1[p][:], w1_v[bass.ds(e + 2, 1)].rearrange("e p k h -> p (e k) h")).then_inc(e_loaded[p], 16)
                    sp.dma_start(b1_sb[p][:], b1T[bass.ds(e + 2, 1)].rearrange("e p m -> p (e m)")).then_inc(e_loaded[p], 16)
                    sp.wait_ge(y_done, NT * e + NT)
                    sp.dma_start(w2[p][:], w2_v[bass.ds(e + 2, 1)].rearrange("e p k h -> p (e k) h")).then_inc(e_loaded[p], 16)
                    sp.wait_ge(y_sent[p], 16 * NT * (i + 1))
                    sp.dma_start(rows[p][:], xg_v[bass.ds(e + 2, 1)].rearrange("e p i c -> p (e i) c")).then_inc(rows_loaded[p], 16)
            for p in range(2):
                sp.wait_ge(y_sent[p], 16 * NT * (E // 2))
            for g in range(2):
                for c in range(2):
                    sp.dma_start(part[g][:, c], fin_v[g * GB:(g + 1) * GB, :, c, :].rearrange("b t d -> t b d")).then_inc(part_loaded[g], 16)
            for g in range(GROUPS):
                p = g % 2
                sp.wait_ge(norm_done, g + 1)
                sp.dma_start(out_v[:, g * GB:(g + 1) * GB, :], part[p][:, 0]).then_inc(o_sent[p], 16)
                if g + 2 < GROUPS:
                    sp.wait_ge(o_sent[p], 16 * (g // 2 + 1))
                    for c in range(2):
                        sp.dma_start(part[p][:, c], fin_v[(g + 2) * GB:(g + 3) * GB, :, c, :].rearrange("b t d -> t b d")).then_inc(
                            part_loaded[p], 16)
            for p in range(2):
                sp.wait_ge(o_sent[p], 16 * (GROUPS // 2))

        @block.gpsimd
        def _(pool):
            pool.memset(neghalf[:], -0.5).then_inc(pool_done, 1)
            pool.iota(first[:], [[-1, E]], base=E, channel_multiplier=0, allow_small_or_imprecise_dtypes=True).then_inc(pool_done, 1)
            pool.iota(token[:], [[T, B]], base=0, channel_multiplier=1, allow_small_or_imprecise_dtypes=True).then_inc(pool_done, 1)
            for c in range(2):
                pool.wait_ge(aux_done, c + 1)
                for b in range(B):
                    pool.indirect_dma_start(xg, bass.IndirectOffsetOnAxis(ap=slot[:, c, b:b + 1], axis=0), xres[:, b, :], None,
                                            bounds_check=E * CAP - 1, oob_is_err=False).then_inc(x_sent[c], 16)
            bound = pool.to_reg(2 * N - 1)
            with pool.Fori(0, E // 2) as i:
                for p in range(2):
                    for t in range(NT):
                        wait_apart(pool, pool_done, (y_scaled, (2 * i + p) * NT + t + 1))
                        pool.indirect_dma_start(fin, bass.IndirectOffsetOnAxis(ap=rows[p][:, t, C + 1:C + 2].bitcast(I32), axis=0),
                                                yrow[p][:, t, :], None, bounds_check=bound, oob_is_err=False).then_inc(y_sent[p], 16)
            for g in range(GROUPS):
                pool.wait_ge(veps_done, g + 1)
                pool.tensor_tensor(rstd[:], veps[:], neghalf[:], ALU.pow).then_inc(rstd_done, 1)

        @block.tensor
        def _(pe):
            pe.wait_ge(consts, 32)
            pe.wait_ge(d, SEL_STEP)
            s = sel[:].rearrange("p b e -> p (b e)")
            pe.matmul(t_ps[0:T, 0, 0:BE], lower_sb[:, 0, :], s, start=True, stop=True)
            pe.matmul(t_ps[0:T, 1, 0:BE], lower_sb[:, 1, :], s, start=True, stop=True).then_inc(counted, 1)

            def turn(p, e, i):
                pe.wait_ge(rows_loaded[p], 16 * (i + 1))
                q = 0
                for k in range(KC):
                    for t in range(NT):
                        if q % 4 == 0:
                            n = e * TB + q // 4
                            if isinstance(n, int) and n < 2:
                                pass
                            else:
                                pe.wait_ge(rt_copied, n - 1)
                        mm = pe.transpose(t_ps[:, (q // 4) % 2, (q % 4) * 128:(q % 4 + 1) * 128], rows[p][:, t, k * 128:(k + 1) * 128], ident_sb[:])
                        q += 1
                        if q % 4 == 0 or q == KC * NT:
                            mm.then_inc(rt_done, 1)

            def expert(p, e, i, last):
                pe.wait_ge(e_loaded[p], 48 * (i + 1))
                pe.wait_ge(rt_copied, (e + 1) * TB)
                for m in range(HM):
                    for half in range(2):
                        n = e * 16 + 2 * m + half
                        if not (isinstance(n, int) and n < 4):
                            pe.wait_ge(h_copied, n - 3)
                        for k in range(KC):
                            mm = pe.matmul(h_ps[:, (2 * m + half) % 4, 0:HALF], w1[p][:, k, m * 128:(m + 1) * 128],
                                           rowsT[p][:, k, half * HALF:(half + 1) * HALF], start=(k == 0), stop=(k == KC - 1))
                        mm.then_inc(h_done, 1)
                if not last:
                    turn(1 - p, e + 1, i + p)
                for t in range(NT):
                    n = e * NT + t
                    if not (isinstance(n, int) and n < 2):
                        pe.wait_ge(y_added, n - 1)
                    if t == 0:
                        pe.wait_ge(h_copied, (e + 1) * 16)
                    for m in range(HM):
                        mm = pe.matmul(y_ps[:, (p * NT + t) % 2, 0:C], hT[:, m, t * 128:(t + 1) * 128], w2[p][:, m, :],
                                       start=(m == 0), stop=(m == HM - 1))
                    mm.then_inc(y_done, 1)

            pe.wait_ge(d, COUNT_STEP)
            turn(0, 0, 0)
            expert(0, 0, 0, False)
            with pe.Fori(0, E // 2 - 1) as i:
                expert(1, 2 * i + 1, i, False)
                expert(0, 2 * i + 2, i + 1, False)
            expert(1, E - 1, E // 2 - 1, True)

        @block.scalar
        def _(act):
            act.wait_ge(d, VAL_STEP)
            act.activation(gate[:, 1, :], gate[:, 1, :], ACT.Exp).then_inc(exp_done, 1)

            def turn(p, e):
                q = 0
                done = 0
                while q < KC * NT:
                    k = min(4, KC * NT - q)
                    act.wait_ge(rt_done, e * TB + done + 1)
                    if done == 0 and not (isinstance(e, int) and e < 2):
                        act.wait_ge(h_done, (e - 1) * 16)
                    flat = rowsT[p][:].rearrange("p k n -> p (k n)")
                    act.activation(flat[:, q * 128:(q + k) * 128], t_ps[:, done % 2, 0:k * 128], ACT.Copy).then_inc(rt_copied, 1)
                    q += k
                    done += 1

            def expert(p, e, last):
                for m in range(HM):
                    for half in range(2):
                        act.wait_ge(h_done, e * 16 + 2 * m + half + 1)
                        if m == 0 and half == 0:
                            act.wait_ge(y_done, e * NT)
                        act.activation(hT[:, m, half * HALF:(half + 1) * HALF], h_ps[:, (2 * m + half) % 4, 0:HALF], ACT.Gelu,
                                       bias=b1_sb[p][:, m:m + 1]).then_inc(h_copied, 1)
                if not last:
                    turn(1 - p, e + 1)

            turn(0, 0)
            expert(0, 0, False)
            with act.Fori(0, E // 2 - 1) as i:
                expert(1, 2 * i + 1, False)
                expert(0, 2 * i + 2, False)
            expert(1, E - 1, True)

        @block.vector
        def _(dve):
            def over_e(a):
                return a.unsqueeze(2).to_broadcast([T, B, E])

            first_b = first[:].unsqueeze(1).to_broadcast([T, B, E])
            n = [0]

            def step(ins):
                ins.then_inc(d, 1)
                n[0] += 1
                dve.wait_ge(d, n[0])

            dve.wait_ge(pool_done, 3)
            step(dve.memset(reset[:], 1.0))
            step(dve.memset(reset[:, :, 0:1], 0.0))
            step(dve.tensor_reduce(val[:, 0, :], logits[:], AX_X, ALU.max))
            step(dve.tensor_tensor(tmp[:], logits[:], over_e(val[:, 0, :]), ALU.is_equal))
            step(dve.tensor_tensor(tmp[:], tmp[:], first_b, ALU.mult))
            step(dve.tensor_reduce(where[:, 0, :], tmp[:], AX_X, ALU.max))
            step(dve.tensor_tensor(pick1[:], over_e(where[:, 0, :]), first_b, ALU.is_equal))
            step(dve.scalar_tensor_tensor(rest[:], pick1[:], GONE, logits[:], ALU.mult, ALU.add))
            step(dve.tensor_reduce(val[:, 1, :], rest[:], AX_X, ALU.max))
            step(dve.tensor_tensor(tmp[:], rest[:], over_e(val[:, 1, :]), ALU.is_equal))
            step(dve.tensor_tensor(tmp[:], tmp[:], first_b, ALU.mult))
            step(dve.tensor_reduce(where[:, 1, :], tmp[:], AX_X, ALU.max))
            step(dve.tensor_tensor(pick2[:], over_e(where[:, 1, :]), first_b, ALU.is_equal))
            step(dve.tensor_tensor(sel[:], pick1[:], pick2[:], ALU.add))
            assert n[0] == SEL_STEP
            step(dve.tensor_tensor(gate[:, 1, :], val[:, 1, :], val[:, 0, :], ALU.subtract))
            assert n[0] == VAL_STEP
            dve.wait_ge(counted, 1)
            step(dve.tensor_copy(count[:], t_ps[0:T, 1, 0:BE].rearrange("p (b e) -> p e b", e=E)))
            step(dve.tensor_tensor_scan(upto[:].rearrange("p e b -> p (e b)"), reset[:].rearrange("p e b -> p (e b)"),
                                        count[:].rearrange("p e b -> p (e b)"), 0.0, ALU.mult, ALU.add))
            step(dve.tensor_tensor(upto[:], upto[:], count[:], ALU.subtract))
            step(dve.tensor_tensor(rank[:], t_ps[0:T, 0, 0:BE].rearrange("p (b e) -> p b e", e=E),
                                   upto[:].rearrange("p e b -> p b e"), ALU.add))
            assert n[0] == COUNT_STEP
            for c, pick in enumerate((pick1, pick2)):
                step(dve.tensor_tensor(tmp[:], rank[:], pick[:], ALU.mult))
                step(dve.tensor_reduce(rankc[:, c, :], tmp[:], AX_X, ALU.add))
            step(dve.tensor_scalar(over[:], rankc[:], float(CAP), float(E * CAP), ALU.is_ge, ALU.mult))
            step(dve.tensor_scalar(slot_f[:], where[:], -float(CAP), float(E * CAP), ALU.mult, ALU.add))
            step(dve.tensor_tensor(slot_f[:], slot_f[:], rankc[:], ALU.add))
            step(dve.tensor_tensor(slot_f[:], slot_f[:], over[:], ALU.add))
            step(dve.tensor_copy(slot[:], slot_f[:]))
            step(dve.tensor_copy(target[:, 0, :], token[:]))
            step(dve.tensor_scalar(target[:, 1, :], token[:], float(N), None, ALU.add))
            dve.wait_ge(exp_done, 1)
            step(dve.tensor_scalar(den[:], gate[:, 1, :], 1.0, None, ALU.add))
            step(dve.reciprocal(gate[:, 0, :], den[:]))
            step(dve.tensor_tensor(gate[:, 1, :], gate[:, 1, :], gate[:, 0, :], ALU.mult))
            for c in range(2):
                if c:
                    dve.wait_ge(x_sent[0], 16 * B)
                step(dve.tensor_copy(xres[:, 0:B, C], gate[:, c, :]))
                dve.tensor_copy(xres[:, 0:B, C + 1].bitcast(I32), target[:, c, :]).then_inc(aux_done, 1)

            def expert(p, e, i):
                for t in range(NT):
                    dve.wait_ge(y_done, e * NT + t + 1)
                    if not (isinstance(e, int) and e == 0 and t < 2):
                        dve.wait_ge(y_scaled, e * NT + (t - 1))
                    dve.tensor_tensor(ysum[:, (p * NT + t) % 2, :], y_ps[:, (p * NT + t) % 2, 0:C], b2_of(e), ALU.add).then_inc(y_added, 1)
                    if t == 0:
                        dve.wait_ge(y_sent[p], 16 * NT * i)
                    dve.wait_ge(y_added, e * NT + t + 1)
                    dve.tensor_scalar(yrow[p][:, t, :], ysum[:, (p * NT + t) % 2, :], rows[p][:, t, C:C + 1], None, ALU.mult).then_inc(y_scaled, 1)

            def b2_of(e):
                if isinstance(e, int):
                    return b2_sb[:, e, :]
                return b2_sb[:, bass.ds(e, 1), :].rearrange("p e c -> p (e c)")

            expert(0, 0, 0)
            expert(1, 1, 0)
            with dve.Fori(1, E // 2) as i:
                expert(0, 2 * i, i)
                expert(1, 2 * i + 1, i)
            for g in range(GROUPS):
                pt = part[g % 2]
                xr = xres[:, g * GB:(g + 1) * GB, 0:C]
                dve.wait_ge(part_loaded[g % 2], 32 * (g // 2 + 1))
                dve.tensor_tensor(pt[:, 0], pt[:, 0], pt[:, 1], ALU.add).then_inc(add1_done, 1)
                dve.wait_ge(add1_done, g + 1)
                dve.tensor_tensor(pt[:, 0], pt[:, 0], xr, ALU.add).then_inc(add2_done, 1)
                dve.wait_ge(add2_done, g + 1)
                for b in range(GB):
                    last = dve.bn_stats(stats[:, b, :], pt[:, 0, b, :])
                last.then_inc(stats_done, 1)
                dve.wait_ge(stats_done, g + 1)
                for b in range(GB):
                    last = dve.bn_aggr(mv[:, b, :], stats[:, b, :])
                last.then_inc(mv_done, 1)
                dve.wait_ge(mv_done, g + 1)
                dve.tensor_scalar(veps[:], mv[:, :, 1], LN_EPS, None, ALU.add).then_inc(veps_done, 1)
                dve.wait_ge(rstd_done, g + 1)
                for b in range(GB):
                    last = dve.tensor_scalar(pt[:, 0, b, :], pt[:, 0, b, :], mv[:, b, 0:1], rstd[:, b:b + 1], ALU.subtract, ALU.mult)
                last.then_inc(norm_done, 1)


def kernel(**inputs):
    import ml_dtypes
    import numpy as np
    from concourse import bacc
    from concourse.bass_utils import run_bass_kernel_spmd

    a = {k: np.asarray(v) for k, v in inputs.items()}
    tri = np.triu(np.ones((T, T)), 1)
    pick_rows = np.zeros((128, B, T), ml_dtypes.bfloat16)
    for b in range(B):
        pick_rows[b, b] = 1
    spread = np.zeros((BC_ROWS, 2 * NSTATE, 128), ml_dtypes.bfloat16)
    for at in BC_AT:
        for r in range(2 * NSTATE):
            spread[at + r, r] = 1
    arrays = {
        "x": a["x"],
        "xT": a["x"].reshape(N, C).T,
        "W_inT": a["L0_attn_W_in"].T,
        "Kx": a["L0_attn_Kx"],
        "Kz": a["L0_attn_Kz"],
        "W_xprojT": a["L0_attn_W_xproj"].T,
        "W_dtT": a["L0_attn_W_dt"].T,
        "b_dt": a["L0_attn_b_dt"],
        "A_log": a["L0_attn_A_log"],
        "D": a["L0_attn_D"],
        "W_outT": a["L0_attn_W_out"].T,
        "ctxT": a["ctx_1024"].transpose(0, 2, 1),
        "mask": a["mask_BxS2_bf1"].view(np.uint8),
        "Wq": a["L0_xattn_Wq"],
        "Wk": a["L0_xattn_Wk"],
        "Wv": a["L0_xattn_Wv"],
        "Wo": a["L0_xattn_Wo"],
        "inv_temp": a["L0_xattn_inv_temp"],
        "Wr": a["L0_ffn_Wr"],
        "br": a["L0_ffn_br"],
        "W1": a["L0_ffn_W1"],
        "b1T": a["L0_ffn_b1"].reshape(E, HM, 128).transpose(0, 2, 1),
        "W2": a["L0_ffn_W2"],
        "b2": a["L0_ffn_b2"],
        "ident": np.eye(128, dtype=np.float32),
        "rows_sel": spread,
        "mask_pick": pick_rows,
        "lower": np.stack([tri, np.ones((T, T))], 1).astype(ml_dtypes.bfloat16),
    }
    nc = bacc.Bacc("TRN2", target_bir_lowering=False, num_devices=1)
    feeds, ins = {}, {}
    for name, value in arrays.items():
        value = np.ascontiguousarray(value)
        feeds[f"in_{name}"] = value
        ins[name] = nc.dram_tensor(f"in_{name}", value.shape, mybir.dt.from_np(value.dtype), kind="ExternalInput").ap()
    out = nc.dram_tensor("out_0", (B, T, C), F32, kind="ExternalOutput").ap()
    decoder_kernel(nc, out, ins)
    result = run_bass_kernel_spmd(nc, [feeds], core_ids=[0])
    return result.results[0]["out_0"]
```

```python
from contextlib import ExitStack

import concourse.bass as bass
from concourse import mybir

F32 = mybir.dt.float32
BF16 = mybir.dt.bfloat16
I32 = mybir.dt.int32
U8 = mybir.dt.uint8
ALU = mybir.AluOpType
ACT = mybir.ActivationFunctionType
AX_X = mybir.AxisListType.X

B, T, C = 32, 112, 256
S2 = 375
KC = C // 128
INNER, NSTATE, RANK, TAPS = 128, 8, 16, 3
GB = 4
GROUPS = B // GB
GT = GB * T
DT_AT, BC_AT, BC_ROWS = 32, (0, 64, 96), 112
BLANK_ROWS = 4
ROW_BANKS = 3
H, DH = 16, 64
INNERX = H * DH
PAIRS = H // 2
V_AHEAD = PAIRS - 2
SC, NSC = 125, 3
TOPK = 32
E = 8
N = B * T
HID = 1024
HM = HID // 128
CAP = N * 2 // E
NT = CAP // 128
HALF = CAP // 2
CX = C + 4
GATE1, GATE2, WHERE, TOKEN = C, C + 1, C + 2, C + 3
TB = -(-KC * NT // 4)
NOWHERE = float(1 << 20)
RANK_STEPS = 15
LAST = 5
CHUNKS = ((0, B - LAST - 1), (B - LAST - 1, B))
SEL_STEP, VAL_STEP = 12, 13
GONE = -3e38
LN_EPS = 1e-5
CLIP_LO, CLIP_HI = 1e-4, 1.0
SOFTPLUS_CAP = 10.0



def wait_apart(eng, met, *waits):
    waits = [(sem, value if isinstance(value, int) else eng.to_reg(value)) for sem, value in waits]
    eng.wait_ge(met, 1)
    for sem, value in waits:
        eng.wait_ge(sem, value)


def decoder_kernel(nc, out, ins):
    ctx = ExitStack()
    with ctx:
        def sb(name, shape, dt=F32):
            return ctx.enter_context(nc.sbuf_tensor(name, shape, dt))

        xres = sb("xres", [T, B + 1, CX])
        ident_sb = sb("ident_sb", [128, 128])
        logits = sb("logits", [T, B, E])
        fin = nc.dram_tensor("fin", [2 * N, C], F32).ap()
        xg = nc.dram_tensor("xg", [E * CAP, CX], F32).ap()
        routing = Routing(nc, ctx, xres, logits, xg)
        with ExitStack() as att_ctx:
            att = AttentionInputs(nc, att_ctx)
            state_space_phase(nc, xres, ident_sb, att, routing, ins, ins["xT"], ins["x"], ins["W_inT"], ins["Kx"], ins["Kz"], ins["W_xprojT"],
                              ins["W_dtT"], ins["b_dt"], ins["A_log"], ins["D"], ins["W_outT"], ins["rows_sel"], ins["ident"], fin, xg)
            attention_phase(nc, xres, logits, ident_sb, att, ins["ctxT"], ins["Wo"], routing, ins["lower"])
        expert_phase(nc, routing, ident_sb, ins["W1"], ins["b1T"], ins["W2"], ins["b2"], fin, xg)
        final_phase(nc, xres, fin, out)


class Routing:

    def __init__(self, nc, ctx, xres, logits, xg):
        def sb(name, shape, dt=F32):
            return ctx.enter_context(nc.sbuf_tensor("r_" + name, shape, dt))

        def sem(name):
            return ctx.enter_context(nc.semaphore("r_" + name))

        self.xres, self.logits, self.xg = xres, logits, xg
        self.lower = sb("lower", [T, 2, T], BF16)
        self.first = sb("first", [128, E])
        self.token = sb("token", [T, B])
        self.pick = [sb(f"pick{c}", [T, B, E]) for c in range(2)]
        self.rest, self.tmp = sb("rest", [T, B, E]), sb("tmp", [T, B, E])
        self.sel = sb("sel", [T, B, E], BF16)
        self.val = sb("val", [T, 2, B])
        self.where = sb("where", [T, 2, B])
        self.gap = sb("gap", [T, B])
        self.den = sb("den", [T, B])
        self.reset = [sb(f"reset{k}", [T, E, hi - lo]) for k, (lo, hi) in enumerate(CHUNKS)]
        self.count = [sb(f"count{k}", [T, E, hi - lo]) for k, (lo, hi) in enumerate(CHUNKS)]
        self.upto = [sb(f"upto{k}", [T, E, hi - lo]) for k, (lo, hi) in enumerate(CHUNKS)]
        self.before = sb("before", [T, E, B])
        self.rank = sb("rank", [T, B, E])
        self.rankc = sb("rankc", [T, 2, B])
        self.over = sb("over", [T, 2, B])
        self.slot_f = sb("slot_f", [T, 2, B])
        self.slot = sb("slot", [T, 2, B], I32)
        self.tables = sem("tables")
        self.lower_loaded = sem("lower_loaded")
        self.step_done = sem("step_done")
        self.exp_done = sem("exp_done")
        self.counted = sem("counted")
        self.count_read = sem("count_read")
        self.slots_done = sem("slots_done")
        self.sent = sem("sent")
        self.n = 0
        self.base = [0, 0]

    def pool_tables(self, pool):
        pool.iota(self.first[:], [[-1, E]], base=E, channel_multiplier=0, allow_small_or_imprecise_dtypes=True).then_inc(self.tables, 1)
        pool.iota(self.token[:], [[T, B]], base=0, channel_multiplier=1, allow_small_or_imprecise_dtypes=True).then_inc(self.tables, 1)

    def dve_tables(self, dve):
        for reset in self.reset:
            dve.memset(reset[:], 1.0).then_inc(self.tables, 1)
        dve.wait_ge(self.tables, 4)
        for reset in self.reset:
            dve.memset(reset[:, :, 0:1], 0.0).then_inc(self.tables, 1)

    def step(self, dve, ins):
        ins.then_inc(self.step_done, 1)
        self.n += 1
        dve.wait_ge(self.step_done, self.n)

    def choose(self, dve, chunk):
        lo, hi = CHUNKS[chunk]
        nb = hi - lo

        def step(ins):
            self.step(dve, ins)

        def over_e(a):
            return a.unsqueeze(2).to_broadcast([T, nb, E])

        first_b = self.first[0:T, :].unsqueeze(1).to_broadcast([T, nb, E])
        lg, rest, tmp = self.logits[:, lo:hi, :], self.rest[:, lo:hi, :], self.tmp[:, lo:hi, :]
        val, where = [self.val[:, c, lo:hi] for c in range(2)], [self.where[:, c, lo:hi] for c in range(2)]
        pick = [self.pick[c][:, lo:hi, :] for c in range(2)]
        start = self.n
        self.base[chunk] = start
        dve.wait_ge(self.tables, 6)
        step(dve.tensor_reduce(val[0], lg, AX_X, ALU.max))
        step(dve.tensor_tensor(tmp, lg, over_e(val[0]), ALU.is_equal))
        step(dve.tensor_tensor(tmp, tmp, first_b, ALU.mult))
        step(dve.tensor_reduce(where[0], tmp, AX_X, ALU.max))
        step(dve.tensor_tensor(pick[0], over_e(where[0]), first_b, ALU.is_equal))
        step(dve.scalar_tensor_tensor(rest, pick[0], GONE, lg, ALU.mult, ALU.add))
        step(dve.tensor_reduce(val[1], rest, AX_X, ALU.max))
        step(dve.tensor_tensor(tmp, rest, over_e(val[1]), ALU.is_equal))
        step(dve.tensor_tensor(tmp, tmp, first_b, ALU.mult))
        step(dve.tensor_reduce(where[1], tmp, AX_X, ALU.max))
        step(dve.tensor_tensor(pick[1], over_e(where[1]), first_b, ALU.is_equal))
        step(dve.tensor_tensor(self.sel[:, lo:hi, :], pick[0], pick[1], ALU.add))
        assert self.n - start == SEL_STEP
        step(dve.tensor_tensor(self.gap[:, lo:hi], val[1], val[0], ALU.subtract))
        assert self.n - start == VAL_STEP

    def chosen(self, eng, chunk, step):
        eng.wait_ge(self.step_done, chunk * (VAL_STEP + RANK_STEPS) + step)

    def counts(self, pe, chunk, bank):
        lo, hi = CHUNKS[chunk]
        be = (hi - lo) * E
        sel = self.sel[:, lo:hi, :].rearrange("p b e -> p (b e)")
        self.chosen(pe, chunk, SEL_STEP)
        pe.wait_ge(self.lower_loaded, 16)
        pe.matmul(bank[0:T, 0:be], self.lower[:, 0, :], sel, start=True, stop=True)
        pe.matmul(bank[0:T, be:2 * be], self.lower[:, 1, :], sel, start=True, stop=True).then_inc(self.counted, 1)

    def exps(self, act, chunk):
        lo, hi = CHUNKS[chunk]
        self.chosen(act, chunk, VAL_STEP)
        act.activation(self.gap[:, lo:hi], self.gap[:, lo:hi], ACT.Exp).then_inc(self.exp_done, 1)

    def rank_chunk(self, dve, chunk, bank):
        lo, hi = CHUNKS[chunk]
        nb = hi - lo
        be = nb * E

        def step(ins):
            self.step(dve, ins)

        start = self.n
        count, upto, before, rank = self.count[chunk], self.upto[chunk], self.before[:, :, lo:hi], self.rank[:, lo:hi, :]
        rankc, over, slot_f = self.rankc[:, :, lo:hi], self.over[:, :, lo:hi], self.slot_f[:, :, lo:hi]
        dve.wait_ge(self.counted, chunk + 1)
        step(dve.tensor_copy(count[:], bank[0:T, be:2 * be].rearrange("p (b e) -> p e b", e=E)))
        step(dve.tensor_tensor_scan(upto[:].rearrange("p e b -> p (e b)"), self.reset[chunk][:].rearrange("p e b -> p (e b)"),
                                    count[:].rearrange("p e b -> p (e b)"), 0.0, ALU.mult, ALU.add))
        step(dve.tensor_tensor(before, upto[:], count[:], ALU.subtract))
        if chunk:
            size = CHUNKS[0][1] - CHUNKS[0][0]
            step(dve.tensor_tensor(before, before, self.upto[0][:, :, size - 1:size].to_broadcast([T, E, nb]), ALU.add))
        dve.tensor_tensor(rank, bank[0:T, 0:be].rearrange("p (b e) -> p b e", e=E), before.rearrange("p e b -> p b e"),
                          ALU.add).then_inc(self.count_read, 1)
        dve.wait_ge(self.count_read, chunk + 1)
        for c in range(2):
            step(dve.tensor_tensor(self.tmp[:, lo:hi, :], rank, self.pick[c][:, lo:hi, :], ALU.mult))
            step(dve.tensor_reduce(rankc[:, c, :], self.tmp[:, lo:hi, :], AX_X, ALU.add))
        step(dve.tensor_scalar(over, rankc, float(CAP), float(E * CAP), ALU.is_ge, ALU.mult))
        step(dve.tensor_scalar(slot_f, self.where[:, :, lo:hi], -float(CAP), float(E * CAP), ALU.mult, ALU.add))
        step(dve.tensor_tensor(slot_f, slot_f, rankc, ALU.add))
        step(dve.tensor_tensor(self.slot[:, :, lo:hi], slot_f, over, ALU.add))
        xres = self.xres
        dve.wait_ge(self.exp_done, chunk + 1)
        step(dve.tensor_scalar(self.den[:, lo:hi], self.gap[:, lo:hi], 1.0, None, ALU.add))
        step(dve.reciprocal(xres[:, lo:hi, GATE1], self.den[:, lo:hi]))
        step(dve.tensor_tensor(xres[:, lo:hi, GATE2], self.gap[:, lo:hi], xres[:, lo:hi, GATE1], ALU.mult))
        step(dve.tensor_copy(xres[:, lo:hi, WHERE], self.where[:, 0, lo:hi]))
        assert self.n - start == RANK_STEPS + chunk
        dve.tensor_copy(xres[:, lo:hi, TOKEN], self.token[:, lo:hi]).then_inc(self.slots_done, 1)

    def send(self, pool, b, c):
        pool.indirect_dma_start(self.xg, bass.IndirectOffsetOnAxis(ap=self.slot[:, c, b:b + 1], axis=0), self.xres[:, b, :], None,
                                bounds_check=E * CAP - 1, oob_is_err=False).then_inc(self.sent, 16)


class AttentionInputs:

    LOADS = 16 * 8

    def __init__(self, nc, ctx):
        def sb(name, shape, dt=F32):
            return ctx.enter_context(nc.sbuf_tensor("x_" + name, shape, dt))

        self.wq = sb("wq", [128, KC, INNERX])
        self.wk = sb("wk", [128, KC, INNERX])
        self.wv = sb("wv", [128, KC, INNERX])
        self.wr = sb("wr", [128, KC, E])
        self.br = sb("br", [T, E])
        self.temp = sb("temp", [128, H])
        self.mask_u8 = sb("mask_u8", [B, S2], U8)
        self.pick = sb("pick", [128, B, T], BF16)
        self.ctx0 = sb("ctx_sb0", [128, KC, S2])
        self.mask_bias = sb("mask_bias", [128, S2], BF16)
        self.v = sb("v", [SC, NSC, H, DH + 1])
        self.kT = sb("kT", [128, PAIRS, S2])
        self.k0_done, self.k0_copied = [ctx.enter_context(nc.semaphore(f"x_k0_{name}")) for name in ("done", "copied")]
        self.v_done, self.v_copied = [ctx.enter_context(nc.semaphore(f"x_v_{name}")) for name in ("done", "copied")]
        self.prepared = ctx.enter_context(nc.semaphore("x_prepared"))
        self.wq_done = ctx.enter_context(nc.semaphore("x_wq_done"))
        self.loaded = ctx.enter_context(nc.semaphore("x_att_loaded"))
        self.ctx_loaded = [ctx.enter_context(nc.semaphore(f"x_ctx_loaded{i}")) for i in range(2)]

    def prepare(self, dve, routing):
        dve.memset(self.v[:, :, :, DH:DH + 1], 1.0)
        dve.memset(self.mask_bias[:], 0.0).then_inc(self.prepared, 1)
        dve.wait_ge(self.prepared, 1)
        dve.wait_ge(self.loaded, self.LOADS)
        dve.tensor_scalar(self.mask_bias[0:B, :], self.mask_u8[:], 1.0, 1e30, ALU.subtract, ALU.mult)
        for k in range(KC):
            w = self.wq[:, k, :].rearrange("p (h d) -> p h d", h=H)
            last = dve.tensor_tensor(w, w, self.temp[:].unsqueeze(2).to_broadcast([128, H, DH]), ALU.mult)
        last.then_inc(self.wq_done, 1)
        routing.dve_tables(dve)

    def first_keys_values(self, pe, bank, p):
        if p > 0:
            pe.wait_ge(self.k0_copied, p)
        for k in range(KC):
            mm = pe.matmul(bank[:, 0, 0:S2], self.wk[:, k, p * 128:(p + 1) * 128], self.ctx0[:, k, :],
                           start=(k == 0), stop=(k == KC - 1))
        mm.then_inc(self.k0_done, 1)
        if p < V_AHEAD:
            if p > 0:
                pe.wait_ge(self.v_copied, p)
            for c in range(NSC):
                for k in range(KC):
                    mm = pe.matmul(bank[0:SC, 1, c * 128:(c + 1) * 128], self.ctx0[:, k, c * SC:(c + 1) * SC],
                                   self.wv[:, k, p * 128:(p + 1) * 128], start=(k == 0), stop=(k == KC - 1))
            mm.then_inc(self.v_done, 1)

    def copy_first_keys_values(self, act, bank, p):
        act.wait_ge(self.k0_done, p + 1)
        act.activation(self.kT[:, p, :], bank[:, 0, 0:S2], ACT.Copy).then_inc(self.k0_copied, 1)
        if p < V_AHEAD:
            act.wait_ge(self.v_done, p + 1)
            act.activation(self.v[:, :, 2 * p:2 * p + 2, 0:DH],
                           bank[0:SC, 1, 0:NSC * 128].rearrange("p (c h d) -> p c h d", c=NSC, h=2),
                           ACT.Copy).then_inc(self.v_copied, 1)

    def load(self, sp, ins):
        def rows(a):
            return a.rearrange("(k p) e -> p k e", p=128)

        sp.dma_start(self.mask_u8[:], ins["mask"]).then_inc(self.loaded, 16)
        sp.dma_start(self.wk[:], rows(ins["Wk"])).then_inc(self.loaded, 16)
        sp.dma_start(self.wq[:], rows(ins["Wq"])).then_inc(self.loaded, 16)
        sp.dma_start(self.temp[:], ins["inv_temp"].rearrange("(a h) -> a h", a=1).to_broadcast([128, H])).then_inc(self.loaded, 16)
        sp.dma_start(self.wv[:], rows(ins["Wv"])).then_inc(self.loaded, 16)
        sp.dma_start(self.pick[:], ins["mask_pick"]).then_inc(self.loaded, 16)
        sp.dma_start(self.wr[:], rows(ins["Wr"])).then_inc(self.loaded, 16)
        sp.dma_start(self.br[:], ins["br"].rearrange("(a h) -> a h", a=1).to_broadcast([T, E])).then_inc(self.loaded, 16)
        sp.dma_start(self.ctx0[:], ins["ctxT"].rearrange("b (k p) s -> b p k s", p=128)[0]).then_inc(self.ctx_loaded[0], 16)


def state_space_phase(nc, xres, ident_sb, att, routing, ins, xT, x, W_inT, Kx, Kz, W_xprojT, W_dtT, b_dt, A_log, D, W_outT, rows_sel, ident, fin, xg):
    ctx = ExitStack()
    with ctx:
        def sb(name, shape, dt=F32):
            return ctx.enter_context(nc.sbuf_tensor("m_" + name, shape, dt))

        def ps(name, shape, dt=F32):
            return ctx.enter_context(nc.psum_tensor("m_" + name, shape, dt))

        def sem(name):
            return ctx.enter_context(nc.semaphore("m_" + name))

        w_in = sb("w_in", [128, KC, 2 * INNER])
        w_xp = sb("w_xp", [INNER, RANK + 2 * NSTATE])
        w_rep = sb("w_rep", [INNER, BC_ROWS])
        w_dt = sb("w_dt", [DT_AT + RANK, INNER])
        w_out = sb("w_out", [INNER, 2, C])
        taps = sb("taps", [INNER, 2, TAPS])
        bdt = sb("bdt", [INNER, 1])
        skip = sb("skip", [INNER, 1])
        dskip = sb("dskip", [INNER, INNER])
        alog = sb("alog", [INNER, NSTATE])
        aneg = sb("aneg", [INNER, NSTATE])
        atmp = sb("atmp", [INNER, 2, NSTATE])
        sel = sb("sel", [BC_ROWS, 2 * NSTATE, 128], BF16)
        bc_sign = sb("bc_sign", [BC_ROWS, 1])
        blank = sb("blank", [128, BLANK_ROWS, CX])
        xt = [sb(f"xt{i}", [128, KC, GT]) for i in range(2)]
        pad = sb("pad", [INNER, 2, GB, T + 2])
        conv = sb("conv", [INNER, 2, GT])
        xz = [sb(f"xz{i}", [INNER, 2, GT]) for i in range(2)]
        dt_sb = sb("dt_sb", [DT_AT + RANK, GT])
        bc = sb("bc", [BC_ROWS, GT])
        bc_rest = sb("bc_rest", [BC_ROWS, GT])
        bc_parts = [sb(f"bc_parts{i}", [BC_ROWS, GT], BF16) for i in range(2)]
        dl = sb("dl", [INNER, 4, GT])
        decay = [sb(f"decay{i}", [INNER, NSTATE, GT]) for i in range(2)]
        drive = sb("drive", [INNER, NSTATE, GT])
        y = sb("y", [INNER, GT])
        stats = sb("stats", [T, GB, 6])
        summed = sb("summed", [T, GB, C])
        mv = sb("mv", [T, GB, 2])
        veps = sb("veps", [T, GB])
        rstd = sb("rstd", [T, GB])
        neghalf = sb("neghalf", [T, GB])

        h_ps = ps("h_ps", [128, 2, 512])
        row_ps = ps("row_ps", [128, ROW_BANKS, 512])
        y_ps = ps("y_ps", [128, 512])
        o_ps = ps("o_ps", [T, 2, 512])

        loaded = sem("weights_loaded")
        x_loaded = [sem(f"x_loaded{i}") for i in range(2)]
        ready, a_step, half_done, set_done = sem("setup_ready"), sem("a_step"), sem("half_done"), sem("set_done")
        blank_done, cleared = sem("blank_done"), sem("cleared")
        h_done, pad_done, taps_done, conv_done = sem("h_done"), sem("pad_done"), sem("taps_done"), sem("conv_done")
        xz_done, proj_done, bc_done, dt_done = sem("xz_done"), sem("proj_done"), sem("bc_done"), sem("dt_done")
        part_done, rest_done, split_done = sem("part_done"), sem("rest_done"), sem("split_done")
        draw_done, dcap_done, exp_done, log_done = sem("draw_done"), sem("dcap_done"), sem("exp_done"), sem("log_done")
        um_done, dfix_done, dsum_done, delta_done = sem("um_done"), sem("dfix_done"), sem("dsum_done"), sem("delta_done")
        decay_done, row_done, row_used = sem("decay_done"), sem("row_done"), sem("row_used")
        clip_done, drive_done, starts_done, scan_done = sem("clip_done"), sem("drive_done"), sem("starts_done"), sem("scan_done")
        ysum_done, y_done, out_done, res_done = sem("ysum_done"), sem("y_done"), sem("out_done"), sem("res_done")
        stats_done, mv_done, veps_done = sem("stats_done"), sem("mv_done"), sem("veps_done")
        rstd_done, norm_done = sem("rstd_done"), sem("norm_done")

        LOADS = 16 * 11
        NR = 2 * NSTATE

        def run(eng, project, step, finish):
            project((0, 0, 0))
            step((0, 0, 0), (1, 0, 1))
            with eng.Fori(0, GROUPS // 2 - 1) as i:
                step((2 * i + 1, i, 1), (2 * i + 2, i + 1, 0))
                step((2 * i + 2, i + 1, 0), (2 * i + 3, i + 1, 1))
            step((GROUPS - 1, GROUPS // 2 - 1, 1), None)
            finish((GROUPS - 1, GROUPS // 2 - 1, 1))

        def is_first(k, below=1):
            return isinstance(k, int) and k < below

        block = ctx.enter_context(nc.Block())

        @block.sync
        def _(sp):
            def load(k, q):
                xt_src = xT.rearrange("(k p) n -> p k n", p=128)
                x_src = x.rearrange("b t c -> t b c")
                if isinstance(k, int):
                    sp.dma_start(xt[q][:], xt_src[:, :, k * GT:(k + 1) * GT]).then_inc(x_loaded[q], 16)
                    sp.dma_start(xres[:, k * GB:(k + 1) * GB, 0:C], x_src[:, k * GB:(k + 1) * GB, :]).then_inc(x_loaded[q], 16)
                else:
                    sp.dma_start(xt[q][:], xt_src[:, :, bass.ds(k * GT, GT)]).then_inc(x_loaded[q], 16)
                    sp.dma_start(xres[:, bass.ds(k * GB, GB), 0:C], x_src[:, bass.ds(k * GB, GB), :]).then_inc(x_loaded[q], 16)

            sp.dma_start(w_in[:], W_inT.rearrange("(k p) e -> p k e", p=128)).then_inc(loaded, 16)
            load(0, 0)
            sp.dma_start(taps[:, 0, :], Kx.rearrange("c a k -> c (a k)")).then_inc(loaded, 16)
            sp.dma_start(taps[:, 1, :], Kz.rearrange("c a k -> c (a k)")).then_inc(loaded, 16)
            sp.dma_start(w_xp[:], W_xprojT).then_inc(loaded, 16)
            sp.dma_start(w_dt[DT_AT:DT_AT + RANK, :], W_dtT).then_inc(loaded, 16)
            sp.dma_start(bdt[:], b_dt.rearrange("(c a) -> c a", a=1)).then_inc(loaded, 16)
            sp.dma_start(skip[:], D.rearrange("(c a) -> c a", a=1)).then_inc(loaded, 16)
            sp.dma_start(alog[:], A_log).then_inc(loaded, 16)
            sp.dma_start(ident_sb[:], ident).then_inc(loaded, 16)
            sp.dma_start(sel[:], rows_sel).then_inc(loaded, 16)
            sp.dma_start(w_out[:], W_outT.rearrange("(k p) e -> p k e", p=128)).then_inc(loaded, 16)
            load(1, 1)
            sp.wait_ge(blank_done, 2)
            n = 0
            for i in range(E * CAP // (128 * BLANK_ROWS)):
                sp.dma_start(xg.rearrange("(i p r) c -> i p r c", p=128, r=BLANK_ROWS)[i], blank[:]).then_inc(cleared, 16)
                n += 1
            for i in range(2 * N // (128 * BLANK_ROWS)):
                sp.dma_start(fin.rearrange("(i p r) c -> i p r c", p=128, r=BLANK_ROWS)[i], blank[:, :, 0:C]).then_inc(cleared, 16)
                n += 1
            with sp.Fori(0, GROUPS // 2 - 1) as i:
                for q in range(2):
                    sp.wait_ge(loaded, LOADS)
                    sp.wait_ge(h_done, 2 * i + q + 1)
                    load(2 * i + q + 2, q)
            att.load(sp, ins)
            sp.wait_ge(cleared, 16 * n)

        @block.tensor
        def _(pe):
            def h_product(k, half_k, q):
                pe.wait_ge(x_loaded[q], 32 * (half_k + 1))
                if not is_first(k):
                    pe.wait_ge(pad_done, 2 * k)
                    pe.wait_ge(dcap_done, k)
                for half in range(2):
                    for c in range(KC):
                        mm = pe.matmul(h_ps[:, half, 0:GT], w_in[:, c, half * INNER:(half + 1) * INNER], xt[q][:, c, :],
                                       start=(c == 0), stop=(c == KC - 1))
                mm.then_inc(h_done, 1)

            def low_rank(k, q):
                pe.wait_ge(xz_done, 2 * k + 1)
                if not is_first(k, 2):
                    pe.wait_ge(y_done, k - 1)
                pe.matmul(y_ps[0:BC_ROWS, 0:GT], w_rep[:], xz[q][:, 0, :], start=True, stop=True).then_inc(proj_done, 1)

            def raw_delta(k):
                pe.wait_ge(dt_done, k + 1)
                pe.matmul(h_ps[:, 0, 0:GT], w_dt[DT_AT:DT_AT + RANK, :], dt_sb[DT_AT:DT_AT + RANK, :],
                          start=True, stop=True).then_inc(draw_done, 1)

            def row(k, q, r):
                if r >= ROW_BANKS:
                    pe.wait_ge(row_used, k * NR + (r - ROW_BANKS + 1))
                elif not is_first(k):
                    last = max(s for s in range(NR) if s % ROW_BANKS == r)
                    pe.wait_ge(row_used, k * NR - (NR - 1 - last))
                pe.matmul(row_ps[:, r % ROW_BANKS, 0:GT], sel[:, r, :], bc_parts[q][:], start=True, stop=True).then_inc(row_done, 1)

            def out_product(k, q):
                pe.wait_ge(y_done, k + 1)
                if not is_first(k):
                    pe.wait_ge(res_done, k)
                for b in range(GB):
                    at = slice((b % 2) * C, (b % 2 + 1) * C)
                    pe.matmul(o_ps[:, b // 2, at], y[:, b * T:(b + 1) * T], w_out[:, 0, :], start=True, stop=False)
                    mm = pe.matmul(o_ps[:, b // 2, at], xz[q][:, 1, b * T:(b + 1) * T], w_out[:, 1, :], start=False, stop=True)
                mm.then_inc(out_done, 1)

            def project(a):
                k, half_k, q = a
                pe.wait_ge(loaded, LOADS)
                h_product(k, half_k, q)
                pe.wait_ge(ready, 1)
                low_rank(k, q)
                raw_delta(k)

            def step(a, nx):
                k, _, q = a
                pe.wait_ge(split_done, k + 1)
                for r in range(ROW_BANKS):
                    row(k, q, r)
                if nx:
                    h_product(*nx)
                else:
                    pe.wait_ge(att.loaded, att.LOADS)
                    pe.wait_ge(att.ctx_loaded[0], 16)
                    pe.wait_ge(dcap_done, GROUPS)
                    att.first_keys_values(pe, h_ps, 0)
                for r in range(ROW_BANKS, NSTATE):
                    row(k, q, r)
                if not is_first(k):
                    out_product(k - 1, 1 - q)
                for r in range(NSTATE, NSTATE + ROW_BANKS):
                    row(k, q, r)
                if nx:
                    low_rank(nx[0], nx[2])
                    raw_delta(nx[0])
                else:
                    for p in range(1, PAIRS // 2 + 1):
                        att.first_keys_values(pe, h_ps, p)
                if not is_first(k):
                    pe.wait_ge(y_done, k)
                pe.matmul(y_ps[:, 0:GT], dskip[:], xz[q][:, 0, :], start=True, stop=False)
                for s in range(NSTATE):
                    pe.wait_ge(row_used, k * NR + NSTATE + s + 1)
                    if s + ROW_BANKS < NSTATE:
                        row(k, q, NSTATE + s + ROW_BANKS)
                    mm = pe.matmul(y_ps[:, 0:GT], ident_sb[:], drive[:, s, :], start=False, stop=(s == NSTATE - 1))
                mm.then_inc(ysum_done, 1)

            def finish(a):
                out_product(a[0], a[2])
                for p in range(PAIRS // 2 + 1, PAIRS):
                    att.first_keys_values(pe, h_ps, p)

            run(pe, project, step, finish)

        @block.scalar
        def _(act):
            def pad_copy(k):
                act.wait_ge(h_done, k + 1)
                if not is_first(k):
                    act.wait_ge(conv_done, 2 * k)
                for half in range(2):
                    act.activation(pad[:, half, :, 1:T + 1], h_ps[:, half, 0:GT].rearrange("p (b t) -> p b t", b=GB),
                                   ACT.Copy).then_inc(pad_done, 1)

            def silu(k, q):
                if not is_first(k, 2):
                    act.wait_ge(out_done, k - 1)
                for half in range(2):
                    act.wait_ge(conv_done, 2 * k + half + 1)
                    act.activation(xz[q][:, half, :], conv[:, half, :], ACT.Silu).then_inc(xz_done, 1)

            def low_rank(k):
                act.wait_ge(proj_done, k + 1)
                if not is_first(k):
                    act.wait_ge(split_done, k)
                act.activation(bc[:], y_ps[0:BC_ROWS, 0:GT], ACT.Tanh, scale=bc_sign[:, 0:1]).then_inc(bc_done, 1)
                act.activation(dt_sb[DT_AT:DT_AT + RANK, :], y_ps[DT_AT:DT_AT + RANK, 0:GT], ACT.Copy).then_inc(dt_done, 1)

            def soft(k):
                act.wait_ge(dcap_done, k + 1)
                act.activation(dl[:, 1, :], dl[:, 0, :], ACT.Exp).then_inc(exp_done, 1)
                act.wait_ge(exp_done, k + 1)
                act.activation(dl[:, 2, :], dl[:, 1, :], ACT.Ln, bias=1.0).then_inc(log_done, 1)

            def decays(k, q):
                act.wait_ge(delta_done, k + 1)
                if not is_first(k, 2):
                    act.wait_ge(scan_done, k - 1)
                for s in range(NSTATE):
                    last = act.activation(decay[q][:, s, :], dl[:, 0, :], ACT.Exp, scale=aneg[:, s:s + 1])
                last.then_inc(decay_done, 1)

            def y_copy(k):
                act.wait_ge(ysum_done, k + 1)
                if not is_first(k):
                    act.wait_ge(out_done, k)
                act.activation(y[:], y_ps[:, 0:GT], ACT.Copy).then_inc(y_done, 1)

            def project(a):
                k, _, q = a
                act.wait_ge(loaded, LOADS)
                act.activation(atmp[:, 0, :], alog[:], ACT.Abs).then_inc(a_step, 1)
                act.wait_ge(a_step, 1)
                act.activation(atmp[:, 0, :], atmp[:, 0, :], ACT.Exp, scale=-1.0).then_inc(a_step, 1)
                act.wait_ge(a_step, 2)
                act.activation(atmp[:, 0, :], atmp[:, 0, :], ACT.Ln, bias=1.0).then_inc(a_step, 1)
                act.wait_ge(set_done, 1)
                pad_copy(k)
                silu(k, q)
                act.wait_ge(ready, 1)
                low_rank(k)
                soft(k)
                decays(k, q)

            def step(a, nx):
                k, _, q = a
                if not is_first(k):
                    y_copy(k - 1)
                if nx:
                    pad_copy(nx[0])
                    silu(nx[0], nx[2])
                    low_rank(nx[0])
                    soft(nx[0])
                    decays(nx[0], nx[2])
                else:
                    for p in range(PAIRS // 2 + 1):
                        att.copy_first_keys_values(act, h_ps, p)

            def finish(a):
                y_copy(a[0])
                for p in range(PAIRS // 2 + 1, PAIRS):
                    att.copy_first_keys_values(act, h_ps, p)

            run(act, project, step, finish)

        @block.gpsimd
        def _(pool):
            pool.memset(neghalf[:], -0.5).then_inc(half_done, 1)
            pool.wait_ge(half_done, 1)

            def split(k, q):
                mid, low = BC_AT[1], BC_AT[2]
                waits = [(bc_done, k + 1)]
                if not is_first(k, 2):
                    waits.append((row_done, (k - 1) * NR))
                wait_apart(pool, half_done, *waits)
                pool.tensor_copy(bc_parts[q][:], bc[:]).then_inc(part_done, 1)
                pool.wait_ge(part_done, 2 * k + 1)
                pool.tensor_tensor(bc_rest[mid:, :], bc[mid:, :], bc_parts[q][mid:, :], ALU.subtract).then_inc(rest_done, 1)
                wait_apart(pool, half_done, (rest_done, 2 * k + 1))
                pool.tensor_copy(bc_parts[q][mid:, :], bc_rest[mid:, :]).then_inc(part_done, 1)
                pool.wait_ge(part_done, 2 * k + 2)
                pool.tensor_tensor(bc_rest[low:, :], bc_rest[low:, :], bc_parts[q][low:, :], ALU.subtract).then_inc(rest_done, 1)
                wait_apart(pool, half_done, (rest_done, 2 * k + 2))
                pool.tensor_copy(bc_parts[q][low:, :], bc_rest[low:, :]).then_inc(split_done, 1)

            def power(k):
                pool.wait_ge(veps_done, k + 1)
                pool.tensor_tensor(rstd[:], veps[:], neghalf[:], ALU.pow).then_inc(rstd_done, 1)

            def project(a):
                split(a[0], a[2])

            def step(a, nx):
                if not is_first(a[0]):
                    power(a[0] - 1)
                if nx:
                    split(nx[0], nx[2])

            def finish(a):
                routing.pool_tables(pool)
                power(a[0])

            run(pool, project, step, finish)

        @block.vector
        def _(dve):
            def convolve(k):
                for tap in range(TAPS):
                    for half in range(2):
                        src = pad[:, half, :, tap:tap + T]
                        dst = conv[:, half, :].rearrange("p (b t) -> p b t", b=GB)
                        w = taps[:, half, tap:tap + 1]
                        if tap == 0:
                            dve.wait_ge(pad_done, 2 * k + half + 1)
                            if not is_first(k):
                                dve.wait_ge(xz_done, 2 * k + (half - 1))
                            dve.tensor_scalar(dst, src, w, None, ALU.mult).then_inc(taps_done, 1)
                        else:
                            dve.wait_ge(taps_done, k * 4 + (tap - 1) * 2 + half + 1)
                            dve.scalar_tensor_tensor(dst, src, w, dst, ALU.mult, ALU.add).then_inc(
                                taps_done if tap == 1 else conv_done, 1)

            def delta(k, part):
                if part == 0:
                    dve.wait_ge(draw_done, k + 1)
                    if not is_first(k):
                        dve.wait_ge(decay_done, k)
                    dve.tensor_scalar(dl[:, 0, :], h_ps[:, 0, 0:GT], bdt[:, 0:1], SOFTPLUS_CAP, ALU.add, ALU.min).then_inc(dcap_done, 1)
                if part == 1:
                    dve.wait_ge(exp_done, k + 1)
                    dve.tensor_scalar(dl[:, 3, :], dl[:, 1, :], 1.0, -1.0, ALU.add, ALU.add).then_inc(um_done, 1)
                if part == 2:
                    dve.wait_ge(um_done, k + 1)
                    dve.tensor_tensor(dl[:, 3, :], dl[:, 1, :], dl[:, 3, :], ALU.subtract).then_inc(dfix_done, 1)
                if part == 3:
                    dve.wait_ge(dfix_done, k + 1)
                    dve.wait_ge(log_done, k + 1)
                    dve.tensor_tensor(dl[:, 3, :], dl[:, 2, :], dl[:, 3, :], ALU.add).then_inc(dsum_done, 1)
                if part == 4:
                    dve.wait_ge(dsum_done, k + 1)
                    dve.tensor_scalar(dl[:, 0, :], dl[:, 3, :], CLIP_LO, CLIP_HI, ALU.max, ALU.min).then_inc(delta_done, 1)

            def norm(k, part):
                if part == 0:
                    dve.wait_ge(out_done, k + 1)
                    if not is_first(k):
                        dve.wait_ge(norm_done, k)
                    for h in range(2):
                        if isinstance(k, int):
                            xr = xres[:, k * GB + 2 * h:k * GB + 2 * h + 2, 0:C]
                        else:
                            xr = xres[:, bass.ds(k * GB + 2 * h, 2), 0:C]
                        last = dve.tensor_tensor(summed[:, 2 * h:2 * h + 2, :], o_ps[:, h, :].rearrange("p (b c) -> p b c", b=2),
                                                 xr, ALU.add)
                    last.then_inc(res_done, 1)
                if part == 1:
                    dve.wait_ge(res_done, k + 1)
                    for b in range(GB):
                        last = dve.bn_stats(stats[:, b, :], summed[:, b, :])
                    last.then_inc(stats_done, 1)
                if part == 2:
                    wait_apart(dve, ready, (stats_done, k + 1))
                    for b in range(GB):
                        last = dve.bn_aggr(mv[:, b, :], stats[:, b, :])
                    last.then_inc(mv_done, 1)
                if part == 3:
                    dve.wait_ge(mv_done, k + 1)
                    dve.tensor_scalar(veps[:], mv[:, :, 1], LN_EPS, None, ALU.add).then_inc(veps_done, 1)
                if part == 4:
                    dve.wait_ge(rstd_done, k + 1)
                    for b in range(GB):
                        if isinstance(k, int):
                            xr = xres[:, k * GB + b, 0:C]
                        else:
                            xr = xres[:, bass.ds(k * GB + b, 1), 0:C].rearrange("p b c -> p (b c)")
                        last = dve.tensor_scalar(xr, summed[:, b, :], mv[:, b, 0:1], rstd[:, b:b + 1], ALU.subtract, ALU.mult)
                    last.then_inc(norm_done, 1)

            def project(a):
                k, _, q = a
                dve.memset(pad[:], 0.0).then_inc(set_done, 1)
                dve.memset(blank[:], 0.0).then_inc(blank_done, 1)
                dve.memset(xres[:, B, :], 0.0)
                dve.memset(w_rep[:], 0.0)
                dve.memset(bc_sign[:], 1.0).then_inc(set_done, 1)
                dve.wait_ge(blank_done, 1)
                dve.memset(blank[:, :, TOKEN:CX], NOWHERE).then_inc(blank_done, 1)
                dve.wait_ge(set_done, 2)
                dve.wait_ge(loaded, LOADS)
                for at in BC_AT:
                    dve.memset(bc_sign[at:at + NSTATE, :], -1.0)
                    dve.tensor_copy(w_rep[:, at:at + NR], w_xp[:, RANK:])
                dve.tensor_copy(w_rep[:, DT_AT:DT_AT + RANK], w_xp[:, 0:RANK])
                dve.tensor_scalar(dskip[:], ident_sb[:], skip[:, 0:1], None, ALU.mult)
                dve.wait_ge(a_step, 3)
                dve.scalar_tensor_tensor(atmp[:, 1, :], alog[:], 0.0, atmp[:, 0, :], ALU.max, ALU.add).then_inc(set_done, 1)
                dve.wait_ge(set_done, 3)
                dve.tensor_scalar(aneg[:], atmp[:, 1, :], 1e-4, -1.0, ALU.add, ALU.mult).then_inc(ready, 1)
                convolve(k)
                for part in range(5):
                    delta(k, part)

            def step(a, nx):
                k, _, q = a
                for s in range(NSTATE):
                    dve.wait_ge(row_done, k * NR + s + 1)
                    if s == 0 and not is_first(k):
                        dve.wait_ge(ysum_done, k)
                    dve.tensor_tensor(drive[:, s, :], row_ps[:, s % ROW_BANKS, 0:GT], xz[q][:, 0, :], ALU.mult).then_inc(row_used, 1)
                    if s == ROW_BANKS - 1:
                        dve.wait_ge(decay_done, k + 1)
                        dve.tensor_scalar(decay[q][:], decay[q][:], CLIP_LO, CLIP_HI, ALU.max, ALU.min).then_inc(clip_done, 1)
                if nx:
                    convolve(nx[0])
                if not is_first(k):
                    norm(k - 1, 0)
                dve.wait_ge(clip_done, k + 1)
                dve.wait_ge(row_used, k * NR + NSTATE)
                dve.scalar_tensor_tensor(drive[:], decay[q][:], 1.0, drive[:], ALU.subtract, ALU.mult).then_inc(drive_done, 1)
                if not is_first(k):
                    norm(k - 1, 1)
                dve.wait_ge(drive_done, k + 1)
                dve.memset(decay[q][:].rearrange("p s (b t) -> p s b t", b=GB)[:, :, :, 0:1], 0.0).then_inc(starts_done, 1)
                if not is_first(k):
                    norm(k - 1, 2)
                if nx:
                    delta(nx[0], 0)
                dve.wait_ge(starts_done, k + 1)
                dve.tensor_tensor_scan(drive[:].rearrange("p s t -> p (s t)"), decay[q][:].rearrange("p s t -> p (s t)"),
                                       drive[:].rearrange("p s t -> p (s t)"), 0.0, ALU.mult, ALU.add).then_inc(scan_done, 1)
                if not is_first(k):
                    norm(k - 1, 3)
                if nx:
                    delta(nx[0], 1)
                    delta(nx[0], 2)
                for s in range(NSTATE):
                    dve.wait_ge(row_done, k * NR + NSTATE + s + 1)
                    if s == 0:
                        dve.wait_ge(scan_done, k + 1)
                    dve.tensor_tensor(drive[:, s, :], row_ps[:, (NSTATE + s) % ROW_BANKS, 0:GT], drive[:, s, :], ALU.mult).then_inc(row_used, 1)
                    if s == 4 and nx:
                        delta(nx[0], 3)
                    if s == 5 and nx:
                        delta(nx[0], 4)
                if not is_first(k):
                    norm(k - 1, 4)

            def finish(a):
                att.prepare(dve, routing)
                for part in range(5):
                    norm(a[0], part)
                dve.wait_ge(norm_done, GROUPS)

            run(dve, project, step, finish)


def attention_phase(nc, xres, logits, ident_sb, att, ctxT, Wo, routing, lower):
    ctx = ExitStack()
    with ctx:
        def sb(name, shape, dt=F32):
            return ctx.enter_context(nc.sbuf_tensor("x_" + name, shape, dt))

        def ps(name, shape, dt=F32):
            return ctx.enter_context(nc.psum_tensor("x_" + name, shape, dt))

        def sem(name):
            return ctx.enter_context(nc.semaphore("x_" + name))

        wq, wk, wv, wr, br_sb, pick = att.wq, att.wk, att.wv, att.wr, att.br, att.pick
        wo = sb("wo", [128, PAIRS, C])
        ctx_sb = [att.ctx0, sb("ctx_sb1", [128, KC, S2])]
        wo_loaded = sem("wo_loaded")
        loaded, ctx_loaded, LOADS = att.loaded, att.ctx_loaded, att.LOADS
        mask_bias, v, wq_done = att.mask_bias, att.v, att.wq_done
        xT = sb("xT_att", [128, KC, T])
        qT = sb("qT", [128, PAIRS, T])
        kT = att.kT
        work = sb("work", [T, 2, S2])
        top = sb("top", [T, 4, 2, TOPK])
        s_sb = sb("s_sb", [T, 8, S2])
        prob = sb("prob", [T, 4, S2])
        nmax = sb("nmax", [T, 4])
        full_sum = sb("full_sum", [T, H])
        kept = sb("kept", [T, 2, S2])
        total = sb("total", [T, H])
        rtotal = sb("rtotal", [T, H])
        pT = sb("pT", [SC, 2, NSC, T])
        o = sb("o", [T, H, DH])
        oT = sb("oT", [128, PAIRS, T])
        out_sb = sb("out_sb", [T, C])
        lg_sb = sb("lg_sb", [T, E])
        summed = sb("summed_att", [T, C])
        stats = sb("stats_att", [T, 6])
        mv = sb("mv_att", [T, 2])
        veps = sb("veps_att", [T, 1])
        rstd = sb("rstd_att", [T, 1])
        neghalf = sb("neghalf_att", [T, 1])
        x_stage = sb("x_stage", [T, C])
        x2 = sb("x2", [T, C])
        x2T = sb("x2T", [128, KC, T])

        s_ps = ps("s_ps", [T, 2, 512])
        pT_ps = ps("pT_ps", [SC, 2, 512])
        o_ps = ps("o_ps", [T, 2, 512])
        w_ps = ps("w_ps", [128, 2, 512])

        half_done = sem("att_half_done")
        xT_done, xT_copied = sem("xT_done"), sem("xT_copied")
        kq_done, kq_copied = sem("kq_done"), sem("kq_copied")
        v_done, v_copied = att.v_done, att.v_copied
        s_done, s_copied, max_done, rep_done = sem("s_done"), sem("s_copied"), sem("max_done"), sem("rep_done")
        nmax_done, exp_done, kept_done, p_done = sem("nmax_done"), sem("exp_done"), sem("kept_done"), sem("p_done")
        pT_done, pT_copied, pv_done = sem("pT_done"), sem("pT_copied"), sem("pv_done")
        total_done, rtotal_done, o_done = sem("total_done"), sem("rtotal_done"), sem("o_done")
        oT_done, oT_copied, wo_done, out_copied = sem("oT_done"), sem("oT_copied"), sem("wo_done"), sem("out_copied")
        sum_done, stats_done, mv_done = sem("sum_done"), sem("stats_done_att"), sem("mv_done_att")
        veps_done, rstd_done, x2_done = sem("veps_done_att"), sem("rstd_done_att"), sem("x2_done")
        x2T_done, x2T_copied = sem("x2T_done"), sem("x2T_copied")
        stage_done, x2_kept = sem("stage_done"), sem("x2_kept")
        lg_done, lg_copied, lg_added = sem("lg_done"), sem("lg_copied"), sem("lg_added")

        scale = float(DH) ** -0.5

        def run(eng, batch, lead_in, lead_out):
            lead_in((0, 0, 0))
            batch((0, 0, 0), (1, 0, 1), False, True)
            with eng.Fori(0, (B - 1 - LAST) // 2) as i:
                batch((2 * i + 1, i, 1), (2 * i + 2, i + 1, 0), True, True)
                batch((2 * i + 2, i + 1, 0), (2 * i + 3, i + 1, 1), True, True)
            for n in range(B - LAST, B):
                batch((n, n // 2, n % 2), (n + 1, (n + 1) // 2, (n + 1) % 2), True, n < B - 1)
            lead_out((B - 1, B // 2 - 1, 1))

        def is_routed(b):
            return isinstance(b[0], int) and b[0] == B - LAST

        block = ctx.enter_context(nc.Block())

        @block.sync
        def _(sp):
            src = ctxT.rearrange("b (k p) s -> b p k s", p=128)
            sp.dma_start(ctx_sb[1][:], src[1]).then_inc(ctx_loaded[1], 16)
            sp.dma_start(wo[:], Wo.rearrange("(k p) e -> p k e", p=128)).then_inc(wo_loaded, 16)
            sp.dma_start(routing.lower[:], lower).then_inc(routing.lower_loaded, 16)
            with sp.Fori(0, B // 2 - 1) as i:
                for p in range(2):
                    sp.wait_ge(loaded, LOADS)
                    sp.wait_ge(v_done, (2 * i + p) * PAIRS + PAIRS)
                    sp.dma_start(ctx_sb[p][:], src[bass.ds(2 * i + p + 2, 1)].rearrange("b p k s -> p (b k) s")).then_inc(
                        ctx_loaded[p], 16)

        @block.tensor
        def _(pe):
            def x_transpose(b):
                n, _, _ = b
                pe.wait_ge(stage_done, n + 1)
                for k in range(KC):
                    mm = pe.transpose(w_ps[:, 1, k * T:(k + 1) * T], x_stage[:, k * 128:(k + 1) * 128], ident_sb[0:T, 0:T])
                mm.then_inc(xT_done, 1)

            def keys_queries(b, p):
                n, half, par = b
                if p == 0:
                    pe.wait_ge(ctx_loaded[par], 16 * (half + 1))
                    pe.wait_ge(xT_copied, n + 1)
                pe.wait_ge(kq_copied, n * PAIRS + p)
                for k in range(KC):
                    pe.matmul(w_ps[:, 0, 0:S2], wk[:, k, p * 128:(p + 1) * 128], ctx_sb[par][:, k, :],
                              start=(k == 0), stop=(k == KC - 1))
                for k in range(KC):
                    mm = pe.matmul(w_ps[:, 0, 384:384 + T], wq[:, k, p * 128:(p + 1) * 128], xT[:, k, :],
                                   start=(k == 0), stop=(k == KC - 1))
                mm.then_inc(kq_done, 1)

            def values(b, p):
                n, half, par = b
                pe.wait_ge(v_copied, n * PAIRS + p)
                for c in range(NSC):
                    for k in range(KC):
                        mm = pe.matmul(w_ps[0:SC, 1, c * 128:(c + 1) * 128], ctx_sb[par][:, k, c * SC:(c + 1) * SC],
                                       wv[:, k, p * 128:(p + 1) * 128], start=(k == 0), stop=(k == KC - 1))
                mm.then_inc(v_done, 1)

            def scores(b, p):
                n, _, _ = b
                for hh in range(2):
                    h = 2 * p + hh
                    at = slice(64 * hh, 64 * hh + 64)
                    pe.wait_ge(loaded, LOADS)
                    if not (isinstance(n, int) and n == 0 and h < 2):
                        pe.wait_ge(s_copied, n * H + (h - 1))
                    pe.matmul(s_ps[:, hh, 0:S2], pick[:, bass.ds(n, 1), :].rearrange("p b t -> p (b t)"), mask_bias[:],
                              start=True, stop=False)
                    if hh == 0:
                        pe.wait_ge(kq_copied, n * PAIRS + p + 1)
                    pe.matmul(s_ps[:, hh, 0:S2], qT[at, p, :], kT[at, p, :], start=False, stop=True).then_inc(s_done, 1)

            def prob_transpose(b, p, hh):
                n, _, _ = b
                h = 2 * p + hh
                pe.wait_ge(p_done, n * H + h + 1)
                if not (isinstance(n, int) and n == 0 and h < 2):
                    pe.wait_ge(pT_copied, n * H + (h - 1))
                for c in range(NSC):
                    mm = pe.transpose(pT_ps[:, hh, c * T:(c + 1) * T], prob[:, h % 4, c * SC:(c + 1) * SC], ident_sb[0:T, 0:T])
                mm.then_inc(pT_done, 1)

            def prob_values(b, p, hh):
                n, _, _ = b
                h = 2 * p + hh
                pe.wait_ge(pT_copied, n * H + h + 1)
                if hh == 0:
                    pe.wait_ge(v_copied, n * PAIRS + p + 1)
                if h % 4 == 0 and not (isinstance(n, int) and n == 0 and h < 8):
                    pe.wait_ge(o_done, n * 4 + (h // 4 - 1))
                for c in range(NSC):
                    at = slice(h % 4 * (DH + 1), (h % 4 + 1) * (DH + 1))
                    mm = pe.matmul(o_ps[:, h % 8 // 4, at], pT[:, hh, c, :], v[:, c, h, :],
                                   start=(c == 0), stop=(c == NSC - 1))
                if hh == 1:
                    mm.then_inc(pv_done, 1)

            def out_transpose(b, half):
                n, _, _ = b
                pe.wait_ge(o_done, n * 4 + 2 * half + 2)
                for q in range(4):
                    h = 8 * half + 2 * q
                    mm = pe.transpose(w_ps[:, 1, q * T:(q + 1) * T], o[:, h:h + 2, :].rearrange("p h d -> p (h d)"),
                                      ident_sb[0:T, 0:T])
                mm.then_inc(oT_done, 1)

            def out_project(b):
                n, _, _ = b
                pe.wait_ge(oT_copied, n * 2 + 2)
                pe.wait_ge(wo_loaded, 16)
                for p in range(PAIRS):
                    mm = pe.matmul(w_ps[0:T, 1, 0:C], oT[:, p, :], wo[:, p, :], start=(p == 0), stop=(p == PAIRS - 1))
                mm.then_inc(wo_done, 1)

            def x2_transpose(b):
                n, _, _ = b
                pe.wait_ge(x2_done, n + 1)
                for k in range(KC):
                    mm = pe.transpose(w_ps[:, 1, k * T:(k + 1) * T], x2[:, k * 128:(k + 1) * 128], ident_sb[0:T, 0:T])
                mm.then_inc(x2T_done, 1)

            def router(b):
                n, _, _ = b
                pe.wait_ge(x2T_copied, n + 1)
                for k in range(KC):
                    mm = pe.matmul(w_ps[0:T, 1, 0:E], x2T[:, k, :], wr[:, k, :], start=(k == 0), stop=(k == KC - 1))
                mm.then_inc(lg_done, 1)

            def before(b):
                return (b[0] - 1, None, None)

            def lead_in(b):
                pe.wait_ge(loaded, LOADS)
                x_transpose(b)
                pe.wait_ge(wq_done, 1)
                pe.wait_ge(xT_copied, 1)
                for p in range(PAIRS):
                    for k in range(KC):
                        mm = pe.matmul(w_ps[:, p // 4, (p % 4) * T:(p % 4 + 1) * T], wq[:, k, p * 128:(p + 1) * 128], xT[:, k, :],
                                       start=(k == 0), stop=(k == KC - 1))
                    mm.then_inc(kq_done, 1)
                pe.wait_ge(kq_copied, PAIRS)
                scores(b, 0)
                x_transpose((1, 0, 1))
                scores(b, 1)

            def batch(b, nb, has_prev, has_next):
                for j in range(PAIRS):
                    prev, p = (b, j - 1) if j else (before(b), PAIRS - 1)
                    prev2, p2 = (b, j - 2) if j > 1 else (before(b), PAIRS - 2 + j)
                    if j < PAIRS - 2:
                        scores(b, j + 2)
                    elif has_next:
                        scores(nb, j - (PAIRS - 2))
                    if j > 1 or has_prev:
                        prob_values(prev2, p2, 1)
                    if j == 2 and has_prev:
                        pe.wait_ge(v_copied, b[0] * PAIRS + PAIRS)
                        out_transpose(before(b), 1)
                    if has_next:
                        keys_queries(nb, j)
                    if j == 2 and has_prev:
                        out_project(before(b))
                    if j == 7 and has_prev:
                        if has_next:
                            pe.wait_ge(v_copied, b[0] * PAIRS + PAIRS + 5)
                        router(before(b))
                    if j or has_prev:
                        prob_transpose(prev, p, 0)
                    if j < 2:
                        if j == 0:
                            pe.wait_ge(xT_copied, b[0] + 2)
                        elif has_prev:
                            pe.wait_ge(oT_copied, b[0] * 2 - 1)
                        values(b, PAIRS - 2 + j)
                    elif has_next:
                        if j == 2 and has_prev:
                            pe.wait_ge(out_copied, b[0])
                        if j == 4 and is_routed(b):
                            pe.wait_ge(routing.count_read, 1)
                        if j == 6 and has_prev:
                            pe.wait_ge(x2T_copied, b[0])
                        if j == 7 and has_prev:
                            pe.wait_ge(lg_copied, b[0])
                        values(nb, j - 2)
                    if j or has_prev:
                        prob_transpose(prev, p, 1)
                    if j or has_prev:
                        prob_values(prev, p, 0)
                    copied = b[0] * PAIRS + PAIRS - 1 + j
                    if j == 0 and has_prev:
                        pe.wait_ge(v_copied, copied)
                        out_transpose(before(b), 0)
                    if j == 3 and is_routed(b):
                        pe.wait_ge(v_copied, copied)
                        routing.counts(pe, 0, w_ps[:, 1, :])
                    if j == 5 and has_prev:
                        if has_next:
                            pe.wait_ge(v_copied, copied)
                        else:
                            pe.wait_ge(out_copied, b[0])
                        x2_transpose(before(b))
                    if j == PAIRS - 1 and has_next:
                        pe.wait_ge(v_copied, copied)
                        x_transpose((nb[0] + 1, None, None))

            def lead_out(b):
                prob_values(b, PAIRS - 2, 1)
                prob_transpose(b, PAIRS - 1, 0)
                prob_transpose(b, PAIRS - 1, 1)
                prob_values(b, PAIRS - 1, 0)
                prob_values(b, PAIRS - 1, 1)
                pe.wait_ge(lg_copied, b[0])
                out_transpose(b, 0)
                pe.wait_ge(oT_copied, 2 * b[0] + 1)
                out_transpose(b, 1)
                out_project(b)
                pe.wait_ge(out_copied, b[0] + 1)
                x2_transpose(b)
                router(b)

            run(pe, batch, lead_in, lead_out)

        @block.scalar
        def _(act):
            def x_copy(n):
                act.wait_ge(xT_done, n + 1)
                act.wait_ge(kq_done, n * PAIRS)
                act.activation(xT[:].rearrange("p k t -> p (k t)"), w_ps[:, 1, 0:KC * T], ACT.Copy).then_inc(xT_copied, 1)

            def keys_queries(b, p):
                n, _, _ = b
                act.wait_ge(kq_done, n * PAIRS + p + 1)
                if not (isinstance(n, int) and n == 0):
                    act.wait_ge(s_done, (n - 1) * H + 2 * p + 2)
                act.activation(kT[:, p, :], w_ps[:, 0, 0:S2], ACT.Copy)
                act.activation(qT[:, p, :], w_ps[:, 0, 384:384 + T], ACT.Copy).then_inc(kq_copied, 1)

            def values(b, p):
                n, _, _ = b
                act.wait_ge(v_done, n * PAIRS + p + 1)
                if not (isinstance(n, int) and n == 0):
                    act.wait_ge(pv_done, (n - 1) * PAIRS + p + 1)
                act.activation(v[:, :, 2 * p:2 * p + 2, 0:DH],
                               w_ps[0:SC, 1, 0:NSC * 128].rearrange("p (c h d) -> p c h d", c=NSC, h=2),
                               ACT.Copy).then_inc(v_copied, 1)

            def prob_copy(b, p, hh):
                n, _, _ = b
                h = 2 * p + hh
                act.wait_ge(pT_done, n * H + h + 1)
                if not (isinstance(n, int) and n == 0 and p == 0):
                    act.wait_ge(pv_done, n * PAIRS + p)
                act.activation(pT[:, hh, :, :].rearrange("p c t -> p (c t)"), pT_ps[:, hh, 0:NSC * T], ACT.Copy).then_inc(pT_copied, 1)

            def score_copy(b, p, hh):
                n, _, _ = b
                h = 2 * p + hh
                act.wait_ge(s_done, n * H + h + 1)
                if not (isinstance(n, int) and n == 0 and h < 8):
                    act.wait_ge(kept_done, n * H + (h - 7))
                act.activation(s_sb[:, h % 8, :], s_ps[:, hh, 0:S2], ACT.Copy).then_inc(s_copied, 1)

            def exps(b, p, hh):
                n, _, _ = b
                h = 2 * p + hh
                act.wait_ge(nmax_done, n * H + h + 1)
                if not (isinstance(n, int) and n == 0 and h < 4):
                    act.wait_ge(pT_done, n * H + (h - 3))
                act.activation(prob[:, h % 4, :], s_sb[:, h % 8, :], ACT.Exp, bias=nmax[:, h % 4:h % 4 + 1], scale=scale,
                               accum_out=full_sum[:, h:h + 1]).then_inc(exp_done, 1)

            def out_copy(b, half):
                n, _, _ = b
                act.wait_ge(oT_done, n * 2 + half + 1)
                act.activation(oT[:, 4 * half:4 * half + 4, :].rearrange("p q t -> p (q t)"), w_ps[:, 1, 0:4 * T],
                               ACT.Copy).then_inc(oT_copied, 1)

            def project_copy(b):
                n, _, _ = b
                act.wait_ge(wo_done, n + 1)
                act.activation(out_sb[:], w_ps[0:T, 1, 0:C], ACT.Copy).then_inc(out_copied, 1)

            def logit_copy(b):
                n, _, _ = b
                act.wait_ge(lg_done, n + 1)
                act.activation(lg_sb[:], w_ps[0:T, 1, 0:E], ACT.Copy).then_inc(lg_copied, 1)

            def x2_copy(b):
                n, _, _ = b
                act.wait_ge(x2T_done, n + 1)
                act.activation(x2T[:].rearrange("p k t -> p (k t)"), w_ps[:, 1, 0:KC * T], ACT.Copy).then_inc(x2T_copied, 1)

            def before(b):
                return (b[0] - 1, None, None)

            def lead_in(b):
                x_copy(0)
                for q in range(2):
                    act.wait_ge(kq_done, 4 * q + 4)
                    act.activation(qT[:, 4 * q:4 * q + 4, :].rearrange("p q t -> p (q t)"), w_ps[:, q, 0:4 * T], ACT.Copy).then_inc(
                        kq_copied, 4)
                score_copy(b, 0, 0)
                score_copy(b, 0, 1)
                x_copy(1)
                score_copy(b, 1, 0)
                score_copy(b, 1, 1)

            def batch(b, nb, has_prev, has_next):
                for j in range(PAIRS):
                    prev, p = (b, j - 1) if j else (before(b), PAIRS - 1)
                    exps(b, j, 0)
                    exps(b, j, 1)
                    if j < PAIRS - 2:
                        score_copy(b, j + 2, 0)
                    elif has_next:
                        score_copy(nb, j - (PAIRS - 2), 0)
                    if j == 2 and has_prev:
                        out_copy(before(b), 1)
                    if has_next:
                        keys_queries(nb, j)
                    if j == 2 and has_prev:
                        project_copy(before(b))
                    if j == 7 and has_prev:
                        logit_copy(before(b))
                    if j or has_prev:
                        prob_copy(prev, p, 0)
                    if j < PAIRS - 2:
                        score_copy(b, j + 2, 1)
                    elif has_next:
                        score_copy(nb, j - (PAIRS - 2), 1)
                    if j < 2:
                        values(b, PAIRS - 2 + j)
                    elif has_next:
                        values(nb, j - 2)
                    if j or has_prev:
                        prob_copy(prev, p, 1)
                    if j == 2 and is_routed(b):
                        routing.exps(act, 0)
                    if j == 0 and has_prev:
                        out_copy(before(b), 0)
                    if j == 5 and has_prev:
                        x2_copy(before(b))
                    if j == PAIRS - 1 and has_next:
                        x_copy(nb[0] + 1)

            def lead_out(b):
                prob_copy(b, PAIRS - 1, 0)
                prob_copy(b, PAIRS - 1, 1)
                out_copy(b, 0)
                out_copy(b, 1)
                project_copy(b)
                x2_copy(b)
                logit_copy(b)

            run(act, batch, lead_in, lead_out)

        @block.gpsimd
        def _(pool):
            pool.memset(neghalf[:], -0.5).then_inc(half_done, 1)
            pool.wait_ge(half_done, 1)

            def stage(n):
                pool.wait_ge(half_done, 1)
                pool.wait_ge(xT_done, n)
                pool.tensor_copy(x_stage[:], xres[:, bass.ds(n, 1), 0:C].rearrange("p b c -> p (b c)")).then_inc(stage_done, 1)

            def lead_in(b):
                stage(0)
                stage(1)

            def keep(n):
                pool.wait_ge(half_done, 1)
                pool.wait_ge(x2_done, n + 1)
                pool.tensor_copy(xres[:, bass.ds(n, 1), 0:C].rearrange("p b c -> p (b c)"), x2[:]).then_inc(x2_kept, 1)

            def norm(n):
                pool.wait_ge(veps_done, n + 1)
                pool.tensor_tensor(rstd[:], veps[:], neghalf[:], ALU.pow).then_inc(rstd_done, 1)

            def keep_mask(b, p, hh):
                n, _, _ = b
                waits = [(max_done, n * 64 + p * 8 + 6 + hh + 1)]
                if not (isinstance(n, int) and n == 0 and p == 0):
                    waits.append((p_done, n * H + (2 * p + hh - 1)))
                wait_apart(pool, half_done, *waits)
                pool.tensor_scalar(kept[:, hh, :], s_sb[:, (2 * p + hh) % 8, :], top[:, p % 4, hh, TOPK - 1:TOPK], None,
                                   ALU.is_ge).then_inc(kept_done, 1)

            def keep_probs(b, p, hh):
                n, _, _ = b
                h = 2 * p + hh
                pool.wait_ge(kept_done, n * H + h + 1)
                pool.wait_ge(exp_done, n * H + h + 1)
                pool.tensor_tensor(prob[:, h % 4, :], prob[:, h % 4, :], kept[:, hh, :], ALU.mult).then_inc(p_done, 1)

            def max_negate(b, j, hh):
                n, _, _ = b
                h = 2 * j + hh
                if not (isinstance(n, int) and n == 0 and h < 4):
                    pool.wait_ge(exp_done, n * H + (h - 3))
                wait_apart(pool, half_done, (max_done, n * 64 + j * 8 + hh + 1))
                pool.tensor_scalar(nmax[:, h % 4:h % 4 + 1], top[:, j % 4, hh, 0:1], -scale, 0.0, ALU.mult, ALU.add).then_inc(
                    nmax_done, 1)

            def before(b):
                return (b[0] - 1, None, None)

            def batch(b, nb, has_prev, has_next):
                n = b[0]
                for j in range(PAIRS):
                    prev, p = (b, j - 1) if j else (before(b), PAIRS - 1)
                    if j or has_prev:
                        keep_mask(prev, p, 0)
                    max_negate(b, j, 0)
                    max_negate(b, j, 1)
                    if j or has_prev:
                        keep_probs(prev, p, 0)
                        keep_mask(prev, p, 1)
                        keep_probs(prev, p, 1)
                    if j == 4 and has_prev:
                        norm(n - 1)
                    if j == 5 and has_next:
                        stage(n + 2)
                    if j == 6 and has_prev:
                        keep(n - 1)
                    if isinstance(n, int) and n >= B - LAST:
                        if n == B - LAST and j == 5:
                            pool.wait_ge(routing.slots_done, 1)
                            pool.wait_ge(x2_kept, CHUNKS[0][1])
                        at = (n - (B - LAST)) * PAIRS + j - 5
                        if 0 <= at < CHUNKS[0][1]:
                            for c in range(2):
                                routing.send(pool, at, c)

            def lead_out(b):
                for hh in range(2):
                    keep_mask(b, PAIRS - 1, hh)
                    keep_probs(b, PAIRS - 1, hh)
                norm(b[0])
                keep(b[0])

            run(pool, batch, lead_in, lead_out)

        @block.vector
        def _(dve):
            def quarter_out(b, q, part):
                n, _, _ = b
                hs = slice(4 * q, 4 * q + 4)
                m = n * 4 + q + 1
                o_bank = o_ps[:, q % 2, 0:4 * (DH + 1)].rearrange("p (h d) -> p h d", d=DH + 1)
                if part == 0:
                    dve.wait_ge(pv_done, n * PAIRS + 2 * q + 2)
                    dve.scalar_tensor_tensor(total[:, hs], full_sum[:, hs], 1e-8, o_bank[:, :, DH], ALU.mult, ALU.add).then_inc(
                        total_done, 1)
                if part == 1:
                    dve.wait_ge(total_done, m)
                    dve.reciprocal(rtotal[:, hs], total[:, hs]).then_inc(rtotal_done, 1)
                if part == 2:
                    dve.wait_ge(rtotal_done, m)
                    if q == 0 and not (isinstance(n, int) and n == 0):
                        dve.wait_ge(oT_done, 2 * n)
                    dve.tensor_tensor(o[:, hs, :], o_bank[:, :, 0:DH], rtotal[:, hs].unsqueeze(2).to_broadcast([T, 4, DH]),
                                      ALU.mult).then_inc(o_done, 1)

            def residual(b, part):
                n, _, _ = b
                xr = xres[:, bass.ds(n, 1), 0:C].rearrange("p b c -> p (b c)")
                if part == 0:
                    dve.wait_ge(out_copied, n + 1)
                    dve.tensor_tensor(summed[:], out_sb[:], xr, ALU.add).then_inc(sum_done, 1)
                if part == 1:
                    dve.wait_ge(sum_done, n + 1)
                    dve.bn_stats(stats[:], summed[:]).then_inc(stats_done, 1)
                if part == 2:
                    dve.wait_ge(wq_done, 1)
                    dve.wait_ge(stats_done, n + 1)
                    dve.bn_aggr(mv[:], stats[:]).then_inc(mv_done, 1)
                if part == 3:
                    dve.wait_ge(mv_done, n + 1)
                    dve.tensor_scalar(veps[:], mv[:, 1:2], LN_EPS, None, ALU.add).then_inc(veps_done, 1)
                if part == 4:
                    dve.wait_ge(rstd_done, n + 1)
                    dve.tensor_scalar(x2[:], summed[:], mv[:, 0:1], rstd[:, 0:1], ALU.subtract, ALU.mult).then_inc(x2_done, 1)

            def logit_add(b):
                n, _, _ = b
                dve.wait_ge(lg_copied, n + 1)
                dve.tensor_tensor(logits[:, bass.ds(n, 1), :].rearrange("p b e -> p (b e)"), lg_sb[:], br_sb[:], ALU.add).then_inc(
                    lg_added, 1)

            def before(b):
                return (b[0] - 1, None, None)

            def lead_in(b):
                pass

            def batch(b, nb, has_prev, has_next):
                n = b[0]
                for j in range(PAIRS):
                    if is_routed(b) and j == 1:
                        routing.choose(dve, 0)
                    if is_routed(b) and j == 4:
                        routing.rank_chunk(dve, 0, w_ps[:, 1, :])
                    for r in range(TOPK // 8):
                        for hh in range(2):
                            h = 2 * j + hh
                            src = s_sb[:, h % 8, :] if r == 0 else work[:, hh, :]
                            if r == 0:
                                wait_apart(dve, wq_done, (s_copied, n * H + h + 1))
                            else:
                                wait_apart(dve, wq_done, (rep_done, n * 48 + j * 6 + 2 * (r - 1) + hh + 1))
                            dve.max(top[:, j % 4, hh, 8 * r:8 * r + 8], src).then_inc(max_done, 1)
                        if j == 0 and has_prev and r < 3:
                            quarter_out(before(b), 2, r)
                        if j == 1 and has_prev and r > 1:
                            quarter_out(before(b), 3, r - 2)
                        if j == 2 and has_prev and r == 0:
                            quarter_out(before(b), 3, 2)
                        if j == 4 and r < 3:
                            quarter_out(b, 0, r)
                        if j == 6 and r < 3:
                            quarter_out(b, 1, r)
                        if j == 7 and has_prev and r == 3:
                            logit_add(before(b))
                        if r == TOPK // 8 - 1:
                            break
                        for hh in range(2):
                            h = 2 * j + hh
                            src = s_sb[:, h % 8, :] if r == 0 else work[:, hh, :]
                            wait_apart(dve, wq_done, (max_done, n * 64 + j * 8 + 2 * r + hh + 1))
                            dve.match_replace(work[:, hh, :], top[:, j % 4, hh, 8 * r:8 * r + 8], src, GONE).then_inc(rep_done, 1)
                        if j == 3 and has_prev:
                            residual(before(b), r)
                        if j == 4 and has_prev and r == 0:
                            residual(before(b), 3)
                        if j == 5 and has_prev and r == 0:
                            residual(before(b), 4)

            def lead_out(b):
                for q in (2, 3):
                    for part in range(3):
                        quarter_out(b, q, part)
                for part in range(5):
                    residual(b, part)
                logit_add(b)

            run(dve, batch, lead_in, lead_out)
            dve.wait_ge(x2_kept, B)
            dve.wait_ge(lg_added, B)


def expert_phase(nc, routing, ident_sb, W1, b1T, W2, b2, fin, xg):
    ctx = ExitStack()
    with ctx:
        def sb(name, shape, dt=F32):
            return ctx.enter_context(nc.sbuf_tensor("e_" + name, shape, dt))

        def ps(name, shape, dt=F32):
            return ctx.enter_context(nc.psum_tensor("e_" + name, shape, dt))

        def sem(name):
            return ctx.enter_context(nc.semaphore("e_" + name))

        w1 = [sb(f"w1_{i}", [128, KC, HID]) for i in range(2)]
        w2 = [sb(f"w2_{i}", [128, HM, C]) for i in range(2)]
        b1_sb = [sb(f"b1_{i}", [128, HM]) for i in range(2)]
        b2_sb = sb("b2_sb", [128, E, C])
        rows = [sb(f"rows{i}", [128, NT, CX]) for i in range(2)]
        rowsT = [sb(f"rowsT{i}", [128, KC, CAP]) for i in range(2)]
        hT = sb("hT", [128, HM, CAP])
        ysum = sb("ysum_e", [128, 2, C])
        yrow = [sb(f"yrow{i}", [128, NT, C]) for i in range(2)]
        is_first = [sb(f"is_first{i}", [128, NT]) for i in range(2)]
        is_second = [sb(f"is_second{i}", [128, NT]) for i in range(2)]
        part_w = [sb(f"part_w{i}", [128, 2, NT]) for i in range(2)]
        weight = [sb(f"weight{i}", [128, NT]) for i in range(2)]
        target = [sb(f"target{i}", [128, NT], I32) for i in range(2)]

        t_ps = ps("t_ps", [128, 2, 512])
        h_ps = ps("h_ps_e", [128, 4, 512])
        y_ps = ps("y_ps", [128, 2, 512])

        consts = sem("consts")
        fate_done, weight_done = sem("fate_done"), sem("weight_done")
        e_loaded = [sem(f"e_loaded{i}") for i in range(2)]
        rows_loaded = [sem(f"rows_loaded{i}") for i in range(2)]
        rt_done, rt_copied = sem("rt_done"), sem("rt_copied")
        h_done, h_copied = sem("h_done_e"), sem("h_copied")
        y_done, y_added, y_scaled = sem("y_done_e"), sem("y_added"), sem("y_scaled")
        y_sent = [sem(f"y_sent{i}") for i in range(2)]

        block = ctx.enter_context(nc.Block())
        w1_v = W1.rearrange("e (k p) h -> e p k h", p=128)
        w2_v = W2.rearrange("e (m p) c -> e p m c", p=128)
        xg_v = xg.rearrange("(e i p) c -> e p i c", e=E, p=128)

        @block.sync
        def _(sp):
            sp.dma_start(b2_sb[:], b2.rearrange("(a e) c -> a e c", a=1).to_broadcast([128, E, C])).then_inc(consts, 16)
            for p in range(2):
                sp.dma_start(w1[p][:], w1_v[p]).then_inc(e_loaded[p], 16)
                sp.dma_start(w2[p][:], w2_v[p]).then_inc(e_loaded[p], 16)
                sp.dma_start(b1_sb[p][:], b1T[p]).then_inc(e_loaded[p], 16)
            sp.wait_ge(routing.sent, 16 * 2 * B)
            for p in range(2):
                sp.dma_start(rows[p][:], xg_v[p]).then_inc(rows_loaded[p], 16)
            with sp.Fori(0, E // 2 - 1) as i:
                for p in range(2):
                    e = 2 * i + p
                    sp.wait_ge(consts, 16)
                    sp.wait_ge(h_copied, 16 * e + 16)
                    sp.dma_start(w1[p][:], w1_v[bass.ds(e + 2, 1)].rearrange("e p k h -> p (e k) h")).then_inc(e_loaded[p], 16)
                    sp.dma_start(b1_sb[p][:], b1T[bass.ds(e + 2, 1)].rearrange("e p m -> p (e m)")).then_inc(e_loaded[p], 16)
                    sp.wait_ge(y_done, NT * e + NT)
                    sp.dma_start(w2[p][:], w2_v[bass.ds(e + 2, 1)].rearrange("e p k h -> p (e k) h")).then_inc(e_loaded[p], 16)
                    sp.wait_ge(y_sent[p], 16 * NT * (i + 1))
                    sp.dma_start(rows[p][:], xg_v[bass.ds(e + 2, 1)].rearrange("e p i c -> p (e i) c")).then_inc(rows_loaded[p], 16)
            for p in range(2):
                sp.wait_ge(y_sent[p], 16 * NT * (E // 2))

        @block.gpsimd
        def _(pool):
            pool.wait_ge(routing.slots_done, 2)
            for b in range(*CHUNKS[1]):
                for c in range(2):
                    routing.send(pool, b, c)
            bound = pool.to_reg(2 * N - 1)
            with pool.Fori(0, E // 2) as i:
                for p in range(2):
                    for t in range(NT):
                        wait_apart(pool, routing.slots_done, (y_scaled, (2 * i + p) * NT + t + 1))
                        pool.indirect_dma_start(fin, bass.IndirectOffsetOnAxis(ap=target[p][:, t:t + 1], axis=0),
                                                yrow[p][:, t, :], None, bounds_check=bound, oob_is_err=False).then_inc(y_sent[p], 16)

        @block.tensor
        def _(pe):
            pe.wait_ge(consts, 16)
            routing.counts(pe, 1, t_ps[:, 0, :])

            def turn(p, e, i):
                pe.wait_ge(rows_loaded[p], 16 * (i + 1))
                q = 0
                for k in range(KC):
                    for t in range(NT):
                        if q % 4 == 0:
                            n = e * TB + q // 4
                            if isinstance(n, int) and n < 2:
                                pass
                            else:
                                pe.wait_ge(rt_copied, n - 1)
                        mm = pe.transpose(t_ps[:, (q // 4) % 2, (q % 4) * 128:(q % 4 + 1) * 128], rows[p][:, t, k * 128:(k + 1) * 128], ident_sb[:])
                        q += 1
                        if q % 4 == 0 or q == KC * NT:
                            mm.then_inc(rt_done, 1)

            def expert(p, e, i, last):
                pe.wait_ge(e_loaded[p], 48 * (i + 1))
                pe.wait_ge(rt_copied, (e + 1) * TB)
                for m in range(HM):
                    for half in range(2):
                        n = e * 16 + 2 * m + half
                        if not (isinstance(n, int) and n < 4):
                            pe.wait_ge(h_copied, n - 3)
                        for k in range(KC):
                            mm = pe.matmul(h_ps[:, (2 * m + half) % 4, 0:HALF], w1[p][:, k, m * 128:(m + 1) * 128],
                                           rowsT[p][:, k, half * HALF:(half + 1) * HALF], start=(k == 0), stop=(k == KC - 1))
                        mm.then_inc(h_done, 1)
                if not last:
                    turn(1 - p, e + 1, i + p)
                for t in range(NT):
                    n = e * NT + t
                    if not (isinstance(n, int) and n < 2):
                        pe.wait_ge(y_added, n - 1)
                    if t == 0:
                        pe.wait_ge(h_copied, (e + 1) * 16)
                    for m in range(HM):
                        mm = pe.matmul(y_ps[:, (p * NT + t) % 2, 0:C], hT[:, m, t * 128:(t + 1) * 128], w2[p][:, m, :],
                                       start=(m == 0), stop=(m == HM - 1))
                    mm.then_inc(y_done, 1)

            pe.wait_ge(routing.count_read, 2)
            turn(0, 0, 0)
            expert(0, 0, 0, False)
            with pe.Fori(0, E // 2 - 1) as i:
                expert(1, 2 * i + 1, i, False)
                expert(0, 2 * i + 2, i + 1, False)
            expert(1, E - 1, E // 2 - 1, True)

        @block.scalar
        def _(act):
            routing.exps(act, 1)

            def turn(p, e):
                q = 0
                done = 0
                while q < KC * NT:
                    k = min(4, KC * NT - q)
                    act.wait_ge(rt_done, e * TB + done + 1)
                    if done == 0 and not (isinstance(e, int) and e < 2):
                        act.wait_ge(h_done, (e - 1) * 16)
                    flat = rowsT[p][:].rearrange("p k n -> p (k n)")
                    act.activation(flat[:, q * 128:(q + k) * 128], t_ps[:, done % 2, 0:k * 128], ACT.Copy).then_inc(rt_copied, 1)
                    q += k
                    done += 1

            def expert(p, e, last):
                for m in range(HM):
                    for half in range(2):
                        act.wait_ge(h_done, e * 16 + 2 * m + half + 1)
                        if m == 0 and half == 0:
                            act.wait_ge(y_done, e * NT)
                        act.activation(hT[:, m, half * HALF:(half + 1) * HALF], h_ps[:, (2 * m + half) % 4, 0:HALF], ACT.Gelu,
                                       bias=b1_sb[p][:, m:m + 1]).then_inc(h_copied, 1)
                if not last:
                    turn(1 - p, e + 1)

            turn(0, 0)
            expert(0, 0, False)
            with act.Fori(0, E // 2 - 1) as i:
                expert(1, 2 * i + 1, False)
                expert(0, 2 * i + 2, False)
            expert(1, E - 1, True)

        @block.vector
        def _(dve):
            routing.choose(dve, 1)
            routing.rank_chunk(dve, 1, t_ps[:, 0, :])

            def fates(p, e, i):
                gates = [rows[p][:, :, at] for at in (GATE1, GATE2)]
                if isinstance(e, int):
                    first = routing.first[:, e:e + 1]
                else:
                    first = routing.first[:, bass.ds(e, 1)]
                dve.wait_ge(rows_loaded[p], 16 * (i + 1))
                dve.tensor_tensor(is_first[p][:], rows[p][:, :, WHERE], first.to_broadcast([128, NT]), ALU.is_equal).then_inc(fate_done, 1)
                dve.wait_ge(fate_done, 3 * e + 1)
                dve.tensor_scalar(is_second[p][:], is_first[p][:], -1.0, 1.0, ALU.mult, ALU.add)
                dve.tensor_tensor(part_w[p][:, 0, :], is_first[p][:], gates[0], ALU.mult).then_inc(fate_done, 1)
                dve.wait_ge(fate_done, 3 * e + 2)
                if not isinstance(i, int) or i > 0:
                    dve.wait_ge(y_sent[p], 16 * NT * i)
                dve.scalar_tensor_tensor(target[p][:], is_second[p][:], float(N), rows[p][:, :, TOKEN], ALU.mult, ALU.add)
                dve.tensor_tensor(part_w[p][:, 1, :], is_second[p][:], gates[1], ALU.mult).then_inc(fate_done, 1)
                dve.wait_ge(fate_done, 3 * e + 3)
                dve.tensor_tensor(weight[p][:], part_w[p][:, 0, :], part_w[p][:, 1, :], ALU.add).then_inc(weight_done, 1)

            def expert(p, e, i):
                fates(p, e, i)
                for t in range(NT):
                    dve.wait_ge(y_done, e * NT + t + 1)
                    if not (isinstance(e, int) and e == 0 and t < 2):
                        dve.wait_ge(y_scaled, e * NT + (t - 1))
                    dve.tensor_tensor(ysum[:, (p * NT + t) % 2, :], y_ps[:, (p * NT + t) % 2, 0:C], b2_of(e), ALU.add).then_inc(y_added, 1)
                    if t == 0:
                        dve.wait_ge(weight_done, e + 1)
                        if not isinstance(i, int) or i > 0:
                            dve.wait_ge(y_sent[p], 16 * NT * i)
                    dve.wait_ge(y_added, e * NT + t + 1)
                    dve.tensor_scalar(yrow[p][:, t, :], ysum[:, (p * NT + t) % 2, :], weight[p][:, t:t + 1], None, ALU.mult).then_inc(y_scaled, 1)

            def b2_of(e):
                if isinstance(e, int):
                    return b2_sb[:, e, :]
                return b2_sb[:, bass.ds(e, 1), :].rearrange("p e c -> p (e c)")

            expert(0, 0, 0)
            expert(1, 1, 0)
            with dve.Fori(1, E // 2) as i:
                expert(0, 2 * i, i)
                expert(1, 2 * i + 1, i)


def final_phase(nc, xres, fin, out):
    ctx = ExitStack()
    with ctx:
        def sb(name, shape, dt=F32):
            return ctx.enter_context(nc.sbuf_tensor("f_" + name, shape, dt))

        def sem(name):
            return ctx.enter_context(nc.semaphore("f_" + name))

        part = sb("part", [T, GROUPS, 2, GB, C])
        stats = sb("stats", [T, 2, GB, 6])
        mv = sb("mv", [T, GROUPS, GB, 2])
        veps = sb("veps", [T, GROUPS, GB])
        rstd = sb("rstd", [T, GROUPS, GB])
        shift = sb("shift", [T, GROUPS, GB])
        neghalf = sb("neghalf", [T, GB])

        loaded = [sem(f"loaded{g}") for g in range(GROUPS)]
        half_done, add1_done, add2_done, stats_done = sem("half_done"), sem("add1_done"), sem("add2_done"), sem("stats_done")
        mv_done, veps_done, rstd_done = sem("mv_done"), sem("veps_done"), sem("rstd_done")
        shift_done, norm_done, sent = sem("shift_done"), sem("norm_done"), sem("sent")

        fin_v = fin.rearrange("(c b t) d -> b t c d", c=2, t=T)
        block = ctx.enter_context(nc.Block())

        @block.sync
        def _(sp):
            for g in range(GROUPS):
                for c in range(2):
                    sp.dma_start(part[:, g, c], fin_v[g * GB:(g + 1) * GB, :, c, :].rearrange("b t d -> t b d")).then_inc(loaded[g], 16)
            for g in range(GROUPS):
                sp.wait_ge(norm_done, g + 1)
                sp.dma_start(out.rearrange("b t c -> t b c")[:, g * GB:(g + 1) * GB, :], part[:, g, 0]).then_inc(sent, 16)
            sp.wait_ge(sent, 16 * GROUPS)

        @block.gpsimd
        def _(pool):
            pool.memset(neghalf[:], -0.5).then_inc(half_done, 1)
            pool.wait_ge(half_done, 1)

            def power(g):
                pool.wait_ge(veps_done, g + 1)
                pool.tensor_tensor(rstd[:, g], veps[:, g], neghalf[:], ALU.pow).then_inc(rstd_done, 1)

            for g in range(GROUPS):
                pool.wait_ge(loaded[g], 32)
                pool.tensor_tensor(part[:, g, 0], part[:, g, 0], part[:, g, 1], ALU.add).then_inc(add1_done, 1)
                if g > 1:
                    power(g - 2)
            power(GROUPS - 2)
            power(GROUPS - 1)

        @block.scalar
        def _(act):
            for g in range(GROUPS):
                act.wait_ge(shift_done, g + 1)
                for b in range(GB):
                    last = act.activation(part[:, g, 0, b, :], part[:, g, 0, b, :], ACT.Identity, scale=rstd[:, g, b:b + 1],
                                          bias=shift[:, g, b:b + 1])
                last.then_inc(norm_done, 1)

        @block.vector
        def _(dve):
            def residual(g):
                dve.wait_ge(add1_done, g + 1)
                dve.tensor_tensor(part[:, g, 0], part[:, g, 0], xres[:, g * GB:(g + 1) * GB, 0:C], ALU.add).then_inc(add2_done, 1)

            def shifts(g):
                dve.wait_ge(rstd_done, g + 1)
                dve.scalar_tensor_tensor(shift[:, g], mv[:, g, :, 0], -1.0, rstd[:, g], ALU.mult, ALU.mult).then_inc(shift_done, 1)

            residual(0)
            for g in range(GROUPS):
                dve.wait_ge(add2_done, g + 1)
                for b in range(GB):
                    last = dve.bn_stats(stats[:, g % 2, b, :], part[:, g, 0, b, :])
                last.then_inc(stats_done, 1)
                if g + 1 < GROUPS:
                    residual(g + 1)
                dve.wait_ge(stats_done, g + 1)
                for b in range(GB):
                    last = dve.bn_aggr(mv[:, g, b, :], stats[:, g % 2, b, :])
                last.then_inc(mv_done, 1)
                if g > 1:
                    shifts(g - 2)
                dve.wait_ge(mv_done, g + 1)
                dve.tensor_scalar(veps[:, g], mv[:, g, :, 1], LN_EPS, None, ALU.add).then_inc(veps_done, 1)
            shifts(GROUPS - 2)
            shifts(GROUPS - 1)


def kernel(**inputs):
    import ml_dtypes
    import numpy as np
    from concourse import bacc
    from concourse.bass_utils import run_bass_kernel_spmd

    a = {k: np.asarray(v) for k, v in inputs.items()}
    tri = np.triu(np.ones((T, T)), 1)
    pick_rows = np.zeros((128, B, T), ml_dtypes.bfloat16)
    for b in range(B):
        pick_rows[b, b] = 1
    spread = np.zeros((BC_ROWS, 2 * NSTATE, 128), ml_dtypes.bfloat16)
    for at in BC_AT:
        for r in range(2 * NSTATE):
            spread[at + r, r] = 1
    arrays = {
        "x": a["x"],
        "xT": a["x"].reshape(N, C).T,
        "W_inT": a["L0_attn_W_in"].T,
        "Kx": a["L0_attn_Kx"],
        "Kz": a["L0_attn_Kz"],
        "W_xprojT": a["L0_attn_W_xproj"].T,
        "W_dtT": a["L0_attn_W_dt"].T,
        "b_dt": a["L0_attn_b_dt"],
        "A_log": a["L0_attn_A_log"],
        "D": a["L0_attn_D"],
        "W_outT": a["L0_attn_W_out"].T,
        "ctxT": a["ctx_1024"].transpose(0, 2, 1),
        "mask": a["mask_BxS2_bf1"].view(np.uint8),
        "Wq": a["L0_xattn_Wq"],
        "Wk": a["L0_xattn_Wk"],
        "Wv": a["L0_xattn_Wv"],
        "Wo": a["L0_xattn_Wo"],
        "inv_temp": a["L0_xattn_inv_temp"],
        "Wr": a["L0_ffn_Wr"],
        "br": a["L0_ffn_br"],
        "W1": a["L0_ffn_W1"],
        "b1T": a["L0_ffn_b1"].reshape(E, HM, 128).transpose(0, 2, 1),
        "W2": a["L0_ffn_W2"],
        "b2": a["L0_ffn_b2"],
        "ident": np.eye(128, dtype=np.float32),
        "rows_sel": spread,
        "mask_pick": pick_rows,
        "lower": np.stack([tri, np.ones((T, T))], 1).astype(ml_dtypes.bfloat16),
    }
    nc = bacc.Bacc("TRN2", target_bir_lowering=False, num_devices=1)
    feeds, ins = {}, {}
    for name, value in arrays.items():
        value = np.ascontiguousarray(value)
        feeds[f"in_{name}"] = value
        ins[name] = nc.dram_tensor(f"in_{name}", value.shape, mybir.dt.from_np(value.dtype), kind="ExternalInput").ap()
    out = nc.dram_tensor("out_0", (B, T, C), F32, kind="ExternalOutput").ap()
    decoder_kernel(nc, out, ins)
    result = run_bass_kernel_spmd(nc, [feeds], core_ids=[0])
    return result.results[0]["out_0"]
```
